# Optimizing a Trainium2 kernel written in Bass

```python
import numpy as np
import jax
import jax.numpy as jnp

def _softmax(x, axis=-1):
    return jax.nn.softmax(x, axis=axis)

def _gelu(x):
    return jax.nn.gelu(x, approximate=True)

def _silu(x):
    return jax.nn.silu(x)

def _sigmoid(x):
    return jax.nn.sigmoid(x)

def _layernorm(x, axis=-1, eps=1e-05):
    m = jnp.mean(x, axis=axis, keepdims=True)
    v = jnp.var(x, axis=axis, keepdims=True)
    return (x - m) / jnp.sqrt(v + eps)

def _scatter_add(tgt, idx, src, axis=0):
    return tgt.at[idx].add(src)

def _segment_sum(src, seg, n):
    return jax.ops.segment_sum(src, seg, n)
kernel_name = 'mk_pixart_seq_d4_seqx_r8_2205f4'

def setup_inputs(seed: int=0):
    np.random.seed(seed)
    _w = jnp.asarray

    def _rec_inputs():
        import jax
        import jax.numpy as jnp
        _rk = jax.random.key(seed)
        x = -0.0002928 + 1 * jax.random.normal(jax.random.fold_in(_rk, 1), (32, 128, 128), jnp.float32)
        _lenS = 128 - jax.random.randint(jax.random.fold_in(_rk, 7), (32,), 0, max(1, 128 // 4) + 1, jnp.int32)
        _lenS2 = 77 - jax.random.randint(jax.random.fold_in(_rk, 8), (32,), 0, max(1, 77 // 4) + 1, jnp.int32)
        cond_1024 = 0.000887014 + 1.03683 * jax.random.normal(jax.random.fold_in(_rk, 11), (32, 128), jnp.float32)
        _ctx_1024P = jax.random.normal(jax.random.fold_in(_rk, 12), (32, 16, 128), jnp.float32)
        _ctx_1024c = jax.random.dirichlet(jax.random.fold_in(_rk, 512), 0.3 * jnp.ones((16,), jnp.float32), (32, 77))
        _ctx_1024t = jnp.einsum('bsk,bkd->bsd', _ctx_1024c, _ctx_1024P)
        _ctx_1024t = _ctx_1024t * jax.lax.rsqrt(jnp.mean(jnp.square(_ctx_1024t)) + 1e-12) * 0.953939
        ctx_1024 = -0.00606593 + 0.997213 * (_ctx_1024t + 0.3 * jax.random.normal(jax.random.fold_in(_rk, 612), (32, 77, 128), jnp.float32))
        _validS = jnp.arange(128)[None, :] < _lenS[:, None]
        _validS2 = jnp.arange(77)[None, :] < _lenS2[:, None]
        _causal = jnp.tril(jnp.ones((128, 128), dtype=bool))
        mask_BxS2_bf1 = jnp.ones((32, 77), dtype=bool)
        mask_SxS_bk0 = jnp.logical_not(jnp.broadcast_to(_validS[0:1, :], (128, 128)))
        return (x, cond_1024, ctx_1024, mask_BxS2_bf1, mask_SxS_bk0)
    x, cond_1024, ctx_1024, mask_BxS2_bf1, mask_SxS_bk0 = _rec_inputs()

    def _L0_xcond_setup():
        import jax, jax.numpy as jnp
        import numpy as np
        B, N, D, H, LC = (2, 128, 128, 16, 77)
        HD = D // H
        BLOCK = 16
        ROPE_BASE = 10000.0
        EPS = 1e-05

        def _block_diff_mask(n, block_size):
            idx = np.arange(2 * n)
            q = idx[:, None]
            kv = idx[None, :]
            fq = q >= n
            fkv = kv >= n
            bq = np.where(fq, (q - n) // block_size, q // block_size)
            bkv = np.where(fkv, (kv - n) // block_size, kv // block_size)
            block_diagonal = (bq == bkv) & (fq == fkv)
            offset_block_causal = (bq > bkv) & fkv & ~fq
            block_causal = (bq >= bkv) & fq & fkv
            return jnp.asarray(block_diagonal | offset_block_causal | block_causal)

        def _rope_tables(n):
            inv_freq = 1.0 / ROPE_BASE ** (np.arange(0, HD, 2, dtype=np.float32) / HD)
            freqs = np.outer(np.arange(n, dtype=np.float32), inv_freq)
            emb = np.concatenate([freqs, freqs], axis=-1)
            cos = jnp.asarray(np.cos(emb), jnp.float32)[None, :, None, :]
            sin = jnp.asarray(np.sin(emb), jnp.float32)[None, :, None, :]
            return (cos, sin)

        def _ln(x, w):
            xf = x.astype(jnp.float32)
            mu = jnp.mean(xf, axis=-1, keepdims=True)
            var = jnp.mean(jnp.square(xf - mu), axis=-1, keepdims=True)
            y = (xf - mu) * jax.lax.rsqrt(var + EPS)
            return y * w[None, None, :]

        def _apply_rope(t, cos, sin):
            t1, t2 = jnp.split(t, 2, axis=-1)
            rot = jnp.concatenate([-t2, t1], axis=-1)
            return t * cos + rot * sin

        def _attn(q, k, v, mask):
            scale = 1.0 / np.sqrt(HD)
            s = jnp.einsum('bqhd,bkhd->bhqk', q, k) * scale
            s = jnp.where(mask, s, jnp.finfo(s.dtype).min)
            a = jax.nn.softmax(s, axis=-1)
            return jnp.einsum('bhqk,bkhd->bqhd', a, v)
        key = jax.random.key(seed)
        ks = jax.random.split(key, 16)
        w = lambda k, shp: jax.random.normal(k, shp, jnp.float32) * 0.02
        inp = {'x': jax.random.normal(ks[0], (B, 2 * N, D), jnp.float32), 'cond_global': jax.random.normal(ks[1], (B, D), jnp.float32), 'cond_tokens': jax.random.normal(ks[2], (B, LC, D), jnp.float32), 'adaLN_W': w(ks[3], (D, 9 * D)), 'adaLN_b': w(ks[4], (9 * D,)), 'norm1_w': jnp.ones((D,), jnp.float32), 'qkv_W': w(ks[5], (D, 3 * D)), 'attn_out_W': w(ks[6], (D, D)), 'normc_w': jnp.ones((D,), jnp.float32), 'cq_W': w(ks[7], (D, D)), 'ck_W': w(ks[8], (D, D)), 'cv_W': w(ks[9], (D, D)), 'co_W': w(ks[10], (D, D)), 'norm2_w': jnp.ones((D,), jnp.float32), 'mlp_W1': w(ks[11], (D, 4 * D)), 'mlp_b1': w(ks[12], (4 * D,)), 'mlp_W2': w(ks[13], (4 * D, D)), 'mlp_b2': w(ks[14], (D,)), 'cond_kv_mask': jnp.ones((B, LC), bool), 'attn_mask': _block_diff_mask(N, BLOCK)}
        return inp
    _L0_xcond_all = _L0_xcond_setup()
    _L0_xcond_in = {k: v for k, v in _L0_xcond_all.items() if k in ('adaLN_W', 'adaLN_b', 'norm1_w', 'qkv_W', 'attn_out_W', 'normc_w', 'cq_W', 'ck_W', 'cv_W', 'co_W', 'norm2_w', 'mlp_W1', 'mlp_b1', 'mlp_W2', 'mlp_b2')}
    del _L0_xcond_all

    def _L1_xcond_setup():
        import jax, jax.numpy as jnp
        import numpy as np
        H = 128
        RH = 2 * H
        E = 3
        B, T, P = (8, 256, 64)
        LN_EPS = 1e-05

        def _layer_norm(x, gamma, beta):
            mu = jnp.mean(x, axis=-1, keepdims=True)
            var = jnp.mean(jnp.square(x - mu), axis=-1, keepdims=True)
            return (x - mu) * jax.lax.rsqrt(var + LN_EPS) * gamma + beta
        key = jax.random.key(seed)
        ks = jax.random.split(key, 24)
        s = lambda fan_in: 1.0 / np.sqrt(fan_in)
        inp = {'mix_hidden_states': jax.random.normal(ks[0], (B, T, H), jnp.float32), 'global_anchor': jax.random.normal(ks[1], (B, H), jnp.float32), 'prototype_bank': jax.random.normal(ks[2], (B, P, H), jnp.float32), 'ln_gamma': jnp.ones((H,), jnp.float32), 'ln_beta': jnp.zeros((H,), jnp.float32), 'Wq': jax.random.normal(ks[3], (H, H), jnp.float32) * s(H), 'Wk': jax.random.normal(ks[4], (H, H), jnp.float32) * s(H), 'Wv': jax.random.normal(ks[5], (H, H), jnp.float32) * s(H), 'router_W': jax.random.normal(ks[6], (3 * H, E), jnp.float32) * s(3 * H), 'router_b': jnp.zeros((E,), jnp.float32), 'e_w1': jax.random.normal(ks[7], (E, 3 * H, RH), jnp.float32) * s(3 * H), 'e_b1': jnp.zeros((E, RH), jnp.float32), 'e_w2': jax.random.normal(ks[8], (E, RH, H), jnp.float32) * s(RH), 'e_b2': jnp.zeros((E, H), jnp.float32), 'gate_w1': jax.random.normal(ks[9], (3 * H, H), jnp.float32) * s(3 * H), 'gate_b1': jnp.zeros((H,), jnp.float32), 'gate_w2': jax.random.normal(ks[10], (H, H), jnp.float32) * s(H), 'gate_b2': jnp.zeros((H,), jnp.float32), 'out_w': jax.random.normal(ks[11], (H, H), jnp.float32) * s(H), 'out_b': jnp.zeros((H,), jnp.float32)}
        return inp
    _L1_xcond_all = _L1_xcond_setup()
    _L1_xcond_in = {k: v for k, v in _L1_xcond_all.items() if k in ('ln_gamma', 'ln_beta', 'Wq', 'Wk', 'Wv', 'router_W', 'router_b', 'e_w1', 'e_b1', 'e_w2', 'e_b2', 'gate_w1', 'gate_b1', 'gate_w2', 'gate_b2', 'out_w', 'out_b')}
    del _L1_xcond_all

    def _L2_xcond_setup():
        import jax, jax.numpy as jnp
        import numpy as np
        EPS = 1e-05

        def _ada_ln(x, c, W_ss, b_ss):
            mu = jnp.mean(x, axis=-1, keepdims=True)
            var = jnp.mean((x - mu) ** 2, axis=-1, keepdims=True)
            h = (x - mu) / jnp.sqrt(var + EPS)
            ss = jax.nn.silu(c) @ W_ss + b_ss
            scale, bias = jnp.split(ss, 2, axis=-1)
            return (1.0 + scale)[:, None, :] * h + bias[:, None, :]
        key = jax.random.key(seed)
        ks = jax.random.split(key, 12)
        B, Lq, Lkv, H = (8, 256, 64, 128)
        s = 0.02
        return {'x_q': jax.random.normal(ks[0], (B, Lq, H), jnp.float32), 'x_kv': jax.random.normal(ks[1], (B, Lkv, H), jnp.float32), 't_vec': jax.random.normal(ks[2], (B, H), jnp.float32), 'Wq': jax.random.normal(ks[3], (H, H), jnp.float32) * s, 'bq': jnp.zeros((H,), jnp.float32), 'Wkv': jax.random.normal(ks[4], (H, 2 * H), jnp.float32) * s, 'bkv': jnp.zeros((2 * H,), jnp.float32), 'Wp': jax.random.normal(ks[5], (H, H), jnp.float32) * s, 'bp': jnp.zeros((H,), jnp.float32), 'Wss_q': jax.random.normal(ks[6], (H, 2 * H), jnp.float32) * s, 'bss_q': jnp.zeros((2 * H,), jnp.float32), 'Wss_kv': jax.random.normal(ks[7], (H, 2 * H), jnp.float32) * s, 'bss_kv': jnp.zeros((2 * H,), jnp.float32)}
    _L2_xcond_all = _L2_xcond_setup()
    _L2_xcond_in = {k: v for k, v in _L2_xcond_all.items() if k in ('Wq', 'bq', 'Wkv', 'bkv', 'Wp', 'bp', 'Wss_q', 'bss_q', 'Wss_kv', 'bss_kv')}
    del _L2_xcond_all

    def _L3_xcond_setup():
        import jax, jax.numpy as jnp
        import numpy as np
        D = 128
        H = 16
        DH = D // H
        DFF = 512
        B = 2
        L = 256
        EPS = 1e-05

        def layer_norm(x, g, b):
            mu = jnp.mean(x, axis=-1, keepdims=True)
            var = jnp.mean(jnp.square(x - mu), axis=-1, keepdims=True)
            return (x - mu) * jax.lax.rsqrt(var + EPS) * g + b

        def ada_ln(x, t_emb, ln_g, ln_b, aff_w, aff_b):
            normed = layer_norm(x, ln_g, ln_b)
            affine = t_emb @ aff_w + aff_b
            gamma, beta = jnp.split(affine, 2, axis=-1)
            return gamma[:, None, :] * normed + beta[:, None, :]

        def mha(q_in, k_in, v_in, qw, qb, kw, kb, vw, vb, ow, ob):
            Bq, Lq, _ = q_in.shape
            Lk = k_in.shape[1]
            Q = (q_in @ qw + qb).reshape(Bq, Lq, H, DH)
            K = (k_in @ kw + kb).reshape(Bq, Lk, H, DH)
            V = (v_in @ vw + vb).reshape(Bq, Lk, H, DH)
            scores = jnp.einsum('bqhd,bkhd->bhqk', Q, K) / np.sqrt(DH).astype(np.float32)
            attn = jax.nn.softmax(scores, axis=-1)
            out = jnp.einsum('bhqk,bkhd->bqhd', attn, V).reshape(Bq, Lq, D)
            return out @ ow + ob
        key = jax.random.key(seed)
        ks = jax.random.split(key, 32)
        s = lambda k, shape, scale=0.02: jax.random.normal(k, shape, dtype=jnp.float32) * scale
        inp = {'x': jax.random.normal(ks[0], (B, L, D), dtype=jnp.float32), 'u': jax.random.normal(ks[1], (B, L, D), dtype=jnp.float32), 't_emb': jax.random.normal(ks[2], (B, D), dtype=jnp.float32), 'ln1_g': jnp.ones((D,), jnp.float32), 'ln1_b': jnp.zeros((D,), jnp.float32), 'aff1_w': s(ks[3], (D, 2 * D)), 'aff1_b': jnp.zeros((2 * D,), jnp.float32), 'ln2_g': jnp.ones((D,), jnp.float32), 'ln2_b': jnp.zeros((D,), jnp.float32), 'aff2_w': s(ks[4], (D, 2 * D)), 'aff2_b': jnp.zeros((2 * D,), jnp.float32), 'sa_qw': s(ks[5], (D, D)), 'sa_qb': jnp.zeros((D,), jnp.float32), 'sa_kw': s(ks[6], (D, D)), 'sa_kb': jnp.zeros((D,), jnp.float32), 'sa_vw': s(ks[7], (D, D)), 'sa_vb': jnp.zeros((D,), jnp.float32), 'sa_ow': s(ks[8], (D, D)), 'sa_ob': jnp.zeros((D,), jnp.float32), 'ca_qw': s(ks[9], (D, D)), 'ca_qb': jnp.zeros((D,), jnp.float32), 'ca_kw': s(ks[10], (D, D)), 'ca_kb': jnp.zeros((D,), jnp.float32), 'ca_vw': s(ks[11], (D, D)), 'ca_vb': jnp.zeros((D,), jnp.float32), 'ca_ow': s(ks[12], (D, D)), 'ca_ob': jnp.zeros((D,), jnp.float32), 'ffn_w1': s(ks[13], (D, DFF)), 'ffn_b1': jnp.zeros((DFF,), jnp.float32), 'ffn_w2': s(ks[14], (DFF, D)), 'ffn_b2': jnp.zeros((D,), jnp.float32)}
        return inp
    _L3_xcond_all = _L3_xcond_setup()
    _L3_xcond_in = {k: v for k, v in _L3_xcond_all.items() if k in ('ln1_g', 'ln1_b', 'aff1_w', 'aff1_b', 'ln2_g', 'ln2_b', 'aff2_w', 'aff2_b', 'sa_qw', 'sa_qb', 'sa_kw', 'sa_kb', 'sa_vw', 'sa_vb', 'sa_ow', 'sa_ob', 'ca_qw', 'ca_qb', 'ca_kw', 'ca_kb', 'ca_vw', 'ca_vb', 'ca_ow', 'ca_ob', 'ffn_w1', 'ffn_b1', 'ffn_w2', 'ffn_b2')}
    del _L3_xcond_all
    return {'x': x, 'cond_1024': cond_1024, 'ctx_1024': ctx_1024, 'mask_BxS2_bf1': mask_BxS2_bf1, 'mask_SxS_bk0': mask_SxS_bk0, 'L0_xcond_adaLN_W': _L0_xcond_in['adaLN_W'], 'L0_xcond_adaLN_b': _L0_xcond_in['adaLN_b'], 'L0_xcond_norm1_w': _L0_xcond_in['norm1_w'], 'L0_xcond_qkv_W': _L0_xcond_in['qkv_W'], 'L0_xcond_attn_out_W': _L0_xcond_in['attn_out_W'], 'L0_xcond_normc_w': _L0_xcond_in['normc_w'], 'L0_xcond_cq_W': _L0_xcond_in['cq_W'], 'L0_xcond_ck_W': _L0_xcond_in['ck_W'], 'L0_xcond_cv_W': _L0_xcond_in['cv_W'], 'L0_xcond_co_W': _L0_xcond_in['co_W'], 'L0_xcond_norm2_w': _L0_xcond_in['norm2_w'], 'L0_xcond_mlp_W1': _L0_xcond_in['mlp_W1'], 'L0_xcond_mlp_b1': _L0_xcond_in['mlp_b1'], 'L0_xcond_mlp_W2': _L0_xcond_in['mlp_W2'], 'L0_xcond_mlp_b2': _L0_xcond_in['mlp_b2'], 'L1_xcond_ln_gamma': _L1_xcond_in['ln_gamma'], 'L1_xcond_ln_beta': _L1_xcond_in['ln_beta'], 'L1_xcond_Wq': _L1_xcond_in['Wq'], 'L1_xcond_Wk': _L1_xcond_in['Wk'], 'L1_xcond_Wv': _L1_xcond_in['Wv'], 'L1_xcond_router_W': _L1_xcond_in['router_W'], 'L1_xcond_router_b': _L1_xcond_in['router_b'], 'L1_xcond_e_w1': _L1_xcond_in['e_w1'], 'L1_xcond_e_b1': _L1_xcond_in['e_b1'], 'L1_xcond_e_w2': _L1_xcond_in['e_w2'], 'L1_xcond_e_b2': _L1_xcond_in['e_b2'], 'L1_xcond_gate_w1': _L1_xcond_in['gate_w1'], 'L1_xcond_gate_b1': _L1_xcond_in['gate_b1'], 'L1_xcond_gate_w2': _L1_xcond_in['gate_w2'], 'L1_xcond_gate_b2': _L1_xcond_in['gate_b2'], 'L1_xcond_out_w': _L1_xcond_in['out_w'], 'L1_xcond_out_b': _L1_xcond_in['out_b'], 'L2_xcond_Wq': _L2_xcond_in['Wq'], 'L2_xcond_bq': _L2_xcond_in['bq'], 'L2_xcond_Wkv': _L2_xcond_in['Wkv'], 'L2_xcond_bkv': _L2_xcond_in['bkv'], 'L2_xcond_Wp': _L2_xcond_in['Wp'], 'L2_xcond_bp': _L2_xcond_in['bp'], 'L2_xcond_Wss_q': _L2_xcond_in['Wss_q'], 'L2_xcond_bss_q': _L2_xcond_in['bss_q'], 'L2_xcond_Wss_kv': _L2_xcond_in['Wss_kv'], 'L2_xcond_bss_kv': _L2_xcond_in['bss_kv'], 'L3_xcond_ln1_g': _L3_xcond_in['ln1_g'], 'L3_xcond_ln1_b': _L3_xcond_in['ln1_b'], 'L3_xcond_aff1_w': _L3_xcond_in['aff1_w'], 'L3_xcond_aff1_b': _L3_xcond_in['aff1_b'], 'L3_xcond_ln2_g': _L3_xcond_in['ln2_g'], 'L3_xcond_ln2_b': _L3_xcond_in['ln2_b'], 'L3_xcond_aff2_w': _L3_xcond_in['aff2_w'], 'L3_xcond_aff2_b': _L3_xcond_in['aff2_b'], 'L3_xcond_sa_qw': _L3_xcond_in['sa_qw'], 'L3_xcond_sa_qb': _L3_xcond_in['sa_qb'], 'L3_xcond_sa_kw': _L3_xcond_in['sa_kw'], 'L3_xcond_sa_kb': _L3_xcond_in['sa_kb'], 'L3_xcond_sa_vw': _L3_xcond_in['sa_vw'], 'L3_xcond_sa_vb': _L3_xcond_in['sa_vb'], 'L3_xcond_sa_ow': _L3_xcond_in['sa_ow'], 'L3_xcond_sa_ob': _L3_xcond_in['sa_ob'], 'L3_xcond_ca_qw': _L3_xcond_in['ca_qw'], 'L3_xcond_ca_qb': _L3_xcond_in['ca_qb'], 'L3_xcond_ca_kw': _L3_xcond_in['ca_kw'], 'L3_xcond_ca_kb': _L3_xcond_in['ca_kb'], 'L3_xcond_ca_vw': _L3_xcond_in['ca_vw'], 'L3_xcond_ca_vb': _L3_xcond_in['ca_vb'], 'L3_xcond_ca_ow': _L3_xcond_in['ca_ow'], 'L3_xcond_ca_ob': _L3_xcond_in['ca_ob'], 'L3_xcond_ffn_w1': _L3_xcond_in['ffn_w1'], 'L3_xcond_ffn_b1': _L3_xcond_in['ffn_b1'], 'L3_xcond_ffn_w2': _L3_xcond_in['ffn_w2'], 'L3_xcond_ffn_b2': _L3_xcond_in['ffn_b2']}

def reference(x, cond_1024, ctx_1024, mask_BxS2_bf1, mask_SxS_bk0, L0_xcond_adaLN_W, L0_xcond_adaLN_b, L0_xcond_norm1_w, L0_xcond_qkv_W, L0_xcond_attn_out_W, L0_xcond_normc_w, L0_xcond_cq_W, L0_xcond_ck_W, L0_xcond_cv_W, L0_xcond_co_W, L0_xcond_norm2_w, L0_xcond_mlp_W1, L0_xcond_mlp_b1, L0_xcond_mlp_W2, L0_xcond_mlp_b2, L1_xcond_ln_gamma, L1_xcond_ln_beta, L1_xcond_Wq, L1_xcond_Wk, L1_xcond_Wv, L1_xcond_router_W, L1_xcond_router_b, L1_xcond_e_w1, L1_xcond_e_b1, L1_xcond_e_w2, L1_xcond_e_b2, L1_xcond_gate_w1, L1_xcond_gate_b1, L1_xcond_gate_w2, L1_xcond_gate_b2, L1_xcond_out_w, L1_xcond_out_b, L2_xcond_Wq, L2_xcond_bq, L2_xcond_Wkv, L2_xcond_bkv, L2_xcond_Wp, L2_xcond_bp, L2_xcond_Wss_q, L2_xcond_bss_q, L2_xcond_Wss_kv, L2_xcond_bss_kv, L3_xcond_ln1_g, L3_xcond_ln1_b, L3_xcond_aff1_w, L3_xcond_aff1_b, L3_xcond_ln2_g, L3_xcond_ln2_b, L3_xcond_aff2_w, L3_xcond_aff2_b, L3_xcond_sa_qw, L3_xcond_sa_qb, L3_xcond_sa_kw, L3_xcond_sa_kb, L3_xcond_sa_vw, L3_xcond_sa_vb, L3_xcond_sa_ow, L3_xcond_sa_ob, L3_xcond_ca_qw, L3_xcond_ca_qb, L3_xcond_ca_kw, L3_xcond_ca_kb, L3_xcond_ca_vw, L3_xcond_ca_vb, L3_xcond_ca_ow, L3_xcond_ca_ob, L3_xcond_ffn_w1, L3_xcond_ffn_b1, L3_xcond_ffn_w2, L3_xcond_ffn_b2):
    import jax
    import jax.numpy as jnp

    def _L0_xcond_ref(x, cond_global, cond_tokens, adaLN_W, adaLN_b, norm1_w, qkv_W, attn_out_W, normc_w, cq_W, ck_W, cv_W, co_W, norm2_w, mlp_W1, mlp_b1, mlp_W2, mlp_b2, cond_kv_mask, attn_mask):
        import jax, jax.numpy as jnp
        import numpy as np
        B, N, D, H, LC = (2, 128, 128, 16, 77)
        HD = D // H
        BLOCK = 16
        ROPE_BASE = 10000.0
        EPS = 1e-05

        def _block_diff_mask(n, block_size):
            idx = np.arange(2 * n)
            q = idx[:, None]
            kv = idx[None, :]
            fq = q >= n
            fkv = kv >= n
            bq = np.where(fq, (q - n) // block_size, q // block_size)
            bkv = np.where(fkv, (kv - n) // block_size, kv // block_size)
            block_diagonal = (bq == bkv) & (fq == fkv)
            offset_block_causal = (bq > bkv) & fkv & ~fq
            block_causal = (bq >= bkv) & fq & fkv
            return jnp.asarray(block_diagonal | offset_block_causal | block_causal)

        def _rope_tables(n):
            inv_freq = 1.0 / ROPE_BASE ** (np.arange(0, HD, 2, dtype=np.float32) / HD)
            freqs = np.outer(np.arange(n, dtype=np.float32), inv_freq)
            emb = np.concatenate([freqs, freqs], axis=-1)
            cos = jnp.asarray(np.cos(emb), jnp.float32)[None, :, None, :]
            sin = jnp.asarray(np.sin(emb), jnp.float32)[None, :, None, :]
            return (cos, sin)

        def _ln(x, w):
            xf = x.astype(jnp.float32)
            mu = jnp.mean(xf, axis=-1, keepdims=True)
            var = jnp.mean(jnp.square(xf - mu), axis=-1, keepdims=True)
            y = (xf - mu) * jax.lax.rsqrt(var + EPS)
            return y * w[None, None, :]

        def _apply_rope(t, cos, sin):
            t1, t2 = jnp.split(t, 2, axis=-1)
            rot = jnp.concatenate([-t2, t1], axis=-1)
            return t * cos + rot * sin

        def _attn(q, k, v, mask):
            scale = 1.0 / np.sqrt(HD)
            s = jnp.einsum('bqhd,bkhd->bhqk', q, k) * scale
            s = jnp.where(mask, s, jnp.finfo(s.dtype).min)
            a = jax.nn.softmax(s, axis=-1)
            return jnp.einsum('bhqk,bkhd->bqhd', a, v)
        b, s, d = x.shape
        n = s // 2
        mod = (cond_global @ adaLN_W + adaLN_b)[:, None, :]
        sh_msa, sc_msa, g_msa, sh_x, sc_x, g_x, sh_mlp, sc_mlp, g_mlp = jnp.split(mod, 9, axis=-1)
        x_norm = _ln(x, norm1_w) * (1 + sc_msa) + sh_msa
        cos, sin = _rope_tables(n)

        def qkv(h):
            t = (h @ qkv_W).reshape(b, n, 3, H, HD)
            q, k, v = (t[:, :, 0], t[:, :, 1], t[:, :, 2])
            return (_apply_rope(q, cos, sin), _apply_rope(k, cos, sin), v)
        q1, k1, v1 = qkv(x_norm[:, :n])
        q2, k2, v2 = qkv(x_norm[:, n:])
        q = jnp.concatenate([q1, q2], axis=1)
        k = jnp.concatenate([k1, k2], axis=1)
        v = jnp.concatenate([v1, v2], axis=1)
        self_out = _attn(q, k, v, attn_mask[None, None]).reshape(b, s, d) @ attn_out_W
        x = x + g_msa * self_out
        xc = _ln(x, normc_w) * (1 + sc_x) + sh_x
        qc = (xc @ cq_W).reshape(b, s, H, HD)
        kc = (cond_tokens @ ck_W).reshape(b, LC, H, HD)
        vc = (cond_tokens @ cv_W).reshape(b, LC, H, HD)
        cross = _attn(qc, kc, vc, cond_kv_mask[:, None, None, :]).reshape(b, s, d) @ co_W
        x = x + g_x * cross
        xm = _ln(x, norm2_w) * (1 + sc_mlp) + sh_mlp
        h = jax.nn.gelu(xm @ mlp_W1 + mlp_b1, approximate=True)
        mlp_out = h @ mlp_W2 + mlp_b2
        return x + g_mlp * mlp_out

    def _L1_xcond_ref(mix_hidden_states, global_anchor, prototype_bank, ln_gamma, ln_beta, Wq, Wk, Wv, router_W, router_b, e_w1, e_b1, e_w2, e_b2, gate_w1, gate_b1, gate_w2, gate_b2, out_w, out_b):
        import jax, jax.numpy as jnp
        import numpy as np
        H = 128
        RH = 2 * H
        E = 3
        B, T, P = (8, 256, 64)
        LN_EPS = 1e-05

        def _layer_norm(x, gamma, beta):
            mu = jnp.mean(x, axis=-1, keepdims=True)
            var = jnp.mean(jnp.square(x - mu), axis=-1, keepdims=True)
            return (x - mu) * jax.lax.rsqrt(var + LN_EPS) * gamma + beta
        x = mix_hidden_states
        nx = _layer_norm(x, ln_gamma, ln_beta)
        q = nx @ Wq
        k = prototype_bank @ Wk
        v = prototype_bank @ Wv
        scores = jnp.einsum('bth,bph->btp', q, k) * H ** (-0.5)
        weights = jax.nn.softmax(scores, axis=-1)
        evidence = jnp.einsum('btp,bph->bth', weights, v)
        anchor = jnp.broadcast_to(global_anchor[:, None, :], nx.shape)
        combined = jnp.concatenate([nx, evidence, anchor], axis=-1)
        router_logits = combined @ router_W + router_b
        router_probs = jax.nn.softmax(router_logits, axis=-1)
        h = jax.nn.silu(jnp.einsum('btc,ecr->bter', combined, e_w1) + e_b1)
        expert_out = jnp.einsum('bter,erh->bteh', h, e_w2) + e_b2
        routed = jnp.sum(expert_out * router_probs[..., None], axis=-2)
        g = jax.nn.sigmoid(jax.nn.silu(combined @ gate_w1 + gate_b1) @ gate_w2 + gate_b2)
        refined_delta = g * (routed @ out_w + out_b)
        return x + refined_delta

    def _L2_xcond_ref(x_q, x_kv, t_vec, Wq, bq, Wkv, bkv, Wp, bp, Wss_q, bss_q, Wss_kv, bss_kv):
        import jax, jax.numpy as jnp
        import numpy as np
        EPS = 1e-05

        def _ada_ln(x, c, W_ss, b_ss):
            mu = jnp.mean(x, axis=-1, keepdims=True)
            var = jnp.mean((x - mu) ** 2, axis=-1, keepdims=True)
            h = (x - mu) / jnp.sqrt(var + EPS)
            ss = jax.nn.silu(c) @ W_ss + b_ss
            scale, bias = jnp.split(ss, 2, axis=-1)
            return (1.0 + scale)[:, None, :] * h + bias[:, None, :]
        B, Lq, H = x_q.shape
        Lkv = x_kv.shape[1]
        nh = 16
        dh = H // nh
        xq = _ada_ln(x_q, t_vec, Wss_q, bss_q)
        xkv = _ada_ln(x_kv, t_vec, Wss_kv, bss_kv)
        q = (xq @ Wq + bq).reshape(B, Lq, nh, dh)
        kv = (xkv @ Wkv + bkv).reshape(B, Lkv, 2, nh, dh)
        k = kv[:, :, 0]
        v = kv[:, :, 1]
        scores = jnp.einsum('bqhd,bkhd->bhqk', q, k) / jnp.sqrt(jnp.float32(dh))
        attn = jax.nn.softmax(scores, axis=-1)
        out = jnp.einsum('bhqk,bkhd->bqhd', attn, v).reshape(B, Lq, H)
        return x_q + (out @ Wp + bp)

    def _L3_xcond_ref(x, u, t_emb, ln1_g, ln1_b, aff1_w, aff1_b, ln2_g, ln2_b, aff2_w, aff2_b, sa_qw, sa_qb, sa_kw, sa_kb, sa_vw, sa_vb, sa_ow, sa_ob, ca_qw, ca_qb, ca_kw, ca_kb, ca_vw, ca_vb, ca_ow, ca_ob, ffn_w1, ffn_b1, ffn_w2, ffn_b2):
        import jax, jax.numpy as jnp
        import numpy as np
        D = 128
        H = 16
        DH = D // H
        DFF = 512
        B = 2
        L = 256
        EPS = 1e-05

        def layer_norm(x, g, b):
            mu = jnp.mean(x, axis=-1, keepdims=True)
            var = jnp.mean(jnp.square(x - mu), axis=-1, keepdims=True)
            return (x - mu) * jax.lax.rsqrt(var + EPS) * g + b

        def ada_ln(x, t_emb, ln_g, ln_b, aff_w, aff_b):
            normed = layer_norm(x, ln_g, ln_b)
            affine = t_emb @ aff_w + aff_b
            gamma, beta = jnp.split(affine, 2, axis=-1)
            return gamma[:, None, :] * normed + beta[:, None, :]

        def mha(q_in, k_in, v_in, qw, qb, kw, kb, vw, vb, ow, ob):
            Bq, Lq, _ = q_in.shape
            Lk = k_in.shape[1]
            Q = (q_in @ qw + qb).reshape(Bq, Lq, H, DH)
            K = (k_in @ kw + kb).reshape(Bq, Lk, H, DH)
            V = (v_in @ vw + vb).reshape(Bq, Lk, H, DH)
            scores = jnp.einsum('bqhd,bkhd->bhqk', Q, K) / np.sqrt(DH).astype(np.float32)
            attn = jax.nn.softmax(scores, axis=-1)
            out = jnp.einsum('bhqk,bkhd->bqhd', attn, V).reshape(Bq, Lq, D)
            return out @ ow + ob
        xn = ada_ln(x, t_emb, ln1_g, ln1_b, aff1_w, aff1_b)
        x = x + mha(xn, xn, xn, sa_qw, sa_qb, sa_kw, sa_kb, sa_vw, sa_vb, sa_ow, sa_ob)
        x = x + mha(x, u, u, ca_qw, ca_qb, ca_kw, ca_kb, ca_vw, ca_vb, ca_ow, ca_ob)
        xn = ada_ln(x, t_emb, ln2_g, ln2_b, aff2_w, aff2_b)
        h = jax.nn.gelu(xn @ ffn_w1 + ffn_b1, approximate=False)
        x = x + (h @ ffn_w2 + ffn_b2)
        return x
    x = _L0_xcond_ref(x, cond_1024, ctx_1024, L0_xcond_adaLN_W, L0_xcond_adaLN_b, L0_xcond_norm1_w, L0_xcond_qkv_W, L0_xcond_attn_out_W, L0_xcond_normc_w, L0_xcond_cq_W, L0_xcond_ck_W, L0_xcond_cv_W, L0_xcond_co_W, L0_xcond_norm2_w, L0_xcond_mlp_W1, L0_xcond_mlp_b1, L0_xcond_mlp_W2, L0_xcond_mlp_b2, mask_BxS2_bf1, mask_SxS_bk0)
    x = _L1_xcond_ref(x, cond_1024, ctx_1024, L1_xcond_ln_gamma, L1_xcond_ln_beta, L1_xcond_Wq, L1_xcond_Wk, L1_xcond_Wv, L1_xcond_router_W, L1_xcond_router_b, L1_xcond_e_w1, L1_xcond_e_b1, L1_xcond_e_w2, L1_xcond_e_b2, L1_xcond_gate_w1, L1_xcond_gate_b1, L1_xcond_gate_w2, L1_xcond_gate_b2, L1_xcond_out_w, L1_xcond_out_b)
    x = _L2_xcond_ref(x, ctx_1024, cond_1024, L2_xcond_Wq, L2_xcond_bq, L2_xcond_Wkv, L2_xcond_bkv, L2_xcond_Wp, L2_xcond_bp, L2_xcond_Wss_q, L2_xcond_bss_q, L2_xcond_Wss_kv, L2_xcond_bss_kv)
    x = _L3_xcond_ref(x, ctx_1024, cond_1024, L3_xcond_ln1_g, L3_xcond_ln1_b, L3_xcond_aff1_w, L3_xcond_aff1_b, L3_xcond_ln2_g, L3_xcond_ln2_b, L3_xcond_aff2_w, L3_xcond_aff2_b, L3_xcond_sa_qw, L3_xcond_sa_qb, L3_xcond_sa_kw, L3_xcond_sa_kb, L3_xcond_sa_vw, L3_xcond_sa_vb, L3_xcond_sa_ow, L3_xcond_sa_ob, L3_xcond_ca_qw, L3_xcond_ca_qb, L3_xcond_ca_kw, L3_xcond_ca_kb, L3_xcond_ca_vw, L3_xcond_ca_vb, L3_xcond_ca_ow, L3_xcond_ca_ob, L3_xcond_ffn_w1, L3_xcond_ffn_b1, L3_xcond_ffn_w2, L3_xcond_ffn_b2)
    return x

_drawn_inputs = setup_inputs


def setup_inputs(seed=0):
    import zlib

    import numpy as np

    out = dict(_drawn_inputs(seed))
    spreads = {'L0_xcond_norm1_w': (1.0, 0.6),
     'L0_xcond_normc_w': (1.0, 0.6),
     'L0_xcond_norm2_w': (1.0, 0.6),
     'L1_xcond_ln_gamma': (1.0, 0.6),
     'L1_xcond_ln_beta': (0.0, 2.0),
     'L1_xcond_router_b': (0.0, 1.179),
     'L1_xcond_e_b1': (0.0, 1.382),
     'L1_xcond_e_b2': (0.0, 0.8),
     'L1_xcond_gate_b1': (0.0, 2.0),
     'L1_xcond_gate_b2': (0.0, 2.0),
     'L1_xcond_out_b': (0.0, 0.611),
     'L2_xcond_bq': (0.0, 2.0),
     'L2_xcond_bkv': (0.0, 1.308),
     'L2_xcond_bp': (0.0, 0.328),
     'L2_xcond_bss_q': (0.0, 2.0),
     'L2_xcond_bss_kv': (0.0, 2.0),
     'L3_xcond_ln1_g': (1.0, 0.6),
     'L3_xcond_ln1_b': (0.0, 0.8),
     'L3_xcond_aff1_b': (0.0, 0.8),
     'L3_xcond_ln2_g': (1.0, 0.6),
     'L3_xcond_ln2_b': (0.0, 0.8),
     'L3_xcond_aff2_b': (0.0, 0.8),
     'L3_xcond_sa_qb': (0.0, 0.8),
     'L3_xcond_sa_kb': (0.0, 2.0),
     'L3_xcond_sa_vb': (0.0, 1.451),
     'L3_xcond_sa_ob': (0.0, 0.353),
     'L3_xcond_ca_qb': (0.0, 2.0),
     'L3_xcond_ca_kb': (0.0, 2.0),
     'L3_xcond_ca_vb': (0.0, 1.663),
     'L3_xcond_ca_ob': (0.0, 0.332),
     'L3_xcond_ffn_b1': (0.0, 1.061),
     'L3_xcond_ffn_b2': (0.0, 0.37)}
    factors = {'L0_xcond_adaLN_W': 3.193,
     'L0_xcond_adaLN_b': 8.0,
     'L0_xcond_qkv_W': 6.097,
     'L0_xcond_attn_out_W': 6.097,
     'L0_xcond_cq_W': 8.0,
     'L0_xcond_ck_W': 8.0,
     'L0_xcond_cv_W': 8.0,
     'L0_xcond_co_W': 8.0,
     'L0_xcond_mlp_W1': 4.308,
     'L0_xcond_mlp_b1': 8.0,
     'L0_xcond_mlp_W2': 4.19,
     'L0_xcond_mlp_b2': 8.0,
     'L2_xcond_Wq': 64.0,
     'L2_xcond_Wss_q': 64.0,
     'L2_xcond_Wss_kv': 27.089,
     'L3_xcond_aff1_w': 5.104,
     'L3_xcond_aff2_w': 3.283,
     'L3_xcond_sa_qw': 8.0,
     'L3_xcond_sa_kw': 8.0,
     'L3_xcond_sa_vw': 4.517,
     'L3_xcond_ca_qw': 40.151,
     'L3_xcond_ca_kw': 39.927,
     'L3_xcond_ffn_w1': 3.028,
     'L1_xcond_Wq': 3.864,
     'L1_xcond_Wk': 4.146,
     'L1_xcond_gate_w1': 3.499,
     'L1_xcond_gate_w2': 2.679,
     'L2_xcond_Wkv': 3.039,
     'L3_xcond_ca_vw': 4.292}
    for name, (base, spread) in spreads.items():
        noise = np.random.default_rng([zlib.crc32(name.encode()), seed]).standard_normal(out[name].shape)
        drawn = base * np.exp(spread * noise) if base else spread * noise
        out[name] = jnp.asarray(drawn.astype(out[name].dtype))
    for name, factor in factors.items():
        out[name] = (out[name] * factor).astype(out[name].dtype)
    return out
```

```python
from contextlib import ExitStack

import numpy as np

import concourse.bass as bass
from concourse import mybir

F32 = mybir.dt.float32
BF16 = mybir.dt.bfloat16
U8 = mybir.dt.uint8
U32 = mybir.dt.uint32
ALU = mybir.AluOpType
ACT = mybir.ActivationFunctionType
AX_X = mybir.AxisListType.X

B, S, D = 32, 128, 128
NH, HD = 16, 8
NG, NJ, TILE = 4, 4, 32
SK = 77
NE, RH, DFF = 3, 256, 512
EPS = 1e-5
HEAD_SCALE = float(HD) ** -0.5
L1_SCALE = float(D) ** -0.5
VW = HD + 1
ONE_ROW = HD
MASKED = -(2.0 ** 96)
QUAD = 4

PACKS = [
    ("const", [("ident", 128), ("one_row", 1), ("rope_cos", 128), ("rope_sin", 128),
               ("spread", NG * 128), ("pick_den", 2 * 128), ("ones", 128)]),
    ("cond", [("condT", B)]),
    ("w_ada", [("l0_ada", 9 * D), ("l0_ada_b", 9), ("l0_norm1", 1), ("l0_normc", 1), ("l0_norm2", 1)]),
    ("w_l0", [("l0_q", D), ("l0_qswap", D), ("l0_k", D), ("l0_kswap", D), ("l0_v", D), ("l0_o", 2 * D),
              ("l0c_q", 512), ("l0c_k", 512), ("l0c_v", D), ("l0c_o", 2 * D)]),
    ("w_mlp", [("l0_w1", DFF), ("l0_b1", 4), ("l0_w2", 4 * D), ("l0_b2", 1)]),
    ("w_l1", [("l1_gamma", 1), ("l1_beta", 1), ("l1_q", D), ("l1_k", D), ("l1_v", D),
              ("l1_router", 3 * NE), ("l1_router_b", 1),
              ("l1_w1", 3 * NE * RH), ("l1_b1", 6), ("l1_w2", 6 * D), ("l1_b2row", NE * D),
              ("l1_gw1", 3 * D), ("l1_gb1", 1), ("l1_gw2", D), ("l1_gb2", 1), ("l1_ow", D), ("l1_ob", 1)]),
    ("w_l2", [("l2_ssq", 2 * D), ("l2_ssq_b", 2), ("l2_sskv", 2 * D), ("l2_sskv_b", 2),
              ("l2_q", 512), ("l2_qb", 4), ("l2_k", 512), ("l2_kb", 4), ("l2_v", D), ("l2_vb", 2),
              ("l2_o", 2 * D), ("l2_ob", 1)]),
    ("w_l3", [("l3_aff1", 2 * D), ("l3_aff1_b", 2), ("l3_aff2", 2 * D), ("l3_aff2_b", 2),
              ("l3_ln1g", 1), ("l3_ln1b", 1), ("l3_ln2g", 1), ("l3_ln2b", 1),
              ("l3s_q", 512), ("l3s_qb", 4), ("l3s_k", 512), ("l3s_kb", 4), ("l3s_v", D), ("l3s_vb", 2),
              ("l3s_o", 2 * D), ("l3s_ob", 1),
              ("l3c_q", 512), ("l3c_qb", 4), ("l3c_k", 512), ("l3c_kb", 4), ("l3c_v", D), ("l3c_vb", 2),
              ("l3c_o", 2 * D), ("l3c_ob", 1),
              ("l3_w1", DFF), ("l3_b1", 4), ("l3_w2", 4 * D), ("l3_b2", 1)]),
]
PACK_COLS = {p: sum(n for _, n in items) for p, items in PACKS}


class Op:

    def __init__(self, sem):
        self.sem, self.signals, self.value = sem, False, None


class Lane:

    def __init__(self, sem):
        self.sem, self.queue = sem, []

    def do(self, issue, *after):
        op = Op(self.sem)
        self.queue.append((op, issue, [p for p in after if p is not None]))
        for p in after:
            if p is not None:
                p.signals = True
        return op

    def dma(self, issue, sem, *after):
        op = self.do(issue, *after)
        op.sem, op.value = sem, 16
        return op

    def number(self):
        n = 0
        for op, _, _ in self.queue:
            if op.value is None and op.signals:
                n += 1
                op.value = n

    def run(self, engine):
        seen = {}
        for op, issue, after in self.queue:
            need = {}
            for p in after:
                need[id(p.sem)] = max(need.get(id(p.sem), (0, None))[0], p.value), p.sem
            for key, (value, sem) in need.items():
                if seen.get(key, 0) < value:
                    engine.wait_ge(sem, value)
                    seen[key] = value
            ins = issue(engine)
            if op.sem is not self.sem:
                ins.then_inc(op.sem, 16)
            elif op.signals:
                ins.then_inc(op.sem, 1)


class Buf:

    def __init__(self, t):
        self.t, self.busy = t, []


def build(nc, a, out_xT):
    with ExitStack() as ctx:
        def sb(name, shape, dt=F32):
            return ctx.enter_context(nc.sbuf_tensor(name, shape, dt))

        def psum(name, shape):
            return ctx.enter_context(nc.psum_tensor(name, shape, F32))

        def sem(name):
            return ctx.enter_context(nc.semaphore(name))

        pe, dve, act, pool, sp = (Lane(sem(f"done_{n}")) for n in ("pe", "dve", "act", "pool", "sp"))

        xT = sb("xT", [D, B, S])
        ctxT = sb("ctxT", [D, B, SK])
        ctx_tok = [sb(f"ctx_tok{i}", [SK, QUAD, D]) for i in range(2)]
        normT = sb("normT", [D, B, S])
        evT = sb("evT", [D, B, S])
        packs = {p: sb("pack_" + p, [128, n]) for p, n in PACK_COLS.items()}
        W = {}
        for p, items in PACKS:
            at = 0
            for name, n in items:
                W[name] = packs[p][:, at:at + n]
                at += n
        pack_of = {name: p for p, items in PACKS for name, _ in items}

        loaded = {}

        def load(key, dst, src, after=None):
            loaded[key] = sp.dma(lambda e, d=dst, s=src: e.dma_start(d, s), sem("ld_" + key), after)

        load("const", packs["const"][:, :], a["const"])
        load("cond", packs["cond"][:, :], a["cond"])
        mask_qk = sb("mask_qk", [S, S // 4], U32)
        mask_kv = sb("mask_kv", [B, SK], U8)
        load("mask_qk", mask_qk[:, :], a["mask_qk"])
        load("mask_kv", mask_kv[:, :], a["mask_kv"])
        load("w_ada", packs["w_ada"][:, :], a["w_ada"])
        for c in range(B // QUAD):
            load(f"x{c}", xT[:, c * QUAD:(c + 1) * QUAD, :], a["xT"][:, c * QUAD:(c + 1) * QUAD, :])
            if c == 0:
                load("w_l0", packs["w_l0"][:, :], a["w_l0"])
                load("ctx", ctxT[:, :, :], a["ctxT"])
        for p in ("w_mlp", "w_l1", "w_l2", "w_l3"):
            load(p, packs[p][:, :], a[p])

        def L(name):
            return loaded[pack_of[name]]

        ident = W["ident"]

        scores = psum("scores", [128, NJ, 512])
        score_busy = [None] * NJ
        qbank = [Buf(psum(f"qbank{i}", [128, 512])) for i in range(2)]
        work_free = [Buf(psum(f"work{i}", [128, 512])) for i in range(2)]

        def take():
            assert work_free, "no free work bank"
            return work_free.pop(0)

        def give(buf, *last):
            buf.busy = list(last)
            work_free.append(buf)

        class Stream:
            def __init__(self, i):
                self.qbank = qbank[i]
                self.q = Buf(sb(f"q{i}", [128, NG, S]))
                self.qm = Buf(sb(f"qm{i}", [128, NG, S]))
                self.k = Buf(sb(f"k{i}", [128, NG, S]))
                self.v = Buf(sb(f"v{i}", [128, NJ, NG, TILE]))
                self.negmax = Buf(sb(f"negmax{i}", [128, NG, 128]))
                self.p = [Buf(sb(f"p{i}_{j}", [128, NG, S])) for j in range(NJ)]
                self.stats = Buf(sb(f"stats{i}", [128, 6]))
                self.mv = Buf(sb(f"mv{i}", [128, 2]))
                self.lnv = Buf(sb(f"lnv{i}", [128, 1]))
                self.rstd = Buf(sb(f"rstd{i}", [128, 1]))
                self.xhat = Buf(sb(f"xhat{i}", [128, D]))
                self.xn = Buf(sb(f"xn{i}", [128, S]))
                self.osum = Buf(sb(f"osum{i}", [128, 2, S]))
                self.lden = Buf(sb(f"lden{i}", [128, 2, S]))
                self.rden = Buf(sb(f"rden{i}", [128, 2, S]))
                self.on = Buf(sb(f"on{i}", [128, 2, S]))
                self.rc = Buf(sb(f"rc{i}", [128, 2, S]))
                self.rs = Buf(sb(f"rs{i}", [128, 2, S]))
                self.rope = Buf(sb(f"rope{i}", [128, 2, S]))
                self.kvn = Buf(sb(f"kvn{i}", [128, SK]))
                self.ready = [
                    pool.do(lambda e, t=self.negmax.t: e.memset(t[:, :, :], 0.0)),
                    pool.do(lambda e, t=self.v.t: e.memset(t[:, :, :, :], 0.0)),
                ]
                v_zero = self.ready[1]
                for j in range(NJ):
                    c = (VW * j if j < 3 else 0) + HD
                    self.ready.append(pool.do(
                        lambda e, t=self.v.t, j=j, c=c: e.memset(t[:, j, :, c:c + 1], 1.0), v_zero))

        streams = [Stream(0), Stream(1)]
        x_last = [loaded[f"x{b // QUAD}"] for b in range(B)]

        def conditioned(name, weight, bias, chunks, rhs, rhs_ready):
            m = sb(name, [128, chunks, B])
            bank = take()
            for c in range(chunks):
                mm = pe.do(lambda e, c=c: e.matmul(bank.t[:, c * B:(c + 1) * B], weight[:, c * 128:(c + 1) * 128],
                                                   rhs, start=True, stop=True),
                           L(weight_name[id(weight)]), rhs_ready, *bank.busy)
            done = dve.do(lambda e: e.tensor_tensor(
                m[:, :, :], bank.t[:, 0:chunks * B].rearrange("p (c b) -> p c b", c=chunks),
                bias[:, 0:chunks].unsqueeze(2).to_broadcast([128, chunks, B]), ALU.add), mm)
            give(bank, done)
            return m, done

        weight_name = {id(w): n for n, w in W.items()}

        def affine_scale(name, src, src_done, weight, weight_done):
            t = sb(name, [128, B])
            return t, dve.do(lambda e: e.tensor_scalar(t[:, :], src, 1.0, weight, ALU.add, ALU.mult),
                             src_done, weight_done)

        condT = W["condT"]
        l0mod, l0mod_done = conditioned("l0mod", W["l0_ada"], W["l0_ada_b"], 9, condT, loaded["cond"])
        l0A = [affine_scale(f"l0A{i}", l0mod[:, 3 * i + 1, :], l0mod_done, W[w], L(w))
               for i, w in enumerate(("l0_norm1", "l0_normc", "l0_norm2"))]
        g_b2 = sb("g_b2", [128, B])

        mq = sb("mq", [S, S])
        live_q = sb("live_q", [S, 1])
        dead_q = sb("dead_q", [S, 1])
        lift_q = sb("lift_q", [S, S])
        neg_qk = sb("neg_qk", [S, S], BF16)
        neg_f = sb("neg_f", [S, S])
        neg_kq = sb("neg_kq", [S, S], BF16)
        ident_bf = sb("ident_bf", [128, 128], BF16)
        ones_bf = sb("ones_bf", [128, 128], BF16)
        cos_live = sb("cos_live", [128, 2, S])
        sin_live = sb("sin_live", [128, 2, S])
        live_rows = sb("live_rows", [S, 128])

        ident_bf_done = dve.do(lambda e: e.tensor_copy(ident_bf[:, :], ident), loaded["const"])
        ones_bf_done = dve.do(lambda e: e.tensor_copy(ones_bf[:, :], W["ones"]), loaded["const"])
        mq_done = dve.do(lambda e: e.tensor_copy(mq[:, :], mask_qk[:, :].bitcast(U8)), loaded["mask_qk"])
        live_done = dve.do(lambda e: e.tensor_reduce(live_q[:, :], mq[:, :], AX_X, ALU.max), mq_done)
        dead_done = dve.do(lambda e: e.tensor_scalar(dead_q[:, :], live_q[:, :], -1.0, 1.0, ALU.mult, ALU.add),
                           live_done)
        lift_done = dve.do(lambda e: e.tensor_scalar(lift_q[:, :], mq[:, :], dead_q[:, 0:1], -1.0,
                                                     ALU.max, ALU.add), dead_done)
        neg_f_done = dve.do(lambda e: e.tensor_scalar(neg_f[:, :], lift_q[:, :], -MASKED, None, ALU.mult), lift_done)
        neg_qk_done = dve.do(lambda e: e.tensor_copy(neg_qk[:, :], neg_f[:, :]), neg_f_done)
        live_rows_done = dve.do(lambda e: e.tensor_scalar(live_rows[:, :], W["ones"], live_q[:, 0:1], None, ALU.mult),
                                live_done)
        bank = take()
        pe.do(lambda e: e.transpose(bank.t[:, 0:S], neg_f[:, :], ident), neg_f_done, *bank.busy)
        mm = pe.do(lambda e: e.matmul(bank.t[:, S:2 * S], live_rows[:, :], ident, start=True, stop=True),
                   live_rows_done)
        neg_kq_done = dve.do(lambda e: e.tensor_copy(neg_kq[:, :], bank.t[:, 0:S]), mm)
        rope_tables = []
        for table, src in ((cos_live, W["rope_cos"]), (sin_live, W["rope_sin"])):
            rope_tables.append(dve.do(lambda e, t=table, s=src: e.tensor_tensor(
                t[:, 0, :], bank.t[:, S:2 * S], s, ALU.mult), mm))
            rope_tables.append(dve.do(lambda e, t=table, s=src: e.tensor_copy(t[:, 1, :], s)))
        give(bank, neg_kq_done, rope_tables[-2])

        mk = sb("mk", [B, SK])
        live_b = sb("live_b", [B, 1])
        dead_b = sb("dead_b", [B, 1])
        lift_b = sb("lift_b", [B, SK])
        neg_bk = sb("neg_bk", [B, SK])
        neg_bk_bf = sb("neg_bk_bf", [B, SK], BF16)
        neg_row = sb("neg_row", [128, B, SK], BF16)
        neg_kb = sb("neg_kb", [SK, B])
        live_diag = sb("live_diag", [B, B])
        live_bc = sb("live_bc", [128, B])
        mk_done = dve.do(lambda e: e.tensor_copy(mk[:, :], mask_kv[:, :]), loaded["mask_kv"])
        live_b_done = dve.do(lambda e: e.tensor_reduce(live_b[:, :], mk[:, :], AX_X, ALU.max), mk_done)
        dead_b_done = dve.do(lambda e: e.tensor_scalar(dead_b[:, :], live_b[:, :], -1.0, 1.0, ALU.mult, ALU.add),
                             live_b_done)
        lift_b_done = dve.do(lambda e: e.tensor_scalar(lift_b[:, :], mk[:, :], dead_b[:, 0:1], -1.0,
                                                       ALU.max, ALU.add), dead_b_done)
        neg_bk_done = dve.do(lambda e: e.tensor_scalar(neg_bk[:, :], lift_b[:, :], -MASKED, None, ALU.mult),
                             lift_b_done)
        neg_bk_bf_done = dve.do(lambda e: e.tensor_copy(neg_bk_bf[:, :], neg_bk[:, :]), neg_bk_done)
        neg_row_done = [sp.dma(lambda e, p=TILE * j: e.dma_start(neg_row[p:p + 1, :, :], neg_bk_bf[:, :]),
                               sem(f"ld_neg_row{j}"), neg_bk_bf_done) for j in range(NJ)]
        diag_done = dve.do(lambda e: e.tensor_scalar(live_diag[:, :], ident[0:B, 0:B], live_b[:, 0:1], None, ALU.mult),
                           live_b_done)
        bank = take()
        pe.do(lambda e: e.transpose(bank.t[0:SK, 0:B], neg_bk[:, :], ident[0:B, 0:B]), neg_bk_done, *bank.busy)
        mm = pe.do(lambda e: e.matmul(bank.t[:, 128:128 + B], W["ones"][0:B, :], live_diag[:, :], start=True, stop=True),
                   diag_done)
        neg_kb_done = dve.do(lambda e: e.tensor_copy(neg_kb[:, :], bank.t[0:SK, 0:B]), mm)
        live_bc_done = dve.do(lambda e: e.tensor_copy(live_bc[:, :], bank.t[:, 128:128 + B]), mm)
        give(bank, neg_kb_done, live_bc_done)

        def layer_norm(st, src, src_done, n, scale, bias, affine_done, dst, dst_busy, token_major=False):
            if token_major:
                tokens, tokens_done, bank = src, src_done, None
            else:
                bank = take()
                tokens_done = pe.do(lambda e: e.transpose(bank.t[0:n, 0:D], src, ident), src_done, *bank.busy)
                tokens = bank.t[0:n, 0:D]
            stats_done = dve.do(lambda e: e.bn_stats(st.stats.t[0:n, :], tokens), tokens_done)
            mv_done = dve.do(lambda e: e.bn_aggr(st.mv.t[0:n, :], st.stats.t[0:n, :]), stats_done, *st.mv.busy)
            yield
            ln_done = act.do(lambda e: e.activation(st.lnv.t[0:n, :], st.mv.t[0:n, 1:2], ACT.Ln,
                                                    bias=eps_col[0:n, 0:1]), mv_done, eps_done)
            rstd_done = act.do(lambda e: e.activation(st.rstd.t[0:n, :], st.lnv.t[0:n, :], ACT.Exp, scale=-0.5),
                               ln_done, *st.rstd.busy)
            yield
            xhat_done = dve.do(lambda e: e.tensor_scalar(st.xhat.t[0:n, :], tokens, st.mv.t[0:n, 0:1],
                                                         st.rstd.t[0:n, 0:1], ALU.subtract, ALU.mult),
                               rstd_done, *st.xhat.busy)
            st.mv.busy = [ln_done]
            st.rstd.busy = [xhat_done]
            if bank:
                give(bank, xhat_done)
            yield
            back = take()
            turned = pe.do(lambda e: e.transpose(back.t[:, 0:n], st.xhat.t[0:n, :], ident[0:n, 0:n]),
                           xhat_done, *back.busy)
            st.xhat.busy = [turned]
            st.ln_done = act.do(lambda e: e.activation(dst, back.t[:, 0:n], ACT.Identity, bias=bias, scale=scale),
                                turned, affine_done, *dst_busy)
            give(back, st.ln_done)
            yield

        eps_col = sb("eps_col", [128, 1])
        eps_done = pool.do(lambda e: e.memset(eps_col[:, :], EPS))

        def project_qk(dst, weight, weight_done, srcT, src_done, n, busy):
            for g in range(NG):
                mm = pe.do(lambda e, g=g: e.matmul(dst[:, g * S:g * S + n], weight[:, g * 128:(g + 1) * 128], srcT,
                                                   start=(g == 0), stop=(g == NG - 1), skip_group_check=True),
                           weight_done, src_done, *busy)
            return mm

        def groups(t, n=S):
            return t[:, :].rearrange("p (g s) -> p g s", g=NG)[:, :, 0:n]

        def column(t, n):
            return t[:, 0:NG].unsqueeze(2).to_broadcast([128, NG, n])

        def values(st, srcT, src_done, n, weight, weight_done):
            bank = take()
            mm = pe.do(lambda e: e.matmul(bank.t[0:n, 0:D], srcT, weight, start=True, stop=True),
                       weight_done, src_done, *bank.busy)
            flat = st.v.t[0:n, :, :, :].rearrange("p j g c -> p (j g c)")
            shifted = []
            for j in range(NJ):
                c = VW * j if j < 3 else 0
                shifted.append(act.do(lambda e, j=j, c=c: e.copy(
                    st.v.t[0:n, j, :, c:c + HD],
                    bank.t[0:n, 32 * j:32 * j + 32].rearrange("p (g d) -> p g d", g=NG)),
                    mm, *st.v.busy, *st.ready))
            give(bank, shifted[-1])
            return shifted[-1]

        def score_steps(st, nk, q_done, k_done, v_done, second_q, mask):
            n_head = [slice(TILE * j, TILE * j + TILE) for j in range(NJ)]
            max_done = []
            for j in range(NJ):
                rows, start = n_head[j], True
                if mask and mask[0] == "qk":
                    pe.do(lambda e, j=j: e.matmul(
                        scores[:, j, :].rearrange("p (g k) -> p g k", g=NG), ident_bf[:, :],
                        neg_qk[:, :].unsqueeze(1).to_broadcast([S, NG, S]), start=True, stop=False,
                        skip_group_check=True), score_busy[j], neg_qk_done, ident_bf_done)
                    start = False
                elif mask:
                    pe.do(lambda e, j=j, p=TILE * j: e.matmul(
                        scores[:, j, :].rearrange("p (g k) -> p g k", g=NG)[:, :, 0:nk], ones_bf[p:p + 1, :],
                        neg_row[p:p + 1, mask[1]:mask[1] + 1, :].to_broadcast([1, NG, SK]), start=True, stop=False,
                        skip_group_check=True, tile_position=(p, 0)), score_busy[j], neg_row_done[j], ones_bf_done)
                    start = False
                for g in range(NG):
                    mm = pe.do(lambda e, j=j, g=g, rows=rows, first=start and g == 0: e.matmul(
                        scores[:, j, g * S:g * S + nk], st.q.t[rows, g, :], st.k.t[rows, g, 0:nk],
                        start=first, stop=(g == NG - 1), skip_group_check=True, tile_position=(rows.start, 0)),
                        q_done, k_done, score_busy[j])
                c = TILE * j + ONE_ROW
                max_done.append(dve.do(lambda e, j=j, c=c: e.tensor_reduce(
                    st.negmax.t[:, :, c:c + 1].rearrange("p g o -> p (g o)"),
                    scores[:, j, :].rearrange("p (g k) -> p g k", g=NG)[:, :, 0:nk], AX_X, ALU.max, negate=True),
                    mm, *st.negmax.busy, *st.ready))
                st.q.busy = [mm]
                yield
            yield
            for g in range(NG):
                mm = pe.do(lambda e, g=g: e.matmul(st.qbank.t[:, g * S:(g + 1) * S], st.negmax.t[:, g, :], ident,
                                                   start=False, stop=(g == NG - 1), skip_group_check=True),
                           max_done[-1], q_done)
            st.negmax.busy = [mm]
            qm_done = second_q(mm)
            yield
            st.exp_done = []
            for j in range(NJ):
                rows, start = n_head[j], True
                if mask and mask[0] == "qk":
                    pe.do(lambda e, j=j: e.matmul(
                        scores[:, j, :].rearrange("p (g q) -> p g q", g=NG), ident_bf[:, :],
                        neg_kq[:, :].unsqueeze(1).to_broadcast([S, NG, S]), start=True, stop=False,
                        skip_group_check=True), max_done[j], neg_kq_done)
                    start = False
                for g in range(NG):
                    mm = pe.do(lambda e, j=j, g=g, rows=rows, first=start and g == 0: e.matmul(
                        scores[0:nk, j, g * S:(g + 1) * S], st.k.t[rows, g, 0:nk], st.qm.t[rows, g, :],
                        start=first, stop=(g == NG - 1), skip_group_check=True, tile_position=(rows.start, 0)),
                        qm_done, max_done[j])
                hide = neg_kb[:, mask[1]:mask[1] + 1] if mask and mask[0] == "kv" else 0.0
                done = act.do(lambda e, j=j, hide=hide: e.activation(
                    st.p[j].t[0:nk, :, :], scores[0:nk, j, :].rearrange("p (g q) -> p g q", g=NG), ACT.Exp,
                    bias=hide, scale=HEAD_SCALE), mm, *st.p[j].busy, neg_kb_done)
                score_busy[j] = done
                st.exp_done.append(done)
                yield
            st.qm.busy = [mm]
            st.k.busy = [mm]
            st.v_done = v_done
            st.nk = nk

        def attend(st, b, wo, wo_done, finish):
            nk = st.nk
            obank = take()
            for j in range(NJ):
                blk = 1 if j == 3 else 0
                for g in range(NG):
                    mm = pe.do(lambda e, j=j, g=g, blk=blk: e.matmul(
                        obank.t[TILE * g:TILE * g + TILE, blk * S:(blk + 1) * S], st.v.t[0:nk, j, g, :],
                        st.p[j].t[0:nk, g, :], start=(j == 0 or j == 3), stop=(j >= 2), skip_group_check=True,
                        tile_position=(0, TILE * g)), st.v_done, st.exp_done[j], *obank.busy)
                st.p[j].busy = [mm]
                yield
            st.v.busy = [mm]
            both = obank.t[:, 0:2 * S].rearrange("p (c s) -> p c s", c=2)
            os_done = act.do(lambda e: e.copy(st.osum.t[:, :, :], both), mm, *st.osum.busy)
            yield
            dbank = take()
            for c in range(2):
                mm = pe.do(lambda e, c=c: e.matmul(dbank.t[:, c * S:(c + 1) * S], W["pick_den"][:, c * 128:(c + 1) * 128],
                                                   st.osum.t[:, c, :], start=True, stop=True), os_done, *dbank.busy)
            st.osum.busy = [mm]
            ld_done = act.do(lambda e: e.activation(st.lden.t[:, :, :], dbank.t[:, 0:2 * S].rearrange(
                "p (c s) -> p c s", c=2), ACT.Ln), mm)
            rd_done = act.do(lambda e: e.activation(st.rden.t[:, :, :], st.lden.t[:, :, :], ACT.Exp, scale=-1.0),
                             ld_done, *st.rden.busy)
            yield
            on_done = dve.do(lambda e: e.tensor_tensor(st.on.t[:, :, :], both, st.rden.t[:, :, :], ALU.mult),
                             rd_done, *st.on.busy)
            st.rden.busy = [on_done]
            give(obank, on_done)
            yield
            for c in range(2):
                mm = pe.do(lambda e, c=c: e.matmul(dbank.t[:, 0:S], wo[:, c * D:(c + 1) * D], st.on.t[:, c, :],
                                                   start=(c == 0), stop=(c == 1)), on_done, wo_done, ld_done)
            st.on.busy = [mm]
            x_last[b] = finish(dbank.t[:, 0:S], mm)
            give(dbank, x_last[b])
            yield

        def gated(b, gate, gate_done):
            return lambda o, mm: dve.do(lambda e: e.scalar_tensor_tensor(
                xT[:, b, :], o, gate, xT[:, b, :], ALU.mult, ALU.add), mm, gate_done)

        def biased(b, bias, bias_done):
            return lambda o, mm: dve.do(lambda e: e.scalar_tensor_tensor(
                xT[:, b, :], o, bias, xT[:, b, :], ALU.add, ALU.add), mm, bias_done)

        one_row = W["one_row"]

        def l0_self_head(st, b):
            yield from layer_norm(st, xT[:, b, :], x_last[b], S, l0A[0][0][:, b:b + 1], l0mod[:, 0, b:b + 1],
                                  l0A[0][1], st.xn.t[:, :], st.xn.busy)
            bank = take()
            for i, w in enumerate(("l0_q", "l0_k", "l0_qswap", "l0_kswap")):
                mm = pe.do(lambda e, i=i, w=w: e.matmul(bank.t[:, i * S:(i + 1) * S], W[w], st.xn.t[:, :],
                                                        start=True, stop=True), st.ln_done, L(w), *bank.busy)
            v_done = values(st, st.xn.t[:, :], st.ln_done, S, W["l0_v"], L("l0_v"))
            yield
            half = lambda i: bank.t[:, i * 2 * S:(i + 1) * 2 * S].rearrange("p (c s) -> p c s", c=2)
            rc = dve.do(lambda e: e.tensor_tensor(st.rc.t[:, :, :], half(0), cos_live[:, :, :], ALU.mult),
                        mm, *rope_tables, *st.rc.busy)
            rs = dve.do(lambda e: e.tensor_tensor(st.rs.t[:, :, :], half(1), sin_live[:, :, :], ALU.mult), mm)
            give(bank, rs)
            rope_done = dve.do(lambda e: e.tensor_tensor(st.rope.t[:, :, :], st.rc.t[:, :, :], st.rs.t[:, :, :],
                                                         ALU.add), rc, rs, *st.rope.busy)
            yield
            q_mm = project_qk(st.qbank.t, W["spread"], rope_done, st.rope.t[:, 0, :], rope_done, S, st.qbank.busy)
            q_done = act.do(lambda e: e.copy(st.q.t[:, :, :], groups(st.qbank.t)), q_mm, *st.q.busy)
            yield
            bank2 = take()
            k_mm = project_qk(bank2.t, W["spread"], rope_done, st.rope.t[:, 1, :], rope_done, S, bank2.busy)
            k_done = act.do(lambda e: e.activation(st.k.t[:, :, :], groups(bank2.t), ACT.Identity,
                                                   bias=one_row[:, 0:1]), k_mm, *st.k.busy)
            give(bank2, k_done)
            st.rope.busy = [k_mm]
            st.xn.busy = [v_done, mm]
            yield

            def second_q(mm):
                done = dve.do(lambda e: e.tensor_copy(st.qm.t[:, :, :], groups(st.qbank.t)), mm, *st.qm.busy)
                st.qbank.busy = [done]
                return done

            st.scoring = lambda: score_steps(st, S, q_done, k_done, v_done, second_q, ("qk",))
            st.tail = lambda: attend(st, b, W["l0_o"], L("l0_o"), gated(b, l0mod[:, 2, b:b + 1], l0mod_done))

        def cross_head(st, b, q_src, q_src_done, kv_src, kv_done, nk, names, q_bias, k_bias, live, mask, tail):
            wq, wk, wv = names
            q_mm = project_qk(st.qbank.t, W[wq], L(wq), q_src, q_src_done, S, st.qbank.busy)

            def evict_q(dst, mm, *busy):
                if live is not None:
                    return dve.do(lambda e: e.tensor_scalar(dst[:, :, :], groups(st.qbank.t), live, None, ALU.mult),
                                  mm, live_bc_done, *busy)
                return dve.do(lambda e: e.tensor_tensor(dst[:, :, :], groups(st.qbank.t), column(q_bias[0], S),
                                                        ALU.add), mm, q_bias[1], *busy)

            q_done = evict_q(st.q.t, q_mm, *st.q.busy)
            yield
            bank = take()
            k_mm = project_qk(bank.t, W[wk], L(wk), kv_src, kv_done, nk, bank.busy)
            if k_bias is None:
                k_done = act.do(lambda e: e.activation(st.k.t[:, :, 0:nk], groups(bank.t, nk), ACT.Identity,
                                                       bias=one_row[:, 0:1]), k_mm, *st.k.busy)
            else:
                k_done = dve.do(lambda e: e.tensor_tensor(st.k.t[:, :, 0:nk], groups(bank.t, nk),
                                                          column(k_bias[0], nk), ALU.add),
                                k_mm, k_bias[1], *st.k.busy)
            give(bank, k_done)
            yield
            v_done = values(st, kv_src, kv_done, nk, W[wv], L(wv))
            st.src_read = v_done
            yield

            def second_q(mm):
                done = evict_q(st.qm.t, mm, *st.qm.busy)
                st.qbank.busy = [done]
                return done

            st.scoring = lambda: score_steps(st, nk, q_done, k_done, v_done, second_q, mask)
            st.tail = tail

        def l0_cross_head(st, b):
            yield from layer_norm(st, xT[:, b, :], x_last[b], S, l0A[1][0][:, b:b + 1], l0mod[:, 3, b:b + 1],
                                  l0A[1][1], st.xn.t[:, :], st.xn.busy)
            yield from cross_head(st, b, st.xn.t[:, :], st.ln_done, ctxT[:, b, :], loaded["ctx"], SK,
                                  ("l0c_q", "l0c_k", "l0c_v"), None, None, live_bc[:, b:b + 1], ("kv", b),
                                  lambda: attend(st, b, W["l0c_o"], L("l0c_o"),
                                                 gated(b, l0mod[:, 5, b:b + 1], l0mod_done)))
            st.xn.busy = [st.src_read]

        norm_done = [None] * B

        def l0_mlp_norm(st, b):
            yield from layer_norm(st, xT[:, b, :], x_last[b], S, l0A[2][0][:, b:b + 1], l0mod[:, 6, b:b + 1],
                                  l0A[2][1], normT[:, b, :], [])
            norm_done[b] = st.ln_done

        def chain(st, seqs, heads, after_tail):
            def fill(parts):
                for p in parts:
                    yield from p()
            pending = []
            for b in seqs:
                for h in heads:
                    parts = pending + [lambda h=h, b=b: h(st, b)]
                    yield fill(parts)
                    yield st.scoring()
                    pending = [st.tail]
                pending = pending + [lambda b=b: after_tail(st, b)] if after_tail else pending
            yield fill(pending)
            yield iter(())

        def merge(one, two):
            live = [g for g in (one, two) if g is not None]
            while live:
                for g in list(live):
                    try:
                        next(g)
                    except StopIteration:
                        live.remove(g)

        def both_streams(heads, after_tail=None):
            chains = [chain(streams[i], range(i, B, 2), heads, after_tail) for i in range(2)]
            one, two = chains
            held = next(one)
            merge(held, None)
            while True:
                a_score, b_fill = next(one, None), next(two, None)
                if a_score is None and b_fill is None:
                    break
                merge(a_score, b_fill)
                b_score, a_fill = next(two, None), next(one, None)
                merge(b_score, a_fill)

        both_streams([l0_self_head, l0_cross_head], l0_mlp_norm)

        hid = Buf([x.t[:, :, :].rearrange("p g s -> p (g s)")
                   for st in streams for x in (st.q, st.qm, st.k)])
        sig = streams[0].p[0:2]
        gate_h, gate = streams[0].p[2:4]
        mixT = streams[1].p[0]
        delta = streams[1].p[1:3]
        mix_in = Buf(streams[1].p[3].t[:, :, :].rearrange("p a b -> p (a b)"))
        dense_banks = [Buf(scores[:, j, :]) for j in range(NJ)] + qbank
        for j in range(NJ):
            dense_banks[j].busy = [score_busy[j]]
        turn = [0]

        def dense():
            turn[0] += 1
            return dense_banks[turn[0] % len(dense_banks)]

        def end_dense():
            for j in range(NJ):
                score_busy[j] = dense_banks[j].busy[-1]

        def mlp(c, w1, b1, w2, act_fn, finish):
            src = normT[:, c * QUAD:(c + 1) * QUAD, :].rearrange("p b s -> p (b s)")
            h = hid
            acts = []
            for f in range(4):
                bank = dense()
                mm = pe.do(lambda e, f=f, bank=bank: e.matmul(bank.t[:, :], W[w1][:, f * 128:(f + 1) * 128], src,
                                                              start=True, stop=True),
                           L(w1), *norm_done[c * QUAD:(c + 1) * QUAD], *bank.busy)
                acts.append(act.do(lambda e, f=f, bank=bank: e.activation(
                    h.t[f], bank.t[:, :], act_fn, bias=W[b1][:, f:f + 1]), mm, *h.busy))
                bank.busy = [acts[-1]]
            bank = dense()
            for f in range(4):
                mm = pe.do(lambda e, f=f: e.matmul(bank.t[:, :], W[w2][:, f * 128:(f + 1) * 128], h.t[f],
                                                   start=(f == 0), stop=(f == 3)), acts[f], L(w2), *bank.busy)
            h.busy = [mm]
            bank.busy = [finish(c, bank, mm)]

        g_b2_done = dve.do(lambda e: e.tensor_scalar(g_b2[:, :], l0mod[:, 8, :], W["l0_b2"][:, 0:1], None, ALU.mult),
                           l0mod_done, L("l0_b2"))

        def l0_mlp_out(c, bank, mm):
            t = delta[c % 2]
            for i in range(QUAD):
                b = c * QUAD + i
                done = act.do(lambda e, i=i, b=b: e.activation(
                    t.t[:, i, :], bank.t[:, i * S:(i + 1) * S], ACT.Identity, bias=g_b2[:, b:b + 1],
                    scale=l0mod[:, 8, b:b + 1]), mm, g_b2_done, *t.busy)
            seqs = slice(c * QUAD, (c + 1) * QUAD)
            added = pool.do(lambda e: e.tensor_tensor(xT[:, seqs, :], xT[:, seqs, :], t.t[:, :, :], ALU.add),
                            done, *x_last[seqs])
            t.busy = [added]
            x_last[seqs] = [added] * QUAD
            return done

        for c in range(B // QUAD):
            mlp(c, "l0_w1", "l0_b1", "l0_w2", ACT.Gelu_apprx_tanh, l0_mlp_out)
        end_dense()
        mlp_read = hid.busy[-1]

        def anchored(name, lhs, lhs_name, bias, chunks, width=128):
            m = sb(name, [128, chunks, B])
            bank = take()
            for c in range(chunks):
                mm = pe.do(lambda e, c=c: e.matmul(bank.t[0:width, c * B:(c + 1) * B],
                                                   lhs[:, c * width:(c + 1) * width], condT, start=True, stop=True),
                           L(lhs_name), *bank.busy)
            done = dve.do(lambda e: e.tensor_tensor(
                m[0:width, :, :], bank.t[0:width, 0:chunks * B].rearrange("p (c b) -> p c b", c=chunks),
                bias[0:width, 0:chunks].unsqueeze(2).to_broadcast([width, chunks, B]), ALU.add), mm)
            give(bank, done)
            return m, done

        h_anchor, h_anchor_done = anchored("h_anchor", W["l1_w1"][:, 2 * NE * RH:3 * NE * RH], "l1_w1", W["l1_b1"], 6)
        g_anchor, g_anchor_done = anchored("g_anchor", W["l1_gw1"][:, 2 * D:3 * D], "l1_gw1", W["l1_gb1"], 1)
        r_anchor, r_anchor_done = anchored("r_anchor", W["l1_router"][:, 2 * NE:3 * NE], "l1_router",
                                           W["l1_router_b"], 1, NE)
        b2_rows = sb("b2_rows", [128, NE * D])
        bank = take()
        mm = pe.do(lambda e: e.matmul(bank.t[:, 0:NE * D], W["ones"][0:1, :], W["l1_b2row"][0:1, :],
                                      start=True, stop=True), L("l1_b2row"), *bank.busy)
        b2_rows_done = dve.do(lambda e: e.tensor_copy(b2_rows[:, :], bank.t[:, 0:NE * D]), mm)
        give(bank, b2_rows_done)

        probs = sb("probs", [128, B, NE])
        l1_done = [None] * B

        class L1Buffers:
            def __init__(self, i):
                st = streams[i]
                self.q = Buf(st.osum.t[:, 0, :])
                self.k = Buf(st.osum.t[:, 1, 0:SK])
                self.v = Buf(st.lden.t[0:SK, 0, :])
                self.e = Buf(st.lden.t[:, 1, 0:SK])
                self.pn = Buf(st.rden.t[:, 0, 0:SK])
                self.pT = Buf(st.rden.t[0:SK, 1, :])
                self.lT = Buf(st.on.t[0:NE, 0, :])
                self.m = Buf(sb(f"l1m{i}", [128, 1]))
                self.den = Buf(sb(f"l1den{i}", [128, 1]))
                self.rden = Buf(sb(f"l1rden{i}", [128, 1]))
                self.rm = Buf(sb(f"l1rm{i}", [128, 1]))
                self.re = Buf(sb(f"l1re{i}", [128, NE]))
                self.rsum = Buf(sb(f"l1rsum{i}", [128, 1]))
                self.rr = Buf(sb(f"l1rr{i}", [128, 1]))
                self.qk_read = self.v_read = self.e_read = self.pn_read = self.pT_read = None
                self.lT_read = self.m_read = self.re_read = self.rm_read = None

        def l1_attention(st, t, banks, b):
            def use(k):
                return banks[k]
            nx = normT[:, b, :]
            yield from layer_norm(st, xT[:, b, :], x_last[b], S, W["l1_gamma"], W["l1_beta"], L("l1_gamma"),
                                  nx, [mlp_read])
            nx_done = st.ln_done
            qb, vb = use(0), use(1)
            q_mm = pe.do(lambda e: e.matmul(qb.t[:, 0:S], W["l1_q"], nx, start=True, stop=True), nx_done, *qb.busy)
            k_mm = pe.do(lambda e: e.matmul(qb.t[:, S:S + SK], W["l1_k"], ctxT[:, b, :], start=True, stop=True))
            v_mm = pe.do(lambda e: e.matmul(vb.t[0:SK, 0:D], ctxT[:, b, :], W["l1_v"], start=True, stop=True), *vb.busy)
            q_done = act.do(lambda e: e.activation(t.q.t, qb.t[:, 0:S], ACT.Copy, scale=L1_SCALE),
                            k_mm, t.qk_read)
            k_done = act.do(lambda e: e.copy(t.k.t, qb.t[:, S:S + SK]))
            v_done = dve.do(lambda e: e.tensor_copy(t.v.t, vb.t[0:SK, 0:D]), v_mm, t.v_read)
            yield
            s_mm = pe.do(lambda e: e.matmul(qb.t[:, 256:256 + SK], t.q.t, t.k.t, start=True, stop=True),
                         k_done)
            t.qk_read = s_mm
            m_done = dve.do(lambda e: e.tensor_reduce(t.m.t[:, :], qb.t[:, 256:256 + SK], AX_X, ALU.max, negate=True),
                            s_mm, t.m_read)
            yield
            e_done = act.do(lambda e: e.activation(t.e.t, qb.t[:, 256:256 + SK], ACT.Exp, bias=t.m.t[:, 0:1],
                                                   accum_out=t.den.t[:, :]), m_done, t.e_read)
            t.m_read = e_done
            qb.busy = [e_done]
            yield
            r_done = dve.do(lambda e: e.reciprocal(t.rden.t[:, :], t.den.t[:, :]), e_done)
            pn_done = dve.do(lambda e: e.tensor_scalar(t.pn.t, t.e.t, t.rden.t[:, 0:1], None, ALU.mult),
                             r_done, t.pn_read)
            t.e_read = pn_done
            yield
            t_mm = pe.do(lambda e: e.transpose(vb.t[0:SK, 128:128 + S], t.pn.t, ident), pn_done, v_done)
            t.pn_read = t_mm
            pT_done = act.do(lambda e: e.copy(t.pT.t, vb.t[0:SK, 128:128 + S]), t_mm, t.pT_read)
            yield
            ev_mm = pe.do(lambda e: e.matmul(vb.t[:, 256:256 + S], t.v.t, t.pT.t, start=True, stop=True),
                          pT_done, v_done)
            t.v_read = t.pT_read = ev_mm
            ev_done = dve.do(lambda e: e.tensor_copy(evT[:, b, :], vb.t[:, 256:256 + S]), ev_mm)
            yield
            pe.do(lambda e: e.matmul(qb.t[0:NE, 0:S], W["l1_router"][:, 0:NE], nx, start=True, stop=False),
                  *qb.busy)
            l_mm = pe.do(lambda e: e.matmul(qb.t[0:NE, 0:S], W["l1_router"][:, NE:2 * NE], evT[:, b, :],
                                            start=False, stop=True), ev_done)
            l_done = act.do(lambda e: e.activation(t.lT.t, qb.t[0:NE, 0:S], ACT.Identity,
                                                   bias=r_anchor[0:NE, 0, b:b + 1]), l_mm, r_anchor_done, t.lT_read)
            yield
            t.lT_read = lt_mm = pe.do(lambda e: e.transpose(qb.t[:, 256:256 + NE], t.lT.t, ident[0:NE, 0:NE]),
                                      l_done)
            rm_done = dve.do(lambda e: e.tensor_reduce(t.rm.t[:, :], qb.t[:, 256:256 + NE], AX_X, ALU.max,
                                                       negate=True), lt_mm, t.rm_read)
            yield
            re_done = act.do(lambda e: e.activation(t.re.t[:, :], qb.t[:, 256:256 + NE], ACT.Exp, bias=t.rm.t[:, 0:1],
                                                    accum_out=t.rsum.t[:, :]), rm_done, t.re_read)
            t.rm_read = re_done
            qb.busy = [re_done]
            vb.busy = [ev_done]
            yield
            rr_done = dve.do(lambda e: e.reciprocal(t.rr.t[:, :], t.rsum.t[:, :]), re_done)
            l1_done[b] = dve.do(lambda e: e.tensor_scalar(probs[:, b, :], t.re.t[:, :], t.rr.t[:, 0:1], None,
                                                          ALU.mult), rr_done)
            t.re_read = l1_done[b]
            yield

        l1_banks = [[Buf(scores[:, 0, :]), Buf(scores[:, 1, :])], [Buf(scores[:, 2, :]), Buf(scores[:, 3, :])]]
        for i in range(2):
            for k in range(2):
                l1_banks[i][k].busy = [score_busy[2 * i + k]]
        l1_buf = [L1Buffers(i) for i in range(2)]

        def l1_chain(i):
            for b in range(i, B, 2):
                yield from l1_attention(streams[i], l1_buf[i], l1_banks[i], b)

        chains = [l1_chain(0), l1_chain(1)]
        for _ in range(6):
            next(chains[0])
        merge(*chains)
        for i in range(2):
            for k in range(2):
                score_busy[2 * i + k] = l1_banks[i][k].busy[-1]
        for j in range(NJ):
            dense_banks[j].busy = [score_busy[j]]

        mix = [Buf(t) for t in (streams[0].rc.t[:, 0, :], streams[0].rc.t[:, 1, :], streams[0].rs.t[:, 0, :])]
        silu_c = sb("silu_c", [128, B])
        sig_c = sb("sig_c", [128, B])
        s1 = act.do(lambda e: e.activation(sig_c[:, :], condT, ACT.Sigmoid))
        silu_c_done = dve.do(lambda e: e.tensor_tensor(silu_c[:, :], condT, sig_c[:, :], ALU.mult), s1)

        def silu_of(bank, mm, anchor, anchor_done, chunk, c, dst, dst_busy, k):
            s = sig[k % 2]
            for i in range(QUAD):
                b = c * QUAD + i
                s_done = act.do(lambda e, i=i, b=b: e.activation(
                    s.t[:, i, :], bank.t[:, i * S:(i + 1) * S], ACT.Sigmoid, bias=anchor[:, chunk, b:b + 1]),
                    mm, anchor_done, *s.busy)
            for i in range(QUAD):
                b = c * QUAD + i
                done = dve.do(lambda e, i=i, b=b: e.scalar_tensor_tensor(
                    dst[:, i * S:(i + 1) * S], bank.t[:, i * S:(i + 1) * S], anchor[:, chunk, b:b + 1],
                    s.t[:, i, :], ALU.add, ALU.mult), s_done, *dst_busy)
            s.busy = [done]
            bank.busy = [done]
            return done

        def l1_experts(c):
            seqs = slice(c * QUAD, (c + 1) * QUAD)
            nx = normT[:, seqs, :].rearrange("p b s -> p (b s)")
            ev = evT[:, seqs, :].rearrange("p b s -> p (b s)")
            h = hid
            h_done = []
            for k in range(2 * NE):
                bank = dense()
                for part, src in ((0, nx), (1, ev)):
                    at = part * NE * RH + k * 128
                    mm = pe.do(lambda e, at=at, src=src, part=part, bank=bank: e.matmul(
                        bank.t[:, :], W["l1_w1"][:, at:at + 128], src, start=(part == 0), stop=(part == 1)),
                        *l1_done[seqs], *bank.busy)
                h_done.append(silu_of(bank, mm, h_anchor, h_anchor_done, k, c, h.t[k], h.busy, k))
            bank = dense()
            for part, src in ((0, nx), (1, ev)):
                mm = pe.do(lambda e, src=src, part=part, bank=bank: e.matmul(
                    bank.t[:, :], W["l1_gw1"][:, part * D:(part + 1) * D], src, start=(part == 0), stop=(part == 1)),
                    *bank.busy)
            gh = gate_h.t[:, :, :].rearrange("p b s -> p (b s)")
            gh_done = silu_of(bank, mm, g_anchor, g_anchor_done, 0, c, gh, gate_h.busy, 6)
            for i in range(QUAD):
                b = c * QUAD + i
                bank = dense()
                for x in range(NE):
                    for r in range(2):
                        k = 2 * x + r
                        mm = pe.do(lambda e, x=x, r=r, k=k, i=i, bank=bank: e.matmul(
                            bank.t[:, x * D:(x + 1) * D], h.t[k][:, i * S:(i + 1) * S],
                            W["l1_w2"][:, k * D:(k + 1) * D], start=(r == 0), stop=(r == 1)),
                            h_done[k], *bank.busy)
                in_done = dve.do(lambda e, bank=bank: e.tensor_tensor(mix_in.t[:, 0:NE * D], bank.t[:, 0:NE * D],
                                                                      b2_rows[:, :], ALU.add), mm)
                bank.busy = [in_done]
                m_done = dve.do(lambda e, b=b: e.tensor_scalar(mix[0].t, mix_in.t[:, 0:D], probs[:, b, 0:1],
                                                               None, ALU.mult), in_done)
                for x in range(1, NE):
                    m_done = dve.do(lambda e, b=b, x=x: e.scalar_tensor_tensor(
                        mix[x].t, mix_in.t[:, x * D:(x + 1) * D], probs[:, b, x:x + 1], mix[x - 1].t,
                        ALU.mult, ALU.add), m_done, *mix[x].busy)
                bank = dense()
                turned = pe.do(lambda e, bank=bank: e.transpose(bank.t[:, 0:S], mix[2].t, ident),
                               m_done, *bank.busy)
                mix[2].busy = [turned]
                mT_done = act.do(lambda e, i=i, bank=bank: e.copy(mixT.t[:, i, :], bank.t[:, 0:S]),
                                 turned, *mixT.busy)
                bank.busy = [mT_done]
            h.busy = [mm]
            bank = dense()
            g_mm = pe.do(lambda e, bank=bank: e.matmul(bank.t[:, :], W["l1_gw2"], gh, start=True, stop=True),
                         gh_done, *bank.busy)
            gate_h.busy = [g_mm]
            g_done = act.do(lambda e, bank=bank: e.activation(
                gate.t[:, :, :].rearrange("p b s -> p (b s)"), bank.t[:, :], ACT.Sigmoid, bias=W["l1_gb2"]),
                g_mm, *gate.busy)
            bank.busy = [g_done]
            bank = dense()
            o_mm = pe.do(lambda e, bank=bank: e.matmul(bank.t[:, :], W["l1_ow"], mixT.t[:, :, :].rearrange(
                "p b s -> p (b s)"), start=True, stop=True), mT_done, *bank.busy)
            mixT.busy = [o_mm]
            t = delta[c % 2]
            d_done = dve.do(lambda e, bank=bank: e.scalar_tensor_tensor(
                t.t[:, :, :].rearrange("p b s -> p (b s)"), bank.t[:, :], W["l1_ob"],
                gate.t[:, :, :].rearrange("p b s -> p (b s)"), ALU.add, ALU.mult), o_mm, g_done, *t.busy)
            gate.busy = [d_done]
            bank.busy = [d_done]
            added = pool.do(lambda e: e.tensor_tensor(xT[:, seqs, :], xT[:, seqs, :], t.t[:, :, :], ALU.add),
                            d_done, *x_last[seqs])
            t.busy = [added]
            x_last[seqs] = [added] * QUAD

        for c in range(B // QUAD):
            l1_experts(c)
        end_dense()
        experts_read = o_mm_last = hid.busy[-1]

        l2q, l2q_done = conditioned("l2q_mod", W["l2_ssq"], W["l2_ssq_b"], 2, silu_c[:, :], silu_c_done)
        l2k, l2k_done = conditioned("l2k_mod", W["l2_sskv"], W["l2_sskv_b"], 2, silu_c[:, :], silu_c_done)
        l2qA, l2qA_done = affine_scale("l2qA", l2q[:, 0, :], l2q_done, W["ones"][:, 0:1], None)
        l2kA, l2kA_done = affine_scale("l2kA", l2k[:, 0, :], l2k_done, W["ones"][:, 0:1], None)
        l3A, l3B, l3A_done = [], [], []
        for i, n in enumerate(("l3_aff1", "l3_aff2")):
            m, done = conditioned(f"l3mod{i}", W[n], W[n + "_b"], 2, condT, None)
            scale, shift = sb(f"l3A{i}", [128, B]), sb(f"l3B{i}", [128, B])
            dve.do(lambda e, m=m, t=scale, i=i: e.tensor_scalar(t[:, :], m[:, 0, :], W[f"l3_ln{i + 1}g"], None,
                                                                ALU.mult), done)
            l3A_done.append(dve.do(lambda e, m=m, t=shift, i=i: e.scalar_tensor_tensor(
                t[:, :], m[:, 0, :], W[f"l3_ln{i + 1}b"], m[:, 1, :], ALU.mult, ALU.add), done))
            l3A.append(scale)
            l3B.append(shift)

        def folded(name):
            bo = sb(name + "_bo", [128, 1])
            kb = sb(name + "_kb1", [128, NG])
            bank = take()
            for c in range(2):
                mm = pe.do(lambda e, c=c, bank=bank: e.matmul(
                    bank.t[:, 0:1], W[name + "_o"][:, c * D:(c + 1) * D], W[name + "_vb"][:, c:c + 1],
                    start=(c == 0), stop=(c == 1)), L(name + "_o"), *bank.busy)
            bo_done = dve.do(lambda e, bank=bank: e.tensor_scalar(bo[:, :], bank.t[:, 0:1], W[name + "_ob"], None,
                                                                  ALU.add), mm)
            give(bank, bo_done)
            kb_done = dve.do(lambda e: e.tensor_scalar(kb[:, :], W[name + "_kb"], one_row[:, 0:1], None, ALU.add))
            return (bo[:, 0:1], bo_done), (kb, kb_done)

        l2_bo, l2_kb = folded("l2")
        l3s_bo, l3s_kb = folded("l3s")
        l3c_bo, l3c_kb = folded("l3c")

        ctx_busy = [None, None]
        ctx_load = {}
        for c in range(B // QUAD):
            ctx_load[c] = None

        def l2_head(st, b):
            c, i = divmod(b, QUAD)
            if ctx_load[c] is None:
                ctx_load[c] = sp.dma(lambda e: e.dma_start(ctx_tok[c % 2][:, :, :],
                                                           a["ctx_tok"][:, c * QUAD:(c + 1) * QUAD, :]),
                                     sem(f"ld_ctx_tok{c}"), *(ctx_reads.get(c - 2) or []))
            yield from layer_norm(st, ctx_tok[c % 2][:, i, :], ctx_load[c], SK, l2kA[:, b:b + 1],
                                  l2k[:, 1, b:b + 1], l2kA_done, st.kvn.t[:, :], st.kvn.busy, token_major=True)
            kv_done = st.ln_done
            ctx_reads.setdefault(c, []).append(kv_done)
            yield from layer_norm(st, xT[:, b, :], x_last[b], S, l2qA[:, b:b + 1], l2q[:, 1, b:b + 1],
                                  l2qA_done, st.xn.t[:, :], st.xn.busy)
            yield from cross_head(st, b, st.xn.t[:, :], st.ln_done, st.kvn.t[:, :], kv_done, SK,
                                  ("l2_q", "l2_k", "l2_v"), (W["l2_qb"], L("l2_qb")), l2_kb, None, None,
                                  lambda: attend(st, b, W["l2_o"], L("l2_o"), biased(b, *l2_bo)))
            st.xn.busy = st.kvn.busy = [st.src_read]

        ctx_reads = {}

        def l3_self_head(st, b):
            yield from layer_norm(st, xT[:, b, :], x_last[b], S, l3A[0][:, b:b + 1], l3B[0][:, b:b + 1],
                                  l3A_done[0], st.xn.t[:, :], st.xn.busy)
            yield from cross_head(st, b, st.xn.t[:, :], st.ln_done, st.xn.t[:, :], st.ln_done, S,
                                  ("l3s_q", "l3s_k", "l3s_v"), (W["l3s_qb"], L("l3s_qb")), l3s_kb, None, None,
                                  lambda: attend(st, b, W["l3s_o"], L("l3s_o"), biased(b, *l3s_bo)))
            st.xn.busy = [st.src_read]

        def l3_cross_head(st, b):
            yield from cross_head(st, b, xT[:, b, :], x_last[b], ctxT[:, b, :], loaded["ctx"], SK,
                                  ("l3c_q", "l3c_k", "l3c_v"), (W["l3c_qb"], L("l3c_qb")), l3c_kb, None, None,
                                  lambda: attend(st, b, W["l3c_o"], L("l3c_o"), biased(b, *l3c_bo)))

        def l3_ffn_norm(st, b):
            yield from layer_norm(st, xT[:, b, :], x_last[b], S, l3A[1][:, b:b + 1], l3B[1][:, b:b + 1],
                                  l3A_done[1], normT[:, b, :], [experts_read])
            norm_done[b] = st.ln_done

        both_streams([l2_head, l3_self_head, l3_cross_head], l3_ffn_norm)

        for j in range(NJ):
            dense_banks[j].busy = [score_busy[j]]
        stores = []

        def l3_out(c, bank, mm):
            seqs = slice(c * QUAD, (c + 1) * QUAD)
            flat = xT[:, seqs, :].rearrange("p b s -> p (b s)")
            done = dve.do(lambda e: e.scalar_tensor_tensor(flat, bank.t[:, :], W["l3_b2"], flat, ALU.add, ALU.add),
                          mm, *x_last[seqs])
            stores.append(sp.dma(lambda e: e.dma_start(out_xT[:, seqs, :], xT[:, seqs, :]), sem(f"store{c}"), done))
            return done

        for c in range(B // QUAD):
            mlp(c, "l3_w1", "l3_b1", "l3_w2", ACT.Gelu, l3_out)

        lanes = (pe, dve, act, pool, sp)
        for lane in lanes:
            lane.number()
        block = ctx.enter_context(nc.Block())

        @block.tensor
        def _(e):
            pe.run(e)

        @block.vector
        def _(e):
            dve.run(e)

        @block.scalar
        def _(e):
            act.run(e)

        @block.gpsimd
        def _(e):
            pool.run(e)

        @block.sync
        def _(e):
            sp.run(e)
            for s in stores:
                e.wait_ge(s.sem, 16)


def _pad_qk(w):
    out = np.zeros((w.shape[0], NG, NJ, TILE), w.dtype)
    out[..., :HD] = w.reshape(w.shape[0], NG, NJ, HD)
    return out.reshape(w.shape[0], NG * NJ * TILE)


def _pad_qk_bias(b):
    return _pad_qk(b[None])[0].reshape(NG, 128).T


def _value_cols(w):
    n = w.shape[0]
    return w.reshape(n, NG, NJ, HD).transpose(0, 2, 1, 3).reshape(n, D)


def _pad_out(w):
    n = w.shape[1]
    heads = w.reshape(NG, NJ, HD, n)
    out = np.zeros((NG, TILE, 2, n), w.dtype)
    for j in range(NJ):
        at = VW * j if j < 3 else 0
        out[:, at:at + HD, 1 if j == 3 else 0, :] = heads[:, j]
    return out.reshape(128, 2 * n)


def _constants():
    ident = np.eye(128, dtype=np.float32)
    one_row = np.zeros((128, 1), np.float32)
    one_row[ONE_ROW::TILE] = 1.0
    n = S // 2
    inv_freq = 1.0 / 10000.0 ** (np.arange(0, HD, 2, dtype=np.float32) / HD)
    freqs = np.outer(np.arange(n, dtype=np.float32), inv_freq)
    emb = np.concatenate([freqs, freqs], axis=-1)
    sign = np.where(np.arange(HD) < HD // 2, -1.0, 1.0)
    cos = np.tile(np.tile(np.cos(emb).astype(np.float32).T, (NH, 1)), (1, 2))
    sin = np.tile(np.tile((np.sin(emb) * sign).astype(np.float32).T, (NH, 1)), (1, 2))
    spread = _pad_qk(ident)
    pick = np.zeros((128, 2, 128), np.float32)
    for g in range(NG):
        for r in range(TILE):
            j = r // VW if r < 3 * VW else 0
            pick[TILE * g + VW * j + HD, 0, TILE * g + r] = 1.0
            pick[TILE * g + HD, 1, TILE * g + r] = 1.0
    return {"ident": ident, "one_row": one_row, "rope_cos": cos, "rope_sin": sin, "spread": spread,
            "pick_den": pick.reshape(128, 256), "ones": np.ones((128, 128), np.float32)}


def _swap(w):
    return w.reshape(w.shape[0], NH, 2, HD // 2)[:, :, ::-1].reshape(w.shape[0], D)


def _col(v):
    return v.reshape(-1, 128).T


def _rows(w):
    return w.reshape(-1, 128, w.shape[1]).transpose(1, 0, 2).reshape(128, -1)


def _head_bias(b):
    return _pad_out(b[:, None]).reshape(128, 2)


def kernel(**inputs):
    import concourse.bacc as bacc
    from concourse.bass_utils import run_bass_kernel_spmd

    i = {k: np.asarray(v) for k, v in inputs.items()}
    z = lambda layer, name: i[f"{layer}_xcond_{name}"]
    p = _constants()
    p["condT"] = i["cond_1024"].T
    p["l0_ada"], p["l0_ada_b"] = z("L0", "adaLN_W"), _col(z("L0", "adaLN_b"))
    for n in ("norm1", "normc", "norm2"):
        p["l0_" + n] = _col(z("L0", n + "_w"))
    wq, wk, wv = (z("L0", "qkv_W")[:, c * D:(c + 1) * D] for c in range(3))
    p["l0_q"], p["l0_qswap"], p["l0_k"], p["l0_kswap"] = wq, _swap(wq), wk, _swap(wk)
    p["l0_v"], p["l0_o"] = _value_cols(wv), _pad_out(z("L0", "attn_out_W"))
    p["l0c_q"], p["l0c_k"] = _pad_qk(z("L0", "cq_W")), _pad_qk(z("L0", "ck_W"))
    p["l0c_v"], p["l0c_o"] = _value_cols(z("L0", "cv_W")), _pad_out(z("L0", "co_W"))
    for layer, n, names in (("L0", "l0", ("mlp_W1", "mlp_b1", "mlp_W2", "mlp_b2")),
                            ("L3", "l3", ("ffn_w1", "ffn_b1", "ffn_w2", "ffn_b2"))):
        p[n + "_w1"], p[n + "_b1"] = z(layer, names[0]), _col(z(layer, names[1]))
        p[n + "_w2"], p[n + "_b2"] = _rows(z(layer, names[2])), _col(z(layer, names[3]))
    p["l1_gamma"], p["l1_beta"] = _col(z("L1", "ln_gamma")), _col(z("L1", "ln_beta"))
    p["l1_q"], p["l1_k"], p["l1_v"] = z("L1", "Wq"), z("L1", "Wk"), z("L1", "Wv")
    p["l1_router"] = _rows(z("L1", "router_W"))
    rb = np.zeros((128, 1), np.float32)
    rb[:NE, 0] = z("L1", "router_b")
    p["l1_router_b"] = rb
    w1 = z("L1", "e_w1").transpose(1, 0, 2).reshape(3 * D, NE * RH)
    p["l1_w1"], p["l1_b1"] = _rows(w1), _col(z("L1", "e_b1"))
    p["l1_w2"] = _rows(z("L1", "e_w2").reshape(NE * RH, D))
    b2 = np.zeros((128, NE * D), np.float32)
    b2[0] = z("L1", "e_b2").reshape(-1)
    p["l1_b2row"] = b2
    p["l1_gw1"], p["l1_gb1"] = _rows(z("L1", "gate_w1")), _col(z("L1", "gate_b1"))
    p["l1_gw2"], p["l1_gb2"] = z("L1", "gate_w2"), _col(z("L1", "gate_b2"))
    p["l1_ow"], p["l1_ob"] = z("L1", "out_w"), _col(z("L1", "out_b"))
    p["l2_ssq"], p["l2_ssq_b"] = z("L2", "Wss_q"), _col(z("L2", "bss_q"))
    p["l2_sskv"], p["l2_sskv_b"] = z("L2", "Wss_kv"), _col(z("L2", "bss_kv"))
    kv, bkv = z("L2", "Wkv"), z("L2", "bkv")
    p["l3_aff1"], p["l3_aff1_b"] = z("L3", "aff1_w"), _col(z("L3", "aff1_b"))
    p["l3_aff2"], p["l3_aff2_b"] = z("L3", "aff2_w"), _col(z("L3", "aff2_b"))
    for n in ("ln1", "ln2"):
        p[f"l3_{n}g"], p[f"l3_{n}b"] = _col(z("L3", n + "_g")), _col(z("L3", n + "_b"))
    for n, (q, qb, k, kb, v, vb, o, ob) in {
        "l2": (z("L2", "Wq"), z("L2", "bq"), kv[:, :D], bkv[:D], kv[:, D:], bkv[D:], z("L2", "Wp"), z("L2", "bp")),
        "l3s": [z("L3", "sa_" + s) for s in ("qw", "qb", "kw", "kb", "vw", "vb", "ow", "ob")],
        "l3c": [z("L3", "ca_" + s) for s in ("qw", "qb", "kw", "kb", "vw", "vb", "ow", "ob")],
    }.items():
        p[n + "_q"], p[n + "_qb"] = _pad_qk(q), _pad_qk_bias(qb)
        p[n + "_k"], p[n + "_kb"] = _pad_qk(k), _pad_qk_bias(kb)
        p[n + "_v"], p[n + "_vb"] = _value_cols(v), _head_bias(vb)
        p[n + "_o"], p[n + "_ob"] = _pad_out(o), _col(ob)

    arrays = {name: np.ascontiguousarray(np.concatenate([p[n] for n, _ in items], axis=1))
              for name, items in PACKS}
    for name, items in PACKS:
        assert arrays[name].shape == (128, PACK_COLS[name]), name
    arrays["xT"] = np.ascontiguousarray(i["x"].transpose(2, 0, 1))
    arrays["ctxT"] = np.ascontiguousarray(i["ctx_1024"].transpose(2, 0, 1))
    arrays["ctx_tok"] = np.ascontiguousarray(i["ctx_1024"].transpose(1, 0, 2))
    arrays["mask_qk"] = np.ascontiguousarray(i["mask_SxS_bk0"]).view(np.uint32)
    arrays["mask_kv"] = np.ascontiguousarray(i["mask_BxS2_bf1"]).view(np.uint8)

    nc = bacc.Bacc("TRN2", target_bir_lowering=False, num_devices=1)
    aps = {n: nc.dram_tensor("in_" + n, v.shape, mybir.dt.from_np(v.dtype), kind="ExternalInput").ap()
           for n, v in arrays.items()}
    out = nc.dram_tensor("out_xT", (D, B, S), F32, kind="ExternalOutput").ap()
    build(nc, aps, out)
    r = run_bass_kernel_spmd(nc, [{"in_" + n: v for n, v in arrays.items()}], core_ids=[0])
    return np.ascontiguousarray(r.results[0]["out_xT"].transpose(1, 2, 0))
```

```python
from contextlib import ExitStack

import numpy as np

import concourse.bass as bass
from concourse import mybir

F32 = mybir.dt.float32
F32R = mybir.dt.float32r
BF16 = mybir.dt.bfloat16
U8 = mybir.dt.uint8
U32 = mybir.dt.uint32
ALU = mybir.AluOpType
ACT = mybir.ActivationFunctionType
AX_X = mybir.AxisListType.X

B, S, D = 32, 128, 128
NH, HD = 16, 8
NG, NJ, TILE = 4, 4, 32
SK = 77
NE, RH, DFF = 3, 256, 512
EPS = 1e-5
HEAD_SCALE = float(HD) ** -0.5
L1_SCALE = float(D) ** -0.5
VW = HD + 1
MASKED = -(2.0 ** 96)
QUAD = 4

PACKS = [
    ("const", [("ident", 128), ("rope_cos", 128), ("rope_sin", 128), ("own_head", NH),
               ("pick_den", 2 * 128), ("ones", 128)]),
    ("cond", [("condT", B)]),
    ("w_ada", [("l0_ada", 9 * D), ("l0_ada_b", 9), ("l0_norm1", 1), ("l0_normc", 1), ("l0_norm2", 1)]),
    ("w_l0", [("l0_q", D), ("l0_qswap", D), ("l0_k", D), ("l0_kswap", D), ("l0_v", D), ("l0_o", 2 * D),
              ("l0c_q", D), ("l0c_k", D), ("l0c_v", D), ("l0c_o", 2 * D)]),
    ("w_mlp", [("l0_w1", DFF), ("l0_b1", 4), ("l0_w2", 4 * D), ("l0_b2", 1)]),
    ("w_l1", [("l1_gamma", 1), ("l1_beta", 1), ("l1_q", D), ("l1_k", D), ("l1_v", D),
              ("l1_router", 3 * NE), ("l1_router_b", 1),
              ("l1_w1", 3 * NE * RH), ("l1_b1", 6), ("l1_w2", 6 * D), ("l1_b2row", NE * D),
              ("l1_gw1", 3 * D), ("l1_gb1", 1), ("l1_gw2", D), ("l1_gb2", 1), ("l1_ow", D), ("l1_ob", 1)]),
    ("w_l2", [("l2_ssq", 2 * D), ("l2_ssq_b", 2), ("l2_sskv", 2 * D), ("l2_sskv_b", 2),
              ("l2_q", D), ("l2_qb", 1), ("l2_k", D), ("l2_kb", 1), ("l2_v", D), ("l2_vb", 2),
              ("l2_o", 2 * D), ("l2_ob", 1)]),
    ("w_l3", [("l3_aff1", 2 * D), ("l3_aff1_b", 2), ("l3_aff2", 2 * D), ("l3_aff2_b", 2),
              ("l3_ln1g", 1), ("l3_ln1b", 1), ("l3_ln2g", 1), ("l3_ln2b", 1),
              ("l3s_q", D), ("l3s_qb", 1), ("l3s_k", D), ("l3s_kb", 1), ("l3s_v", D), ("l3s_vb", 2),
              ("l3s_o", 2 * D), ("l3s_ob", 1),
              ("l3c_q", D), ("l3c_qb", 1), ("l3c_k", D), ("l3c_kb", 1), ("l3c_v", D), ("l3c_vb", 2),
              ("l3c_o", 2 * D), ("l3c_ob", 1),
              ("l3_w1", DFF), ("l3_b1", 4), ("l3_w2", 4 * D), ("l3_b2", 1)]),
]
PACK_COLS = {p: sum(n for _, n in items) for p, items in PACKS}


class Op:

    def __init__(self, sem):
        self.sem, self.signals, self.value = sem, False, None


class Lane:

    def __init__(self, sem):
        self.sem, self.queue = sem, []

    def do(self, issue, *after):
        op = Op(self.sem)
        self.queue.append((op, issue, [p for p in after if p is not None]))
        for p in after:
            if p is not None:
                p.signals = True
        return op

    def dma(self, issue, sem, *after):
        op = self.do(issue, *after)
        op.sem, op.value = sem, 16
        return op

    def number(self):
        n = 0
        for op, _, _ in self.queue:
            if op.value is None and op.signals:
                n += 1
                op.value = n

    def run(self, engine):
        seen = {}
        for op, issue, after in self.queue:
            need = {}
            for p in after:
                need[id(p.sem)] = max(need.get(id(p.sem), (0, None))[0], p.value), p.sem
            for key, (value, sem) in need.items():
                if seen.get(key, 0) < value:
                    engine.wait_ge(sem, value)
                    seen[key] = value
            ins = issue(engine)
            if op.sem is not self.sem:
                ins.then_inc(op.sem, 16)
            elif op.signals:
                ins.then_inc(op.sem, 1)


class Buf:

    def __init__(self, t):
        self.t, self.busy = t, []


def build(nc, a, out_xT):
    with ExitStack() as ctx:
        def sb(name, shape, dt=F32):
            return ctx.enter_context(nc.sbuf_tensor(name, shape, dt))

        def psum(name, shape):
            return ctx.enter_context(nc.psum_tensor(name, shape, F32))

        def sem(name):
            return ctx.enter_context(nc.semaphore(name))

        pe, dve, act, pool, sp = (Lane(sem(f"done_{n}")) for n in ("pe", "dve", "act", "pool", "sp"))

        xT = sb("xT", [D, B, S])
        ctxT = sb("ctxT", [D, B, SK])
        ctx_tok = [sb(f"ctx_tok{i}", [SK, QUAD, D]) for i in range(2)]
        normT = sb("normT", [D, B, S])
        packs = {p: sb("pack_" + p, [128, n]) for p, n in PACK_COLS.items()}
        W = {}
        for p, items in PACKS:
            at = 0
            for name, n in items:
                W[name] = packs[p][:, at:at + n]
                at += n
        pack_of = {name: p for p, items in PACKS for name, _ in items}

        loaded = {}

        def load(key, dst, src, after=None):
            loaded[key] = sp.dma(lambda e, d=dst, s=src: e.dma_start(d, s), sem("ld_" + key), after)

        load("const", packs["const"][:, :], a["const"])
        load("cond", packs["cond"][:, :], a["cond"])
        mask_qk = sb("mask_qk", [S, S // 4], U32)
        mask_kv = sb("mask_kv", [B, SK], U8)
        load("mask_qk", mask_qk[:, :], a["mask_qk"])
        load("mask_kv", mask_kv[:, :], a["mask_kv"])
        load("w_ada", packs["w_ada"][:, :], a["w_ada"])
        for c in range(B // QUAD):
            load(f"x{c}", xT[:, c * QUAD:(c + 1) * QUAD, :], a["xT"][:, c * QUAD:(c + 1) * QUAD, :])
            if c == 0:
                load("w_l0", packs["w_l0"][:, :], a["w_l0"])
                load("ctx", ctxT[:, :, :], a["ctxT"])
        for p in ("w_mlp", "w_l1", "w_l2", "w_l3"):
            load(p, packs[p][:, :], a[p])

        def L(name):
            return loaded[pack_of[name]]

        ident = W["ident"]

        scores = psum("scores", [128, NG, 512])
        score_busy = [None] * NG
        row_scores = [Buf(psum(f"row_scores{i}", [128, 512])) for i in range(2)]
        work_free = [Buf(psum(f"work{i}", [128, 512])) for i in range(2)]

        def take():
            assert work_free, "no free work bank"
            return work_free.pop(0)

        def give(buf, *last):
            buf.busy = list(last)
            work_free.append(buf)

        class Stream:
            def __init__(self, i):
                self.q = Buf(sb(f"q{i}", [128, S]))
                self.qr = Buf(sb(f"qr{i}", [128, S], F32R))
                self.k = Buf(sb(f"k{i}", [128, S]))
                self.kblk = Buf(sb(f"kblk{i}", [128, NH * S]))
                self.kblk_r = Buf(sb(f"kblk_r{i}", [128, NH * S], F32R))
                self.v = Buf(sb(f"v{i}", [128, NG * NJ * TILE]))
                self.negmax = Buf(sb(f"negmax{i}", [128, NH]))
                self.negm = Buf(sb(f"negm{i}", [128, 128], BF16))
                self.negmT = Buf(sb(f"negmT{i}", [128, S], BF16))
                self.p = [Buf(sb(f"p{i}_{g}", [128, NJ, S])) for g in range(NG)]
                self.stats = Buf(sb(f"stats{i}", [128, 6]))
                self.mv = Buf(sb(f"mv{i}", [128, 2]))
                self.lnv = Buf(sb(f"lnv{i}", [128, 1]))
                self.rstd = Buf(sb(f"rstd{i}", [128, 1]))
                self.xhat = Buf(sb(f"xhat{i}", [128, D]))
                self.xn = Buf(sb(f"xn{i}", [128, S]))
                self.osum = Buf(sb(f"osum{i}", [128, 2, S]))
                self.lden = Buf(sb(f"lden{i}", [128, 2, S]))
                self.rden = Buf(sb(f"rden{i}", [128, 2, S]))
                self.on = Buf(sb(f"on{i}", [128, 2, S]))
                self.rc = Buf(sb(f"rc{i}", [128, 2, S]))
                self.rs = Buf(sb(f"rs{i}", [128, 2, S]))
                self.kvn = Buf(sb(f"kvn{i}", [128, SK]))
                self.ready = [
                    pool.do(lambda e, t=self.negm.t: e.memset(t[:, :], 0.0)),
                    pool.do(lambda e, t=self.v.t: e.memset(t[:, :], 0.0)),
                ]
                v_zero = self.ready[1]
                for g in range(NG):
                    c = (VW * g if g < 3 else 0) + HD
                    self.ready.append(pool.do(lambda e, t=self.v.t, g=g, c=c: e.memset(
                        t[:, g * 128:(g + 1) * 128].rearrange("p (j c) -> p j c", j=NJ)[:, :, c:c + 1], 1.0),
                        v_zero))

        streams = [Stream(0), Stream(1)]
        evT = [streams[b // 16].kblk.t[:, (b % 16) * S:(b % 16 + 1) * S] for b in range(B)]
        x_last = [loaded[f"x{b // QUAD}"] for b in range(B)]

        def conditioned(name, weight, bias, chunks, rhs, rhs_ready):
            m = sb(name, [128, chunks, B])
            bank = take()
            for c in range(chunks):
                mm = pe.do(lambda e, c=c: e.matmul(bank.t[:, c * B:(c + 1) * B], weight[:, c * 128:(c + 1) * 128],
                                                   rhs, start=True, stop=True),
                           L(weight_name[id(weight)]), rhs_ready, *bank.busy)
            done = dve.do(lambda e: e.tensor_tensor(
                m[:, :, :], bank.t[:, 0:chunks * B].rearrange("p (c b) -> p c b", c=chunks),
                bias[:, 0:chunks].unsqueeze(2).to_broadcast([128, chunks, B]), ALU.add), mm)
            give(bank, done)
            return m, done

        weight_name = {id(w): n for n, w in W.items()}

        def affine_scale(name, src, src_done, weight, weight_done):
            t = sb(name, [128, B])
            return t, dve.do(lambda e: e.tensor_scalar(t[:, :], src, 1.0, weight, ALU.add, ALU.mult),
                             src_done, weight_done)

        condT = W["condT"]
        def exp_ln_tables():
            act.do(lambda e: e.preload_act_table_set("natural_log_exp_and_others"))

        exp_ln_tables()
        l0mod, l0mod_done = conditioned("l0mod", W["l0_ada"], W["l0_ada_b"], 9, condT, loaded["cond"])
        l0A = [affine_scale(f"l0A{i}", l0mod[:, 3 * i + 1, :], l0mod_done, W[w], L(w))
               for i, w in enumerate(("l0_norm1", "l0_normc", "l0_norm2"))]
        g_b2 = sb("g_b2", [128, B])

        mq = sb("mq", [S, S])
        live_q = sb("live_q", [S, 1])
        dead_q = sb("dead_q", [S, 1])
        lift_q = sb("lift_q", [S, S])
        neg_qk = sb("neg_qk", [S, S], BF16)
        neg_f = sb("neg_f", [S, S])
        neg_kq = sb("neg_kq", [S, S], BF16)
        ident_bf = sb("ident_bf", [128, 128], BF16)
        ones_bf = sb("ones_bf", [128, 128], BF16)
        cos_live = sb("cos_live", [128, 2, S])
        sin_live = sb("sin_live", [128, 2, S])
        live_rows = sb("live_rows", [S, 128])

        pick_max = sb("pick_max", [128, NH, S], BF16)
        head_mask = sb("head_mask", [128, NH])
        ident_bf_done = dve.do(lambda e: e.tensor_copy(ident_bf[:, :], ident), loaded["const"])
        ones_bf_done = dve.do(lambda e: e.tensor_copy(ones_bf[:, :], W["ones"]), loaded["const"])
        pm_done = dve.do(lambda e: e.tensor_tensor(head_mask[:, :], ident[:, 0:NH], ident[:, NH:2 * NH], ALU.add),
                         loaded["const"])
        pick_max_done = dve.do(lambda e: e.tensor_copy(
            pick_max[:, :, :], head_mask[:, :].unsqueeze(2).to_broadcast([128, NH, S])), pm_done)
        mq_done = dve.do(lambda e: e.tensor_copy(mq[:, :], mask_qk[:, :].bitcast(U8)), loaded["mask_qk"])
        live_done = dve.do(lambda e: e.tensor_reduce(live_q[:, :], mq[:, :], AX_X, ALU.max), mq_done)
        dead_done = dve.do(lambda e: e.tensor_scalar(dead_q[:, :], live_q[:, :], -1.0, 1.0, ALU.mult, ALU.add),
                           live_done)
        lift_done = dve.do(lambda e: e.tensor_scalar(lift_q[:, :], mq[:, :], dead_q[:, 0:1], -1.0,
                                                     ALU.max, ALU.add), dead_done)
        neg_f_done = dve.do(lambda e: e.tensor_scalar(neg_f[:, :], lift_q[:, :], -MASKED, None, ALU.mult), lift_done)
        neg_qk_done = dve.do(lambda e: e.tensor_copy(neg_qk[:, :], neg_f[:, :]), neg_f_done)
        live_rows_done = dve.do(lambda e: e.tensor_scalar(live_rows[:, :], W["ones"], live_q[:, 0:1], None, ALU.mult),
                                live_done)
        bank = take()
        pe.do(lambda e: e.transpose(bank.t[:, 0:S], neg_f[:, :], ident), neg_f_done, *bank.busy)
        mm = pe.do(lambda e: e.matmul(bank.t[:, S:2 * S], live_rows[:, :], ident, start=True, stop=True),
                   live_rows_done)
        neg_kq_done = dve.do(lambda e: e.tensor_copy(neg_kq[:, :], bank.t[:, 0:S]), mm)
        rope_tables = []
        for table, src in ((cos_live, W["rope_cos"]), (sin_live, W["rope_sin"])):
            rope_tables.append(dve.do(lambda e, t=table, s=src: e.tensor_tensor(
                t[:, 0, :], bank.t[:, S:2 * S], s, ALU.mult), mm))
            rope_tables.append(dve.do(lambda e, t=table, s=src: e.tensor_copy(t[:, 1, :], s)))
        give(bank, neg_kq_done, rope_tables[-2])

        mk = sb("mk", [B, SK])
        live_b = sb("live_b", [B, 1])
        dead_b = sb("dead_b", [B, 1])
        lift_b = sb("lift_b", [B, SK])
        neg_bk = sb("neg_bk", [B, SK])
        neg_bk_bf = sb("neg_bk_bf", [B, SK], BF16)
        neg_row = sb("neg_row", [1, B, SK], BF16)
        neg_kb = sb("neg_kb", [SK, B])
        live_diag = sb("live_diag", [B, B])
        live_bc = sb("live_bc", [128, B])
        mk_done = dve.do(lambda e: e.tensor_copy(mk[:, :], mask_kv[:, :]), loaded["mask_kv"])
        live_b_done = dve.do(lambda e: e.tensor_reduce(live_b[:, :], mk[:, :], AX_X, ALU.max), mk_done)
        dead_b_done = dve.do(lambda e: e.tensor_scalar(dead_b[:, :], live_b[:, :], -1.0, 1.0, ALU.mult, ALU.add),
                             live_b_done)
        lift_b_done = dve.do(lambda e: e.tensor_scalar(lift_b[:, :], mk[:, :], dead_b[:, 0:1], -1.0,
                                                       ALU.max, ALU.add), dead_b_done)
        neg_bk_done = dve.do(lambda e: e.tensor_scalar(neg_bk[:, :], lift_b[:, :], -MASKED, None, ALU.mult),
                             lift_b_done)
        neg_bk_bf_done = dve.do(lambda e: e.tensor_copy(neg_bk_bf[:, :], neg_bk[:, :]), neg_bk_done)
        neg_row_done = sp.dma(lambda e: e.dma_start(neg_row[:, :, :], neg_bk_bf[:, :]), sem("ld_neg_row"),
                              neg_bk_bf_done)
        diag_done = dve.do(lambda e: e.tensor_scalar(live_diag[:, :], ident[0:B, 0:B], live_b[:, 0:1], None, ALU.mult),
                           live_b_done)
        bank = take()
        pe.do(lambda e: e.transpose(bank.t[0:SK, 0:B], neg_bk[:, :], ident[0:B, 0:B]), neg_bk_done, *bank.busy)
        mm = pe.do(lambda e: e.matmul(bank.t[:, 128:128 + B], W["ones"][0:B, :], live_diag[:, :], start=True, stop=True),
                   diag_done)
        neg_kb_done = dve.do(lambda e: e.tensor_copy(neg_kb[:, :], bank.t[0:SK, 0:B]), mm)
        live_bc_done = dve.do(lambda e: e.tensor_copy(live_bc[:, :], bank.t[:, 128:128 + B]), mm)
        give(bank, neg_kb_done, live_bc_done)

        def layer_norm(st, src, src_done, n, scale, bias, affine_done, dst, dst_busy, token_major=False):
            if token_major:
                tokens, tokens_done, bank = src, src_done, None
            else:
                bank = take()
                tokens_done = pe.do(lambda e: e.transpose(bank.t[0:n, 0:D], src, ident), src_done, *bank.busy)
                tokens = bank.t[0:n, 0:D]
            stats_done = dve.do(lambda e: e.bn_stats(st.stats.t[0:n, :], tokens), tokens_done)
            mv_done = dve.do(lambda e: e.bn_aggr(st.mv.t[0:n, :], st.stats.t[0:n, :]), stats_done, *st.mv.busy)
            yield
            ln_done = act.do(lambda e: e.activation(st.lnv.t[0:n, :], st.mv.t[0:n, 1:2], ACT.Ln,
                                                    bias=eps_col[0:n, 0:1]), mv_done, eps_done)
            rstd_done = act.do(lambda e: e.activation(st.rstd.t[0:n, :], st.lnv.t[0:n, :], ACT.Exp, scale=-0.5),
                               ln_done, *st.rstd.busy)
            yield
            xhat_done = dve.do(lambda e: e.tensor_scalar(st.xhat.t[0:n, :], tokens, st.mv.t[0:n, 0:1],
                                                         st.rstd.t[0:n, 0:1], ALU.subtract, ALU.mult),
                               rstd_done, *st.xhat.busy)
            st.mv.busy = [ln_done]
            st.rstd.busy = [xhat_done]
            if bank:
                give(bank, xhat_done)
            yield
            back = take()
            turned = pe.do(lambda e: e.transpose(back.t[:, 0:n], st.xhat.t[0:n, :], ident[0:n, 0:n]),
                           xhat_done, *back.busy)
            st.xhat.busy = [turned]
            st.ln_done = act.do(lambda e: e.activation(dst, back.t[:, 0:n], ACT.Identity, bias=bias, scale=scale),
                                turned, affine_done, *dst_busy)
            give(back, st.ln_done)
            yield

        eps_col = sb("eps_col", [128, 1])
        eps_done = pool.do(lambda e: e.memset(eps_col[:, :], EPS))

        def values(st, srcT, src_done, n, weight, weight_done):
            bank = take()
            mm = pe.do(lambda e: e.matmul(bank.t[0:n, 0:D], srcT, weight, start=True, stop=True),
                       weight_done, src_done, *bank.busy)
            step = NJ * TILE + VW
            first = st.v.t[0:n, 0:3 * step].rearrange("p (g c) -> p g c", c=step)[:, :, 0:NJ * TILE].rearrange(
                "p g (j c) -> p g j c", j=NJ)[:, :, :, 0:HD]
            last = st.v.t[0:n, 3 * NJ * TILE:].rearrange("p (j c) -> p j c", j=NJ)[:, :, 0:HD]
            act.do(lambda e: e.copy(first, bank.t[0:n, 0:96].rearrange("p (g j d) -> p g j d", g=3, j=NJ)),
                   mm, *st.v.busy, *st.ready)
            done = act.do(lambda e: e.copy(last, bank.t[0:n, 96:128].rearrange("p (j d) -> p j d", j=NJ)))
            give(bank, done)
            return done

        own_head = W["own_head"]

        def spread_keys(st, nk, k_done):
            keys = st.k.t[:, 0:nk].unsqueeze(1).to_broadcast([128, NH, nk])
            own = own_head[:, :].unsqueeze(2).to_broadcast([128, NH, nk])
            view = lambda t: t[:, 0:NH * nk].rearrange("p (h k) -> p h k", h=NH)
            exact = pool.do(lambda e: e.tensor_tensor(view(st.kblk.t), keys, own, ALU.mult),
                            k_done, loaded["const"], *st.kblk.busy)
            rounded = dve.do(lambda e: e.tensor_tensor(view(st.kblk_r.t), keys, own, ALU.mult),
                             k_done, *st.kblk_r.busy)
            st.k.busy = [exact, rounded]
            return exact, rounded

        def score_steps(st, nk, q_done, k_done, v_done, mask):

            def row_score(g):
                bank = row_scores[g % 2]
                at = bank.t[:, 0:NJ * nk]
                first = True
                if mask and mask[0] == "qk":
                    pe.do(lambda e: e.matmul(at, ident_bf[:, :], neg_qk[:, :].unsqueeze(1).to_broadcast([S, NJ, S]),
                                             start=True, stop=False, skip_group_check=True),
                          neg_qk_done, ident_bf_done, *bank.busy)
                    first = False
                elif mask:
                    pe.do(lambda e: e.matmul(at, ones_bf[0:1, :],
                                             neg_row[0:1, mask[1]:mask[1] + 1, :].to_broadcast([1, NJ, SK]),
                                             start=True, stop=False, skip_group_check=True),
                          neg_row_done, ones_bf_done, *bank.busy)
                    first = False
                mm = pe.do(lambda e, first=first: e.matmul(
                    at, st.qr.t[:, :], st.kblk_r.t[:, g * NJ * nk:(g + 1) * NJ * nk], start=first, stop=True,
                    skip_group_check=True), q_done[1], k_done[1], *bank.busy)
                done = dve.do(lambda e: e.tensor_reduce(
                    st.negmax.t[:, g * NJ:(g + 1) * NJ], at.rearrange("p (j k) -> p j k", j=NJ), AX_X, ALU.max,
                    negate=True), mm, *st.negmax.busy)
                bank.busy = [done]
                return mm, done

            def turned_score(g):
                first = True
                if mask and mask[0] == "qk":
                    pe.do(lambda e: e.matmul(scores[:, g, :], ident_bf[:, :],
                                             neg_kq[:, :].unsqueeze(1).to_broadcast([S, NJ, S]), start=True,
                                             stop=False, skip_group_check=True), score_busy[g], neg_kq_done)
                    first = False
                for j in range(NJ):
                    h = g * NJ + j
                    mm = pe.do(lambda e, j=j, h=h, first=first and j == 0: e.matmul(
                        scores[0:nk, g, j * S:(j + 1) * S], st.kblk.t[:, h * nk:(h + 1) * nk], st.q.t[:, :],
                        start=first, stop=False, skip_group_check=True), q_done[0], k_done[0], score_busy[g])
                return mm

            row_score(0)
            yield
            row_score(1)
            yield
            for g in range(2):
                turned_score(g)
                yield
                mm, max_done = row_score(g + 2)
                yield
            st.qr.busy = st.kblk_r.busy = [mm]
            turned_score(2)
            hi = dve.do(lambda e: e.tensor_copy(st.negm.t[:, 0:NH], st.negmax.t[:, :]), max_done, *st.ready,
                        *st.negm.busy)
            lo = dve.do(lambda e: e.tensor_tensor(st.negm.t[:, NH:2 * NH], st.negmax.t[:, :], st.negm.t[:, 0:NH],
                                                  ALU.subtract), hi)
            st.negmax.busy = [lo]
            yield
            mm = turned_score(3)
            st.q.busy = st.kblk.busy = [mm]
            yield
            bank = row_scores[0]
            mT = bank.t[:, 0:S // 2].bitcast(BF16)
            turned = pe.do(lambda e: e.transpose(mT, st.negm.t[:, :], ident_bf[:, :]), lo, *bank.busy)
            st.negm.busy = [turned]
            mT_done = act.do(lambda e: e.copy(st.negmT.t[:, :], mT), turned, *st.negmT.busy)
            bank.busy = [mT_done]
            yield
            st.exp_done = []
            hide = neg_kb[:, mask[1]:mask[1] + 1] if mask and mask[0] == "kv" else 0.0
            for g in range(NG):
                for j in range(NJ):
                    mm = pe.do(lambda e, g=g, j=j: e.matmul(
                        scores[0:nk, g, j * S:(j + 1) * S], pick_max[:, g * NJ + j, 0:nk], st.negmT.t[:, :],
                        start=False, stop=(j == NJ - 1), skip_group_check=True), mT_done, pick_max_done)
                done = act.do(lambda e, g=g: e.activation(
                    st.p[g].t[0:nk, :, :], scores[0:nk, g, :].rearrange("p (j q) -> p j q", j=NJ), ACT.Exp,
                    bias=hide, scale=HEAD_SCALE), mm, *st.p[g].busy, neg_kb_done)
                score_busy[g] = done
                st.exp_done.append(done)
                yield
            st.negmT.busy = [mm]
            st.v_done = v_done
            st.nk = nk

        def attend(st, b, wo, wo_done, finish):
            nk = st.nk
            obank = take()
            for g in range(NG):
                blk = 1 if g == 3 else 0
                for j in range(NJ):
                    mm = pe.do(lambda e, j=j, g=g, blk=blk: e.matmul(
                        obank.t[TILE * j:TILE * j + TILE, blk * S:(blk + 1) * S],
                        st.v.t[0:nk, (g * NJ + j) * TILE:(g * NJ + j + 1) * TILE], st.p[g].t[0:nk, j, :],
                        start=(g == 0 or g == 3), stop=(g >= 2), skip_group_check=True,
                        tile_position=(0, TILE * j)), st.v_done, st.exp_done[g], *obank.busy)
                st.p[g].busy = [mm]
                yield
            st.v.busy = [mm]
            both = obank.t[:, 0:2 * S].rearrange("p (c s) -> p c s", c=2)
            os_done = act.do(lambda e: e.copy(st.osum.t[:, :, :], both), mm, *st.osum.busy)
            yield
            dbank = take()
            for c in range(2):
                mm = pe.do(lambda e, c=c: e.matmul(dbank.t[:, c * S:(c + 1) * S], W["pick_den"][:, c * 128:(c + 1) * 128],
                                                   st.osum.t[:, c, :], start=True, stop=True), os_done, *dbank.busy)
            st.osum.busy = [mm]
            ld_done = act.do(lambda e: e.activation(st.lden.t[:, :, :], dbank.t[:, 0:2 * S].rearrange(
                "p (c s) -> p c s", c=2), ACT.Ln), mm)
            rd_done = act.do(lambda e: e.activation(st.rden.t[:, :, :], st.lden.t[:, :, :], ACT.Exp, scale=-1.0),
                             ld_done, *st.rden.busy)
            yield
            on_done = dve.do(lambda e: e.tensor_tensor(st.on.t[:, :, :], both, st.rden.t[:, :, :], ALU.mult),
                             rd_done, *st.on.busy)
            st.rden.busy = [on_done]
            give(obank, on_done)
            yield
            for c in range(2):
                mm = pe.do(lambda e, c=c: e.matmul(dbank.t[:, 0:S], wo[:, c * D:(c + 1) * D], st.on.t[:, c, :],
                                                   start=(c == 0), stop=(c == 1)), on_done, wo_done, ld_done)
            st.on.busy = [mm]
            x_last[b] = finish(dbank.t[:, 0:S], mm)
            give(dbank, x_last[b])
            yield

        def gated(b, gate, gate_done):
            return lambda o, mm: dve.do(lambda e: e.scalar_tensor_tensor(
                xT[:, b, :], o, gate, xT[:, b, :], ALU.mult, ALU.add), mm, gate_done)

        def biased(b, bias, bias_done):
            return lambda o, mm: dve.do(lambda e: e.scalar_tensor_tensor(
                xT[:, b, :], o, bias, xT[:, b, :], ALU.add, ALU.add), mm, bias_done)

        def l0_self_head(st, b):
            yield from layer_norm(st, xT[:, b, :], x_last[b], S, l0A[0][0][:, b:b + 1], l0mod[:, 0, b:b + 1],
                                  l0A[0][1], st.xn.t[:, :], st.xn.busy)
            bank = take()
            for i, w in enumerate(("l0_q", "l0_k", "l0_qswap", "l0_kswap")):
                mm = pe.do(lambda e, i=i, w=w: e.matmul(bank.t[:, i * S:(i + 1) * S], W[w], st.xn.t[:, :],
                                                        start=True, stop=True), st.ln_done, L(w), *bank.busy)
            v_done = values(st, st.xn.t[:, :], st.ln_done, S, W["l0_v"], L("l0_v"))
            yield
            half = lambda i: bank.t[:, i * 2 * S:(i + 1) * 2 * S].rearrange("p (c s) -> p c s", c=2)
            rc = dve.do(lambda e: e.tensor_tensor(st.rc.t[:, :, :], half(0), cos_live[:, :, :], ALU.mult),
                        mm, *rope_tables, *st.rc.busy)
            rs = dve.do(lambda e: e.tensor_tensor(st.rs.t[:, :, :], half(1), sin_live[:, :, :], ALU.mult), mm)
            give(bank, rs)
            k_ok = dve.do(lambda e: e.tensor_tensor(st.k.t[:, :], st.rc.t[:, 1, :], st.rs.t[:, 1, :], ALU.add),
                          rc, rs, *st.k.busy)
            rope_done = dve.do(lambda e: e.tensor_tensor(st.q.t[:, :], st.rc.t[:, 0, :], st.rs.t[:, 0, :], ALU.add),
                               *st.q.busy)
            yield
            q_done = (rope_done, act.do(lambda e: e.copy(st.qr.t[:, :], st.q.t[:, :]), rope_done, *st.qr.busy))
            k_done = spread_keys(st, S, k_ok)
            st.xn.busy = [v_done, mm]
            yield
            st.scoring = lambda: score_steps(st, S, q_done, k_done, v_done, ("qk",))
            st.tail = lambda: attend(st, b, W["l0_o"], L("l0_o"), gated(b, l0mod[:, 2, b:b + 1], l0mod_done))

        def cross_head(st, q_src, q_src_done, kv_src, kv_done, nk, names, q_bias, k_bias, live, mask, tail):
            wq, wk, wv = names
            bank = take()
            q_mm = pe.do(lambda e: e.matmul(bank.t[:, 0:S], W[wq], q_src, start=True, stop=True),
                         L(wq), q_src_done, *bank.busy)
            k_mm = pe.do(lambda e: e.matmul(bank.t[:, S:S + nk], W[wk], kv_src, start=True, stop=True), kv_done)
            at = bank.t[:, 0:S]
            if k_bias is None:
                k_ok = dve.do(lambda e: e.tensor_copy(st.k.t[:, 0:nk], bank.t[:, S:S + nk]), k_mm, *st.k.busy)
                q_ok = dve.do(lambda e: e.tensor_scalar(st.q.t[:, :], at, live, None, ALU.mult),
                              live_bc_done, *st.q.busy)
            else:
                k_ok = dve.do(lambda e: e.tensor_scalar(st.k.t[:, 0:nk], bank.t[:, S:S + nk], k_bias, None, ALU.add),
                              k_mm, *st.k.busy)
                q_ok = dve.do(lambda e: e.tensor_scalar(st.q.t[:, :], at, q_bias, None, ALU.add), *st.q.busy)
            give(bank, q_ok)
            q_done = (q_ok, act.do(lambda e: e.copy(st.qr.t[:, :], st.q.t[:, :]), q_ok, *st.qr.busy))
            yield
            k_done = spread_keys(st, nk, k_ok)
            v_done = values(st, kv_src, kv_done, nk, W[wv], L(wv))
            st.src_read = v_done
            yield
            st.scoring = lambda: score_steps(st, nk, q_done, k_done, v_done, mask)
            st.tail = tail

        def l0_cross_head(st, b):
            yield from layer_norm(st, xT[:, b, :], x_last[b], S, l0A[1][0][:, b:b + 1], l0mod[:, 3, b:b + 1],
                                  l0A[1][1], st.xn.t[:, :], st.xn.busy)
            yield from cross_head(st, st.xn.t[:, :], st.ln_done, ctxT[:, b, :], loaded["ctx"], SK,
                                  ("l0c_q", "l0c_k", "l0c_v"), None, None, live_bc[:, b:b + 1], ("kv", b),
                                  lambda: attend(st, b, W["l0c_o"], L("l0c_o"),
                                                 gated(b, l0mod[:, 5, b:b + 1], l0mod_done)))
            st.xn.busy = [st.src_read]

        norm_done = [None] * B

        def l0_mlp_norm(st, b):
            yield from layer_norm(st, xT[:, b, :], x_last[b], S, l0A[2][0][:, b:b + 1], l0mod[:, 6, b:b + 1],
                                  l0A[2][1], normT[:, b, :], [])
            norm_done[b] = st.ln_done

        def chain(st, seqs, heads, after_tail):
            def fill(parts):
                for p in parts:
                    yield from p()
            pending = []
            for b in seqs:
                for h in heads:
                    parts = pending + [lambda h=h, b=b: h(st, b)]
                    yield fill(parts)
                    yield st.scoring()
                    pending = [st.tail]
                pending = pending + [lambda b=b: after_tail(st, b)] if after_tail else pending
            yield fill(pending)
            yield iter(())

        def merge(one, two):
            live = [g for g in (one, two) if g is not None]
            while live:
                for g in list(live):
                    try:
                        next(g)
                    except StopIteration:
                        live.remove(g)

        def both_streams(heads, after_tail=None):
            chains = [chain(streams[i], range(i, B, 2), heads, after_tail) for i in range(2)]
            one, two = chains
            held = next(one)
            merge(held, None)
            while True:
                a_score, b_fill = next(one, None), next(two, None)
                if a_score is None and b_fill is None:
                    break
                merge(a_score, b_fill)
                b_score, a_fill = next(two, None), next(one, None)
                merge(b_score, a_fill)

        both_streams([l0_self_head, l0_cross_head], l0_mlp_norm)

        hid = Buf([hid_at[:, k * QUAD * S:(k + 1) * QUAD * S]
                   for hid_at in (sb("hid", [128, 6 * QUAD * S]),) for k in range(6)])
        sig = streams[0].p[0:2]
        gate_h, gate = streams[0].p[2:4]
        mixT = streams[1].p[0]
        delta = streams[1].p[1:3]
        mix_in = Buf(streams[1].p[3].t[:, :, :].rearrange("p a b -> p (a b)"))
        dense_banks = [Buf(scores[:, j, :]) for j in range(NJ)] + row_scores
        for j in range(NJ):
            dense_banks[j].busy = [score_busy[j]]
        turn = [0]

        def dense():
            turn[0] += 1
            return dense_banks[turn[0] % len(dense_banks)]

        def end_dense():
            for j in range(NJ):
                score_busy[j] = dense_banks[j].busy[-1]

        def mlp(c, w1, b1, w2, act_fn, finish):
            src = normT[:, c * QUAD:(c + 1) * QUAD, :].rearrange("p b s -> p (b s)")
            h = hid
            acts = []
            for f in range(4):
                bank = dense()
                mm = pe.do(lambda e, f=f, bank=bank: e.matmul(bank.t[:, :], W[w1][:, f * 128:(f + 1) * 128], src,
                                                              start=True, stop=True),
                           L(w1), *norm_done[c * QUAD:(c + 1) * QUAD], *bank.busy)
                acts.append(act.do(lambda e, f=f, bank=bank: e.activation(
                    h.t[f], bank.t[:, :], act_fn, bias=W[b1][:, f:f + 1]), mm, *h.busy))
                bank.busy = [acts[-1]]
            bank = dense()
            for f in range(4):
                mm = pe.do(lambda e, f=f: e.matmul(bank.t[:, :], W[w2][:, f * 128:(f + 1) * 128], h.t[f],
                                                   start=(f == 0), stop=(f == 3)), acts[f], L(w2), *bank.busy)
            h.busy = [mm]
            bank.busy = [finish(c, bank, mm)]

        g_b2_done = dve.do(lambda e: e.tensor_scalar(g_b2[:, :], l0mod[:, 8, :], W["l0_b2"][:, 0:1], None, ALU.mult),
                           l0mod_done, L("l0_b2"))

        def l0_mlp_out(c, bank, mm):
            t = delta[c % 2]
            for i in range(QUAD):
                b = c * QUAD + i
                done = act.do(lambda e, i=i, b=b: e.activation(
                    t.t[:, i, :], bank.t[:, i * S:(i + 1) * S], ACT.Identity, bias=g_b2[:, b:b + 1],
                    scale=l0mod[:, 8, b:b + 1]), mm, g_b2_done, *t.busy)
            seqs = slice(c * QUAD, (c + 1) * QUAD)
            added = pool.do(lambda e: e.tensor_tensor(xT[:, seqs, :], xT[:, seqs, :], t.t[:, :, :], ALU.add),
                            done, *x_last[seqs])
            t.busy = [added]
            x_last[seqs] = [added] * QUAD
            return done

        for c in range(B // QUAD):
            mlp(c, "l0_w1", "l0_b1", "l0_w2", ACT.Gelu_apprx_tanh, l0_mlp_out)
        end_dense()
        mlp_read = hid.busy[-1]

        def anchored(name, lhs, lhs_name, bias, chunks, width=128):
            m = sb(name, [128, chunks, B])
            bank = take()
            for c in range(chunks):
                mm = pe.do(lambda e, c=c: e.matmul(bank.t[0:width, c * B:(c + 1) * B],
                                                   lhs[:, c * width:(c + 1) * width], condT, start=True, stop=True),
                           L(lhs_name), *bank.busy)
            done = dve.do(lambda e: e.tensor_tensor(
                m[0:width, :, :], bank.t[0:width, 0:chunks * B].rearrange("p (c b) -> p c b", c=chunks),
                bias[0:width, 0:chunks].unsqueeze(2).to_broadcast([width, chunks, B]), ALU.add), mm)
            give(bank, done)
            return m, done

        h_anchor, h_anchor_done = anchored("h_anchor", W["l1_w1"][:, 2 * NE * RH:3 * NE * RH], "l1_w1", W["l1_b1"], 6)
        g_anchor, g_anchor_done = anchored("g_anchor", W["l1_gw1"][:, 2 * D:3 * D], "l1_gw1", W["l1_gb1"], 1)
        r_anchor, r_anchor_done = anchored("r_anchor", W["l1_router"][:, 2 * NE:3 * NE], "l1_router",
                                           W["l1_router_b"], 1, NE)
        b2_rows = sb("b2_rows", [128, NE * D])
        bank = take()
        mm = pe.do(lambda e: e.matmul(bank.t[:, 0:NE * D], W["ones"][0:1, :], W["l1_b2row"][0:1, :],
                                      start=True, stop=True), L("l1_b2row"), *bank.busy)
        b2_rows_done = dve.do(lambda e: e.tensor_copy(b2_rows[:, :], bank.t[:, 0:NE * D]), mm)
        give(bank, b2_rows_done)

        exp_ln_tables()
        probs = sb("probs", [128, B, NE])
        l1_done = [None] * B

        class L1Buffers:
            def __init__(self, i):
                st = streams[i]
                self.q = Buf(st.osum.t[:, 0, :])
                self.k = Buf(st.osum.t[:, 1, 0:SK])
                self.v = Buf(st.lden.t[0:SK, 0, :])
                self.e = Buf(st.lden.t[:, 1, 0:SK])
                self.pn = Buf(st.rden.t[:, 0, 0:SK])
                self.pT = Buf(st.rden.t[0:SK, 1, :])
                self.lT = Buf(st.on.t[0:NE, 0, :])
                self.m = Buf(sb(f"l1m{i}", [128, 1]))
                self.den = Buf(sb(f"l1den{i}", [128, 1]))
                self.rden = Buf(sb(f"l1rden{i}", [128, 1]))
                self.rm = Buf(sb(f"l1rm{i}", [128, 1]))
                self.re = Buf(sb(f"l1re{i}", [128, NE]))
                self.rsum = Buf(sb(f"l1rsum{i}", [128, 1]))
                self.rr = Buf(sb(f"l1rr{i}", [128, 1]))
                self.qk_read = self.v_read = self.e_read = self.pn_read = self.pT_read = None
                self.lT_read = self.m_read = self.re_read = self.rm_read = None

        def l1_attention(st, t, banks, b):
            def use(k):
                return banks[k]
            nx = normT[:, b, :]
            yield from layer_norm(st, xT[:, b, :], x_last[b], S, W["l1_gamma"], W["l1_beta"], L("l1_gamma"),
                                  nx, [mlp_read])
            nx_done = st.ln_done
            qb, vb = use(0), use(1)
            q_mm = pe.do(lambda e: e.matmul(qb.t[:, 0:S], W["l1_q"], nx, start=True, stop=True), nx_done, *qb.busy)
            k_mm = pe.do(lambda e: e.matmul(qb.t[:, S:S + SK], W["l1_k"], ctxT[:, b, :], start=True, stop=True))
            v_mm = pe.do(lambda e: e.matmul(vb.t[0:SK, 0:D], ctxT[:, b, :], W["l1_v"], start=True, stop=True), *vb.busy)
            q_done = act.do(lambda e: e.activation(t.q.t, qb.t[:, 0:S], ACT.Copy, scale=L1_SCALE),
                            k_mm, t.qk_read)
            k_done = act.do(lambda e: e.copy(t.k.t, qb.t[:, S:S + SK]))
            v_done = dve.do(lambda e: e.tensor_copy(t.v.t, vb.t[0:SK, 0:D]), v_mm, t.v_read)
            yield
            s_mm = pe.do(lambda e: e.matmul(qb.t[:, 256:256 + SK], t.q.t, t.k.t, start=True, stop=True),
                         k_done)
            t.qk_read = s_mm
            m_done = dve.do(lambda e: e.tensor_reduce(t.m.t[:, :], qb.t[:, 256:256 + SK], AX_X, ALU.max, negate=True),
                            s_mm, t.m_read)
            yield
            e_done = act.do(lambda e: e.activation(t.e.t, qb.t[:, 256:256 + SK], ACT.Exp, bias=t.m.t[:, 0:1],
                                                   accum_out=t.den.t[:, :]), m_done, t.e_read)
            t.m_read = e_done
            qb.busy = [e_done]
            yield
            r_done = dve.do(lambda e: e.reciprocal(t.rden.t[:, :], t.den.t[:, :]), e_done)
            pn_done = dve.do(lambda e: e.tensor_scalar(t.pn.t, t.e.t, t.rden.t[:, 0:1], None, ALU.mult),
                             r_done, t.pn_read)
            t.e_read = pn_done
            yield
            t_mm = pe.do(lambda e: e.transpose(vb.t[0:SK, 128:128 + S], t.pn.t, ident), pn_done, v_done)
            t.pn_read = t_mm
            pT_done = act.do(lambda e: e.copy(t.pT.t, vb.t[0:SK, 128:128 + S]), t_mm, t.pT_read)
            yield
            ev_mm = pe.do(lambda e: e.matmul(vb.t[:, 256:256 + S], t.v.t, t.pT.t, start=True, stop=True),
                          pT_done, v_done)
            t.v_read = t.pT_read = ev_mm
            ev_done = dve.do(lambda e: e.tensor_copy(evT[b], vb.t[:, 256:256 + S]), ev_mm)
            yield
            pe.do(lambda e: e.matmul(qb.t[0:NE, 0:S], W["l1_router"][:, 0:NE], nx, start=True, stop=False),
                  *qb.busy)
            l_mm = pe.do(lambda e: e.matmul(qb.t[0:NE, 0:S], W["l1_router"][:, NE:2 * NE], evT[b],
                                            start=False, stop=True), ev_done)
            l_done = act.do(lambda e: e.activation(t.lT.t, qb.t[0:NE, 0:S], ACT.Identity,
                                                   bias=r_anchor[0:NE, 0, b:b + 1]), l_mm, r_anchor_done, t.lT_read)
            yield
            t.lT_read = lt_mm = pe.do(lambda e: e.transpose(qb.t[:, 256:256 + NE], t.lT.t, ident[0:NE, 0:NE]),
                                      l_done)
            rm_done = dve.do(lambda e: e.tensor_reduce(t.rm.t[:, :], qb.t[:, 256:256 + NE], AX_X, ALU.max,
                                                       negate=True), lt_mm, t.rm_read)
            yield
            re_done = act.do(lambda e: e.activation(t.re.t[:, :], qb.t[:, 256:256 + NE], ACT.Exp, bias=t.rm.t[:, 0:1],
                                                    accum_out=t.rsum.t[:, :]), rm_done, t.re_read)
            t.rm_read = re_done
            qb.busy = [re_done]
            vb.busy = [ev_done]
            yield
            rr_done = dve.do(lambda e: e.reciprocal(t.rr.t[:, :], t.rsum.t[:, :]), re_done)
            l1_done[b] = dve.do(lambda e: e.tensor_scalar(probs[:, b, :], t.re.t[:, :], t.rr.t[:, 0:1], None,
                                                          ALU.mult), rr_done)
            t.re_read = l1_done[b]
            yield

        l1_banks = [[Buf(scores[:, 0, :]), Buf(scores[:, 1, :])], [Buf(scores[:, 2, :]), Buf(scores[:, 3, :])]]
        for i in range(2):
            for k in range(2):
                l1_banks[i][k].busy = [score_busy[2 * i + k]]
        l1_buf = [L1Buffers(i) for i in range(2)]

        def l1_chain(i):
            for b in range(i, B, 2):
                yield from l1_attention(streams[i], l1_buf[i], l1_banks[i], b)

        chains = [l1_chain(0), l1_chain(1)]
        for _ in range(6):
            next(chains[0])
        merge(*chains)
        for i in range(2):
            for k in range(2):
                score_busy[2 * i + k] = l1_banks[i][k].busy[-1]
        for j in range(NJ):
            dense_banks[j].busy = [score_busy[j]]

        mix = [Buf(t) for t in (streams[0].rc.t[:, 0, :], streams[0].rc.t[:, 1, :], streams[0].rs.t[:, 0, :])]
        silu_c = sb("silu_c", [128, B])
        sig_c = sb("sig_c", [128, B])
        s1 = act.do(lambda e: e.activation(sig_c[:, :], condT, ACT.Sigmoid))
        silu_c_done = dve.do(lambda e: e.tensor_tensor(silu_c[:, :], condT, sig_c[:, :], ALU.mult), s1)

        def silu_of(bank, mm, anchor, anchor_done, chunk, c, dst, dst_busy, k):
            s = sig[k % 2]
            for i in range(QUAD):
                b = c * QUAD + i
                s_done = act.do(lambda e, i=i, b=b: e.activation(
                    s.t[:, i, :], bank.t[:, i * S:(i + 1) * S], ACT.Sigmoid, bias=anchor[:, chunk, b:b + 1]),
                    mm, anchor_done, *s.busy)
            for i in range(QUAD):
                b = c * QUAD + i
                done = dve.do(lambda e, i=i, b=b: e.scalar_tensor_tensor(
                    dst[:, i * S:(i + 1) * S], bank.t[:, i * S:(i + 1) * S], anchor[:, chunk, b:b + 1],
                    s.t[:, i, :], ALU.add, ALU.mult), s_done, *dst_busy)
            s.busy = [done]
            bank.busy = [done]
            return done

        def l1_experts(c):
            seqs = slice(c * QUAD, (c + 1) * QUAD)
            nx = normT[:, seqs, :].rearrange("p b s -> p (b s)")
            ev = streams[c // 4].kblk.t[:, (c % 4) * QUAD * S:(c % 4 + 1) * QUAD * S]
            h = hid
            h_done = []
            for k in range(2 * NE):
                bank = dense()
                for part, src in ((0, nx), (1, ev)):
                    at = part * NE * RH + k * 128
                    mm = pe.do(lambda e, at=at, src=src, part=part, bank=bank: e.matmul(
                        bank.t[:, :], W["l1_w1"][:, at:at + 128], src, start=(part == 0), stop=(part == 1)),
                        *l1_done[seqs], *bank.busy)
                h_done.append(silu_of(bank, mm, h_anchor, h_anchor_done, k, c, h.t[k], h.busy, k))
            bank = dense()
            for part, src in ((0, nx), (1, ev)):
                mm = pe.do(lambda e, src=src, part=part, bank=bank: e.matmul(
                    bank.t[:, :], W["l1_gw1"][:, part * D:(part + 1) * D], src, start=(part == 0), stop=(part == 1)),
                    *bank.busy)
            gh = gate_h.t[:, :, :].rearrange("p b s -> p (b s)")
            gh_done = silu_of(bank, mm, g_anchor, g_anchor_done, 0, c, gh, gate_h.busy, 6)
            for i in range(QUAD):
                b = c * QUAD + i
                bank = dense()
                for x in range(NE):
                    for r in range(2):
                        k = 2 * x + r
                        mm = pe.do(lambda e, x=x, r=r, k=k, i=i, bank=bank: e.matmul(
                            bank.t[:, x * D:(x + 1) * D], h.t[k][:, i * S:(i + 1) * S],
                            W["l1_w2"][:, k * D:(k + 1) * D], start=(r == 0), stop=(r == 1)),
                            h_done[k], *bank.busy)
                in_done = dve.do(lambda e, bank=bank: e.tensor_tensor(mix_in.t[:, 0:NE * D], bank.t[:, 0:NE * D],
                                                                      b2_rows[:, :], ALU.add), mm)
                bank.busy = [in_done]
                m_done = dve.do(lambda e, b=b: e.tensor_scalar(mix[0].t, mix_in.t[:, 0:D], probs[:, b, 0:1],
                                                               None, ALU.mult), in_done)
                for x in range(1, NE):
                    m_done = dve.do(lambda e, b=b, x=x: e.scalar_tensor_tensor(
                        mix[x].t, mix_in.t[:, x * D:(x + 1) * D], probs[:, b, x:x + 1], mix[x - 1].t,
                        ALU.mult, ALU.add), m_done, *mix[x].busy)
                bank = dense()
                turned = pe.do(lambda e, bank=bank: e.transpose(bank.t[:, 0:S], mix[2].t, ident),
                               m_done, *bank.busy)
                mix[2].busy = [turned]
                mT_done = act.do(lambda e, i=i, bank=bank: e.copy(mixT.t[:, i, :], bank.t[:, 0:S]),
                                 turned, *mixT.busy)
                bank.busy = [mT_done]
            h.busy = [mm]
            bank = dense()
            g_mm = pe.do(lambda e, bank=bank: e.matmul(bank.t[:, :], W["l1_gw2"], gh, start=True, stop=True),
                         gh_done, *bank.busy)
            gate_h.busy = [g_mm]
            g_done = act.do(lambda e, bank=bank: e.activation(
                gate.t[:, :, :].rearrange("p b s -> p (b s)"), bank.t[:, :], ACT.Sigmoid, bias=W["l1_gb2"]),
                g_mm, *gate.busy)
            bank.busy = [g_done]
            bank = dense()
            o_mm = pe.do(lambda e, bank=bank: e.matmul(bank.t[:, :], W["l1_ow"], mixT.t[:, :, :].rearrange(
                "p b s -> p (b s)"), start=True, stop=True), mT_done, *bank.busy)
            mixT.busy = [o_mm]
            t = delta[c % 2]
            d_done = dve.do(lambda e, bank=bank: e.scalar_tensor_tensor(
                t.t[:, :, :].rearrange("p b s -> p (b s)"), bank.t[:, :], W["l1_ob"],
                gate.t[:, :, :].rearrange("p b s -> p (b s)"), ALU.add, ALU.mult), o_mm, g_done, *t.busy)
            gate.busy = [d_done]
            bank.busy = [d_done]
            added = pool.do(lambda e: e.tensor_tensor(xT[:, seqs, :], xT[:, seqs, :], t.t[:, :, :], ALU.add),
                            d_done, *x_last[seqs])
            t.busy = [added]
            x_last[seqs] = [added] * QUAD

        for c in range(B // QUAD):
            l1_experts(c)
        end_dense()
        experts_read = o_mm_last = hid.busy[-1]

        l2q, l2q_done = conditioned("l2q_mod", W["l2_ssq"], W["l2_ssq_b"], 2, silu_c[:, :], silu_c_done)
        l2k, l2k_done = conditioned("l2k_mod", W["l2_sskv"], W["l2_sskv_b"], 2, silu_c[:, :], silu_c_done)
        l2qA, l2qA_done = affine_scale("l2qA", l2q[:, 0, :], l2q_done, W["ones"][:, 0:1], None)
        l2kA, l2kA_done = affine_scale("l2kA", l2k[:, 0, :], l2k_done, W["ones"][:, 0:1], None)
        l3A, l3B, l3A_done = [], [], []
        for i, n in enumerate(("l3_aff1", "l3_aff2")):
            m, done = conditioned(f"l3mod{i}", W[n], W[n + "_b"], 2, condT, None)
            scale, shift = sb(f"l3A{i}", [128, B]), sb(f"l3B{i}", [128, B])
            dve.do(lambda e, m=m, t=scale, i=i: e.tensor_scalar(t[:, :], m[:, 0, :], W[f"l3_ln{i + 1}g"], None,
                                                                ALU.mult), done)
            l3A_done.append(dve.do(lambda e, m=m, t=shift, i=i: e.scalar_tensor_tensor(
                t[:, :], m[:, 0, :], W[f"l3_ln{i + 1}b"], m[:, 1, :], ALU.mult, ALU.add), done))
            l3A.append(scale)
            l3B.append(shift)

        def folded(name):
            bo = sb(name + "_bo", [128, 1])
            bank = take()
            for c in range(2):
                mm = pe.do(lambda e, c=c, bank=bank: e.matmul(
                    bank.t[:, 0:1], W[name + "_o"][:, c * D:(c + 1) * D], W[name + "_vb"][:, c:c + 1],
                    start=(c == 0), stop=(c == 1)), L(name + "_o"), *bank.busy)
            bo_done = dve.do(lambda e, bank=bank: e.tensor_scalar(bo[:, :], bank.t[:, 0:1], W[name + "_ob"], None,
                                                                  ALU.add), mm)
            give(bank, bo_done)
            return bo[:, 0:1], bo_done

        exp_ln_tables()
        l2_bo = folded("l2")
        l3s_bo = folded("l3s")
        l3c_bo = folded("l3c")

        ctx_busy = [None, None]
        ctx_load = {}
        for c in range(B // QUAD):
            ctx_load[c] = None

        def l2_head(st, b):
            c, i = divmod(b, QUAD)
            if ctx_load[c] is None:
                ctx_load[c] = sp.dma(lambda e: e.dma_start(ctx_tok[c % 2][:, :, :],
                                                           a["ctx_tok"][:, c * QUAD:(c + 1) * QUAD, :]),
                                     sem(f"ld_ctx_tok{c}"), *(ctx_reads.get(c - 2) or []))
            yield from layer_norm(st, ctx_tok[c % 2][:, i, :], ctx_load[c], SK, l2kA[:, b:b + 1],
                                  l2k[:, 1, b:b + 1], l2kA_done, st.kvn.t[:, :], st.kvn.busy, token_major=True)
            kv_done = st.ln_done
            ctx_reads.setdefault(c, []).append(kv_done)
            yield from layer_norm(st, xT[:, b, :], x_last[b], S, l2qA[:, b:b + 1], l2q[:, 1, b:b + 1],
                                  l2qA_done, st.xn.t[:, :], st.xn.busy)
            yield from cross_head(st, st.xn.t[:, :], st.ln_done, st.kvn.t[:, :], kv_done, SK,
                                  ("l2_q", "l2_k", "l2_v"), W["l2_qb"], W["l2_kb"], None, None,
                                  lambda: attend(st, b, W["l2_o"], L("l2_o"), biased(b, *l2_bo)))
            st.xn.busy = st.kvn.busy = [st.src_read]

        ctx_reads = {}

        def l3_self_head(st, b):
            yield from layer_norm(st, xT[:, b, :], x_last[b], S, l3A[0][:, b:b + 1], l3B[0][:, b:b + 1],
                                  l3A_done[0], st.xn.t[:, :], st.xn.busy)
            yield from cross_head(st, st.xn.t[:, :], st.ln_done, st.xn.t[:, :], st.ln_done, S,
                                  ("l3s_q", "l3s_k", "l3s_v"), W["l3s_qb"], W["l3s_kb"], None, None,
                                  lambda: attend(st, b, W["l3s_o"], L("l3s_o"), biased(b, *l3s_bo)))
            st.xn.busy = [st.src_read]

        def l3_cross_head(st, b):
            yield from cross_head(st, xT[:, b, :], x_last[b], ctxT[:, b, :], loaded["ctx"], SK,
                                  ("l3c_q", "l3c_k", "l3c_v"), W["l3c_qb"], W["l3c_kb"], None, None,
                                  lambda: attend(st, b, W["l3c_o"], L("l3c_o"), biased(b, *l3c_bo)))

        def l3_ffn_norm(st, b):
            yield from layer_norm(st, xT[:, b, :], x_last[b], S, l3A[1][:, b:b + 1], l3B[1][:, b:b + 1],
                                  l3A_done[1], normT[:, b, :], [experts_read])
            norm_done[b] = st.ln_done

        both_streams([l2_head, l3_self_head, l3_cross_head], l3_ffn_norm)

        for j in range(NJ):
            dense_banks[j].busy = [score_busy[j]]
        stores = []

        def l3_out(c, bank, mm):
            seqs = slice(c * QUAD, (c + 1) * QUAD)
            flat = xT[:, seqs, :].rearrange("p b s -> p (b s)")
            done = dve.do(lambda e: e.scalar_tensor_tensor(flat, bank.t[:, :], W["l3_b2"], flat, ALU.add, ALU.add),
                          mm, *x_last[seqs])
            stores.append(sp.dma(lambda e: e.dma_start(out_xT[:, seqs, :], xT[:, seqs, :]), sem(f"store{c}"), done))
            return done

        for c in range(B // QUAD):
            mlp(c, "l3_w1", "l3_b1", "l3_w2", ACT.Gelu, l3_out)

        lanes = (pe, dve, act, pool, sp)
        for lane in lanes:
            lane.number()
        block = ctx.enter_context(nc.Block())

        @block.tensor
        def _(e):
            pe.run(e)

        @block.vector
        def _(e):
            dve.run(e)

        @block.scalar
        def _(e):
            act.run(e)

        @block.gpsimd
        def _(e):
            pool.run(e)

        @block.sync
        def _(e):
            sp.run(e)
            for s in stores:
                e.wait_ge(s.sem, 16)


def _pad_out(w):
    n = w.shape[1]
    heads = w.reshape(NG, NJ, HD, n)
    out = np.zeros((NJ, TILE, 2, n), w.dtype)
    for g in range(NG):
        at = VW * g if g < 3 else 0
        out[:, at:at + HD, 1 if g == 3 else 0, :] = heads[g]
    return out.reshape(128, 2 * n)


def _constants():
    ident = np.eye(128, dtype=np.float32)
    own_head = np.repeat(np.eye(NH, dtype=np.float32), HD, axis=0)
    n = S // 2
    inv_freq = 1.0 / 10000.0 ** (np.arange(0, HD, 2, dtype=np.float32) / HD)
    freqs = np.outer(np.arange(n, dtype=np.float32), inv_freq)
    emb = np.concatenate([freqs, freqs], axis=-1)
    sign = np.where(np.arange(HD) < HD // 2, -1.0, 1.0)
    cos = np.tile(np.tile(np.cos(emb).astype(np.float32).T, (NH, 1)), (1, 2))
    sin = np.tile(np.tile((np.sin(emb) * sign).astype(np.float32).T, (NH, 1)), (1, 2))
    pick = np.zeros((128, 2, 128), np.float32)
    for j in range(NJ):
        for r in range(TILE):
            g = r // VW if r < 3 * VW else 0
            pick[TILE * j + VW * g + HD, 0, TILE * j + r] = 1.0
            pick[TILE * j + HD, 1, TILE * j + r] = 1.0
    return {"ident": ident, "own_head": own_head, "rope_cos": cos, "rope_sin": sin,
            "pick_den": pick.reshape(128, 256), "ones": np.ones((128, 128), np.float32)}


def _swap(w):
    return w.reshape(w.shape[0], NH, 2, HD // 2)[:, :, ::-1].reshape(w.shape[0], D)


def _col(v):
    return v.reshape(-1, 128).T


def _rows(w):
    return w.reshape(-1, 128, w.shape[1]).transpose(1, 0, 2).reshape(128, -1)


def _head_bias(b):
    return _pad_out(b[:, None]).reshape(128, 2)


def kernel(**inputs):
    import concourse.bacc as bacc
    from concourse.bass_utils import run_bass_kernel_spmd

    i = {k: np.asarray(v) for k, v in inputs.items()}
    z = lambda layer, name: i[f"{layer}_xcond_{name}"]
    p = _constants()
    p["condT"] = i["cond_1024"].T
    p["l0_ada"], p["l0_ada_b"] = z("L0", "adaLN_W"), _col(z("L0", "adaLN_b"))
    for n in ("norm1", "normc", "norm2"):
        p["l0_" + n] = _col(z("L0", n + "_w"))
    wq, wk, wv = (z("L0", "qkv_W")[:, c * D:(c + 1) * D] for c in range(3))
    p["l0_q"], p["l0_qswap"], p["l0_k"], p["l0_kswap"] = wq, _swap(wq), wk, _swap(wk)
    p["l0_v"], p["l0_o"] = (wv), _pad_out(z("L0", "attn_out_W"))
    p["l0c_q"], p["l0c_k"] = (z("L0", "cq_W")), (z("L0", "ck_W"))
    p["l0c_v"], p["l0c_o"] = (z("L0", "cv_W")), _pad_out(z("L0", "co_W"))
    for layer, n, names in (("L0", "l0", ("mlp_W1", "mlp_b1", "mlp_W2", "mlp_b2")),
                            ("L3", "l3", ("ffn_w1", "ffn_b1", "ffn_w2", "ffn_b2"))):
        p[n + "_w1"], p[n + "_b1"] = z(layer, names[0]), _col(z(layer, names[1]))
        p[n + "_w2"], p[n + "_b2"] = _rows(z(layer, names[2])), _col(z(layer, names[3]))
    p["l1_gamma"], p["l1_beta"] = _col(z("L1", "ln_gamma")), _col(z("L1", "ln_beta"))
    p["l1_q"], p["l1_k"], p["l1_v"] = z("L1", "Wq"), z("L1", "Wk"), z("L1", "Wv")
    p["l1_router"] = _rows(z("L1", "router_W"))
    rb = np.zeros((128, 1), np.float32)
    rb[:NE, 0] = z("L1", "router_b")
    p["l1_router_b"] = rb
    w1 = z("L1", "e_w1").transpose(1, 0, 2).reshape(3 * D, NE * RH)
    p["l1_w1"], p["l1_b1"] = _rows(w1), _col(z("L1", "e_b1"))
    p["l1_w2"] = _rows(z("L1", "e_w2").reshape(NE * RH, D))
    b2 = np.zeros((128, NE * D), np.float32)
    b2[0] = z("L1", "e_b2").reshape(-1)
    p["l1_b2row"] = b2
    p["l1_gw1"], p["l1_gb1"] = _rows(z("L1", "gate_w1")), _col(z("L1", "gate_b1"))
    p["l1_gw2"], p["l1_gb2"] = z("L1", "gate_w2"), _col(z("L1", "gate_b2"))
    p["l1_ow"], p["l1_ob"] = z("L1", "out_w"), _col(z("L1", "out_b"))
    p["l2_ssq"], p["l2_ssq_b"] = z("L2", "Wss_q"), _col(z("L2", "bss_q"))
    p["l2_sskv"], p["l2_sskv_b"] = z("L2", "Wss_kv"), _col(z("L2", "bss_kv"))
    kv, bkv = z("L2", "Wkv"), z("L2", "bkv")
    p["l3_aff1"], p["l3_aff1_b"] = z("L3", "aff1_w"), _col(z("L3", "aff1_b"))
    p["l3_aff2"], p["l3_aff2_b"] = z("L3", "aff2_w"), _col(z("L3", "aff2_b"))
    for n in ("ln1", "ln2"):
        p[f"l3_{n}g"], p[f"l3_{n}b"] = _col(z("L3", n + "_g")), _col(z("L3", n + "_b"))
    for n, (q, qb, k, kb, v, vb, o, ob) in {
        "l2": (z("L2", "Wq"), z("L2", "bq"), kv[:, :D], bkv[:D], kv[:, D:], bkv[D:], z("L2", "Wp"), z("L2", "bp")),
        "l3s": [z("L3", "sa_" + s) for s in ("qw", "qb", "kw", "kb", "vw", "vb", "ow", "ob")],
        "l3c": [z("L3", "ca_" + s) for s in ("qw", "qb", "kw", "kb", "vw", "vb", "ow", "ob")],
    }.items():
        p[n + "_q"], p[n + "_qb"] = (q), _col(qb)
        p[n + "_k"], p[n + "_kb"] = (k), _col(kb)
        p[n + "_v"], p[n + "_vb"] = (v), _head_bias(vb)
        p[n + "_o"], p[n + "_ob"] = _pad_out(o), _col(ob)

    arrays = {name: np.ascontiguousarray(np.concatenate([p[n] for n, _ in items], axis=1))
              for name, items in PACKS}
    for name, items in PACKS:
        assert arrays[name].shape == (128, PACK_COLS[name]), name
    arrays["xT"] = np.ascontiguousarray(i["x"].transpose(2, 0, 1))
    arrays["ctxT"] = np.ascontiguousarray(i["ctx_1024"].transpose(2, 0, 1))
    arrays["ctx_tok"] = np.ascontiguousarray(i["ctx_1024"].transpose(1, 0, 2))
    arrays["mask_qk"] = np.ascontiguousarray(i["mask_SxS_bk0"]).view(np.uint32)
    arrays["mask_kv"] = np.ascontiguousarray(i["mask_BxS2_bf1"]).view(np.uint8)

    nc = bacc.Bacc("TRN2", target_bir_lowering=False, num_devices=1)
    aps = {n: nc.dram_tensor("in_" + n, v.shape, mybir.dt.from_np(v.dtype), kind="ExternalInput").ap()
           for n, v in arrays.items()}
    out = nc.dram_tensor("out_xT", (D, B, S), F32, kind="ExternalOutput").ap()
    build(nc, aps, out)
    r = run_bass_kernel_spmd(nc, [{"in_" + n: v for n, v in arrays.items()}], core_ids=[0])
    return np.ascontiguousarray(r.results[0]["out_xT"].transpose(1, 2, 0))
```

```python
from contextlib import ExitStack

import numpy as np

import concourse.bass as bass
from concourse import mybir

F32 = mybir.dt.float32
F32R = mybir.dt.float32r
BF16 = mybir.dt.bfloat16
U8 = mybir.dt.uint8
U32 = mybir.dt.uint32
ALU = mybir.AluOpType
ACT = mybir.ActivationFunctionType
AX_X = mybir.AxisListType.X

B, S, D = 32, 128, 128
NH, HD = 16, 8
NG, NJ, TILE = 4, 4, 32
SK = 77
NE, RH, DFF = 3, 256, 512
EPS = 1e-5
HEAD_SCALE = float(HD) ** -0.5
L1_SCALE = float(D) ** -0.5
VW = HD + 1
MASKED = -(2.0 ** 96)
QUAD = 4

PACKS = [
    ("const", [("ident", 128), ("rope_cos", 128), ("rope_sin", 128), ("own_head", NH),
               ("pick_den", 2 * 128), ("ones", 128)]),
    ("cond", [("condT", B)]),
    ("w_ada", [("l0_ada", 9 * D), ("l0_ada_b", 9), ("l0_norm1", 1), ("l0_normc", 1), ("l0_norm2", 1)]),
    ("w_l0", [("l0_q", D), ("l0_qswap", D), ("l0_k", D), ("l0_kswap", D), ("l0_v", D), ("l0_o", 2 * D),
              ("l0c_q", D), ("l0c_k", D), ("l0c_v", D), ("l0c_o", 2 * D)]),
    ("w_mlp", [("l0_w1", DFF), ("l0_b1", 4), ("l0_w2", 4 * D), ("l0_b2", 1)]),
    ("w_l1", [("l1_gamma", 1), ("l1_beta", 1), ("l1_q", D), ("l1_k", D), ("l1_v", D),
              ("l1_router", 3 * NE), ("l1_router_b", 1),
              ("l1_w1", 3 * NE * RH), ("l1_b1", 6), ("l1_w2", 6 * D), ("l1_b2row", NE * D),
              ("l1_gw1", 3 * D), ("l1_gb1", 1), ("l1_gw2", D), ("l1_gb2", 1), ("l1_ow", D), ("l1_ob", 1)]),
    ("w_l2", [("l2_ssq", 2 * D), ("l2_ssq_b", 2), ("l2_sskv", 2 * D), ("l2_sskv_b", 2),
              ("l2_q", D), ("l2_qb", 1), ("l2_k", D), ("l2_kb", 1), ("l2_v", D), ("l2_vb", 2),
              ("l2_o", 2 * D), ("l2_ob", 1)]),
    ("w_l3", [("l3_aff1", 2 * D), ("l3_aff1_b", 2), ("l3_aff2", 2 * D), ("l3_aff2_b", 2),
              ("l3_ln1g", 1), ("l3_ln1b", 1), ("l3_ln2g", 1), ("l3_ln2b", 1),
              ("l3s_q", D), ("l3s_qb", 1), ("l3s_k", D), ("l3s_kb", 1), ("l3s_v", D), ("l3s_vb", 2),
              ("l3s_o", 2 * D), ("l3s_ob", 1),
              ("l3c_q", D), ("l3c_qb", 1), ("l3c_k", D), ("l3c_kb", 1), ("l3c_v", D), ("l3c_vb", 2),
              ("l3c_o", 2 * D), ("l3c_ob", 1),
              ("l3_w1", DFF), ("l3_b1", 4), ("l3_w2", 4 * D), ("l3_b2", 1)]),
]
PACK_COLS = {p: sum(n for _, n in items) for p, items in PACKS}


HOP = 200


def mm_ns(cols, passes=4):
    return passes * cols / 2.4


def dve_ns(cols):
    return 70 + 1.04 * cols


def act_ns(cols):
    return 52 + 0.83 * cols


def pool_ns(cols):
    return 100 + 2.3 * cols


class Op:

    def __init__(self, sem):
        self.sem, self.signals, self.value = sem, False, None
        self.end = 0.0


class Lane:

    def __init__(self, sem, ns):
        self.sem, self.queue, self.ns, self.free = sem, [], ns, 0.0

    def do(self, issue, *after, ns=None):
        op = Op(self.sem)
        begin = max([self.free] + [p.end + (HOP if p.sem is not self.sem else 0)
                                   for p in after if p is not None])
        op.end = self.free = begin + (ns or self.ns)
        self.queue.append((op, issue, [p for p in after if p is not None]))
        for p in after:
            if p is not None:
                p.signals = True
        return op

    def dma(self, issue, sem, *after):
        op = self.do(issue, *after)
        op.sem, op.value = sem, 16
        return op

    def number(self):
        n = 0
        for op, _, _ in self.queue:
            if op.value is None and op.signals:
                n += 1
                op.value = n

    def run(self, engine):
        seen = {}
        for op, issue, after in self.queue:
            need = {}
            for p in after:
                need[id(p.sem)] = max(need.get(id(p.sem), (0, None))[0], p.value), p.sem
            for key, (value, sem) in need.items():
                if seen.get(key, 0) < value:
                    engine.wait_ge(sem, value)
                    seen[key] = value
            ins = issue(engine)
            if op.sem is not self.sem:
                ins.then_inc(op.sem, 16)
            elif op.signals:
                ins.then_inc(op.sem, 1)


class Buf:

    def __init__(self, t):
        self.t, self.busy = t, []


def build(nc, a, out_xT):
    with ExitStack() as ctx:
        def sb(name, shape, dt=F32):
            return ctx.enter_context(nc.sbuf_tensor(name, shape, dt))

        def psum(name, shape):
            return ctx.enter_context(nc.psum_tensor(name, shape, F32))

        def sem(name):
            return ctx.enter_context(nc.semaphore(name))

        pe, dve, act, pool, sp = (Lane(sem(f"done_{n}"), ns) for n, ns in (
            ("pe", mm_ns(S)), ("dve", dve_ns(S)), ("act", act_ns(S)), ("pool", pool_ns(S)), ("sp", 100)))

        xT = sb("xT", [D, B, S])
        ctxT = sb("ctxT", [D, B, SK])
        ctx_tok = [sb(f"ctx_tok{i}", [SK, QUAD, D]) for i in range(2)]
        normT = sb("normT", [D, B, S])
        packs = {p: sb("pack_" + p, [128, n]) for p, n in PACK_COLS.items()}
        W = {}
        for p, items in PACKS:
            at = 0
            for name, n in items:
                W[name] = packs[p][:, at:at + n]
                at += n
        pack_of = {name: p for p, items in PACKS for name, _ in items}

        loaded = {}

        def load(key, dst, src, after=None):
            loaded[key] = sp.dma(lambda e, d=dst, s=src: e.dma_start(d, s), sem("ld_" + key), after)

        load("const", packs["const"][:, :], a["const"])
        load("cond", packs["cond"][:, :], a["cond"])
        mask_qk = sb("mask_qk", [S, S // 4], U32)
        mask_kv = sb("mask_kv", [B, SK], U8)
        load("mask_qk", mask_qk[:, :], a["mask_qk"])
        load("mask_kv", mask_kv[:, :], a["mask_kv"])
        load("w_ada", packs["w_ada"][:, :], a["w_ada"])
        for c in range(B // QUAD):
            load(f"x{c}", xT[:, c * QUAD:(c + 1) * QUAD, :], a["xT"][:, c * QUAD:(c + 1) * QUAD, :])
            if c == 0:
                load("w_l0", packs["w_l0"][:, :], a["w_l0"])
                load("ctx", ctxT[:, :, :], a["ctxT"])
        for p in ("w_mlp", "w_l1", "w_l2", "w_l3"):
            load(p, packs[p][:, :], a[p])

        def L(name):
            return loaded[pack_of[name]]

        ident = W["ident"]

        scores = psum("scores", [128, NG, 512])
        score_busy = [None] * NG
        row_scores = Buf(psum("row_scores", [128, 512]))
        work_banks = [Buf(psum(f"work{i}", [128, 512])) for i in range(3)]
        work_free = list(work_banks)

        def take():
            assert work_free, "no free work bank"
            return work_free.pop(0)

        def free_bank():
            while not work_free:
                yield lambda: work_free
            return take()

        def give(buf, *last):
            buf.busy = list(last)
            work_free.append(buf)

        class Norm:

            def __init__(self, name, xhat):
                self.xhat = Buf(xhat)
                self.stats = sb(f"stats_{name}", [128, 6])
                self.mv = Buf(sb(f"mv_{name}", [128, 2]))
                self.lnv = sb(f"lnv_{name}", [128, 1])
                self.rstd = Buf(sb(f"rstd_{name}", [128, 1]))
                self.done = None

        class Prep:

            def __init__(self, i):
                self.norm = Norm(f"prep{i}", sb(f"xhat{i}", [128, D]))
                self.xn = Buf(sb(f"xn{i}", [128, S]))
                self.qk = Buf(sb(f"qk{i}", [128, 2, S]))
                self.q, self.k = self.qk.t[:, 0, :], self.qk.t[:, 1, :]
                self.qr = Buf(sb(f"qr{i}", [128, S], F32R))
                self.v = Buf(sb(f"v{i}", [128, NG * NJ * TILE]))
                self.v_free = True
                v_zero = pool.do(lambda e, t=self.v.t: e.memset(t[:, :], 0.0))
                self.ready = []
                for g in range(NG):
                    c = (VW * g if g < 3 else 0) + HD
                    self.ready.append(pool.do(lambda e, t=self.v.t, g=g, c=c: e.memset(
                        t[:, g * 128:(g + 1) * 128].rearrange("p (j c) -> p j c", j=NJ)[:, :, c:c + 1], 1.0),
                        v_zero))

        class Turn:

            def __init__(self, i):
                self.kblk = Buf(sb(f"kblk{i}", [128, NH * S]))
                self.kblk_r = Buf(sb(f"kblk_r{i}", [128, NH * S], F32R))
                self.negmax = Buf(sb(f"negmax{i}", [128, NH]))
                self.negm = Buf(sb(f"negm{i}", [128, 128], BF16))
                self.negm_zero = pool.do(lambda e, t=self.negm.t: e.memset(t[:, :], 0.0))
                self.negmT = Buf(sb(f"negmT{i}", [128, S], BF16))
                self.p = [Buf(sb(f"p{i}_{g}", [128, NJ, S])) for g in range(NG)]
                self.pair = Buf(sb(f"pair{i}", [128, 2, S]))
                self.sums = Buf(sb(f"sums{i}", [128, 2, S]))

        class Job:

            def __init__(self, n):
                self.n = n
                self.prep, self.turn = preps[n % len(preps)], turns[n % len(turns)]
                self.spread_done = []
                self.exp_done = []
                self.turned = self.weighted = 0
                self.rows_queued = self.exps_queued = self.tail_queued = False
                self.negmT_done = None

        preps = [Prep(i) for i in range(4)]
        turns = [Turn(i) for i in range(2)]
        late_norms = [Norm(f"late{i}", sb(f"xhat_late{i}", [128, D])) for i in range(4)]
        rot = Buf(sb("rot", [128, 2, S]))
        evT = [turns[b // 16].kblk.t[:, (b % 16) * S:(b % 16 + 1) * S] for b in range(B)]
        x_last = [loaded[f"x{b // QUAD}"] for b in range(B)]

        def conditioned(name, weight, bias, chunks, rhs, rhs_ready):
            m = sb(name, [128, chunks, B])
            bank = take()
            for c in range(chunks):
                mm = pe.do(lambda e, c=c: e.matmul(bank.t[:, c * B:(c + 1) * B], weight[:, c * 128:(c + 1) * 128],
                                                   rhs, start=True, stop=True),
                           L(weight_name[id(weight)]), rhs_ready, *bank.busy)
            done = dve.do(lambda e: e.tensor_tensor(
                m[:, :, :], bank.t[:, 0:chunks * B].rearrange("p (c b) -> p c b", c=chunks),
                bias[:, 0:chunks].unsqueeze(2).to_broadcast([128, chunks, B]), ALU.add), mm)
            give(bank, done)
            return m, done

        weight_name = {id(w): n for n, w in W.items()}

        def affine_scale(name, src, src_done, weight, weight_done):
            t = sb(name, [128, B])
            return t, dve.do(lambda e: e.tensor_scalar(t[:, :], src, 1.0, weight, ALU.add, ALU.mult),
                             src_done, weight_done)

        condT = W["condT"]
        def exp_ln_tables():
            act.do(lambda e: e.preload_act_table_set("natural_log_exp_and_others"))

        exp_ln_tables()
        l0mod, l0mod_done = conditioned("l0mod", W["l0_ada"], W["l0_ada_b"], 9, condT, loaded["cond"])
        l0A = [affine_scale(f"l0A{i}", l0mod[:, 3 * i + 1, :], l0mod_done, W[w], L(w))
               for i, w in enumerate(("l0_norm1", "l0_normc", "l0_norm2"))]
        g_b2 = sb("g_b2", [128, B])

        scratch = turns[0].p[0].t
        mq, lift_q, neg_f, live_rows = (scratch[:, i, :] for i in range(NJ))
        live_q = sb("live_q", [S, 1])
        dead_q = sb("dead_q", [S, 1])
        neg_qk = sb("neg_qk", [S, S], BF16)
        neg_kq = sb("neg_kq", [S, S], BF16)
        ident_bf = sb("ident_bf", [128, 128], BF16)
        ones_bf = sb("ones_bf", [128, 128], BF16)
        cos_live = sb("cos_live", [128, 2, S])
        sin_live = sb("sin_live", [128, 2, S])

        pick_max = sb("pick_max", [128, NH, S], BF16)
        head_mask = sb("head_mask", [128, NH])
        ident_bf_done = dve.do(lambda e: e.tensor_copy(ident_bf[:, :], ident), loaded["const"])
        ones_bf_done = dve.do(lambda e: e.tensor_copy(ones_bf[:, :], W["ones"]), loaded["const"])
        pm_done = dve.do(lambda e: e.tensor_tensor(head_mask[:, :], ident[:, 0:NH], ident[:, NH:2 * NH], ALU.add),
                         loaded["const"])
        pick_max_done = dve.do(lambda e: e.tensor_copy(
            pick_max[:, :, :], head_mask[:, :].unsqueeze(2).to_broadcast([128, NH, S])), pm_done)
        mq_done = dve.do(lambda e: e.tensor_copy(mq[:, :], mask_qk[:, :].bitcast(U8)), loaded["mask_qk"])
        live_done = dve.do(lambda e: e.tensor_reduce(live_q[:, :], mq[:, :], AX_X, ALU.max), mq_done)
        dead_done = dve.do(lambda e: e.tensor_scalar(dead_q[:, :], live_q[:, :], -1.0, 1.0, ALU.mult, ALU.add),
                           live_done)
        lift_done = dve.do(lambda e: e.tensor_scalar(lift_q[:, :], mq[:, :], dead_q[:, 0:1], -1.0,
                                                     ALU.max, ALU.add), dead_done)
        neg_f_done = dve.do(lambda e: e.tensor_scalar(neg_f[:, :], lift_q[:, :], -MASKED, None, ALU.mult), lift_done)
        neg_qk_done = dve.do(lambda e: e.tensor_copy(neg_qk[:, :], neg_f[:, :]), neg_f_done)
        live_rows_done = dve.do(lambda e: e.tensor_scalar(live_rows[:, :], W["ones"], live_q[:, 0:1], None, ALU.mult),
                                live_done)
        qk_bank = take()
        pe.do(lambda e: e.transpose(qk_bank.t[:, 0:S], neg_f[:, :], ident), neg_f_done, *qk_bank.busy)
        mm = pe.do(lambda e: e.matmul(qk_bank.t[:, S:2 * S], live_rows[:, :], ident, start=True, stop=True),
                   live_rows_done)
        neg_kq_done = dve.do(lambda e: e.tensor_copy(neg_kq[:, :], qk_bank.t[:, 0:S]), mm)
        rope_tables = []
        for table, src in ((cos_live, W["rope_cos"]), (sin_live, W["rope_sin"])):
            rope_tables.append(dve.do(lambda e, t=table, s=src: e.tensor_tensor(
                t[:, 0, :], qk_bank.t[:, S:2 * S], s, ALU.mult), mm))
            rope_tables.append(dve.do(lambda e, t=table, s=src: e.tensor_copy(t[:, 1, :], s)))
        give(qk_bank, neg_kq_done, rope_tables[-2])

        mk = sb("mk", [B, SK])
        live_b = sb("live_b", [B, 1])
        dead_b = sb("dead_b", [B, 1])
        lift_b = sb("lift_b", [B, SK])
        neg_bk = sb("neg_bk", [B, SK])
        neg_bk_bf = sb("neg_bk_bf", [B, SK], BF16)
        neg_row = sb("neg_row", [1, B, SK], BF16)
        neg_kb = sb("neg_kb", [SK, B])
        live_diag = sb("live_diag", [B, B])
        live_bc = sb("live_bc", [128, B])
        mk_done = dve.do(lambda e: e.tensor_copy(mk[:, :], mask_kv[:, :]), loaded["mask_kv"])
        live_b_done = dve.do(lambda e: e.tensor_reduce(live_b[:, :], mk[:, :], AX_X, ALU.max), mk_done)
        dead_b_done = dve.do(lambda e: e.tensor_scalar(dead_b[:, :], live_b[:, :], -1.0, 1.0, ALU.mult, ALU.add),
                             live_b_done)
        lift_b_done = dve.do(lambda e: e.tensor_scalar(lift_b[:, :], mk[:, :], dead_b[:, 0:1], -1.0,
                                                       ALU.max, ALU.add), dead_b_done)
        neg_bk_done = dve.do(lambda e: e.tensor_scalar(neg_bk[:, :], lift_b[:, :], -MASKED, None, ALU.mult),
                             lift_b_done)
        neg_bk_bf_done = dve.do(lambda e: e.tensor_copy(neg_bk_bf[:, :], neg_bk[:, :]), neg_bk_done)
        neg_row_done = sp.dma(lambda e: e.dma_start(neg_row[:, :, :], neg_bk_bf[:, :]), sem("ld_neg_row"),
                              neg_bk_bf_done)
        diag_done = dve.do(lambda e: e.tensor_scalar(live_diag[:, :], ident[0:B, 0:B], live_b[:, 0:1], None, ALU.mult),
                           live_b_done)
        kv_bank = take()
        pe.do(lambda e: e.transpose(kv_bank.t[0:SK, 0:B], neg_bk[:, :], ident[0:B, 0:B]), neg_bk_done, *kv_bank.busy)
        mm = pe.do(lambda e: e.matmul(kv_bank.t[:, 128:128 + B], W["ones"][0:B, :], live_diag[:, :], start=True, stop=True),
                   diag_done)
        neg_kb_done = dve.do(lambda e: e.tensor_copy(neg_kb[:, :], kv_bank.t[0:SK, 0:B]), mm)
        live_bc_done = dve.do(lambda e: e.tensor_copy(live_bc[:, :], kv_bank.t[:, 128:128 + B]), mm)
        give(kv_bank, neg_kb_done, live_bc_done)

        def layer_norm(ln, src, src_done, n, scale, bias, affine_done, dst, dst_busy, token_major=False, own=None):
            yield src_done
            if token_major:
                tokens, tokens_done, bank = src, src_done, None
            else:
                bank = own or (yield from free_bank())
                tokens_done = pe.do(lambda e: e.transpose(bank.t[0:n, 0:D], src, ident), src_done, *bank.busy, ns=100)
                tokens = bank.t[0:n, 0:D]
            stats_done = dve.do(lambda e: e.bn_stats(ln.stats[0:n, :], tokens), tokens_done)
            mv_done = dve.do(lambda e: e.bn_aggr(ln.mv.t[0:n, :], ln.stats[0:n, :]), stats_done, *ln.mv.busy, ns=70)
            yield mv_done
            ln_done = act.do(lambda e: e.activation(ln.lnv[0:n, :], ln.mv.t[0:n, 1:2], ACT.Ln,
                                                    bias=eps_col[0:n, 0:1]), mv_done, eps_done, ns=188)
            rstd_done = act.do(lambda e: e.activation(ln.rstd.t[0:n, :], ln.lnv[0:n, :], ACT.Exp, scale=-0.5),
                               ln_done, *ln.rstd.busy, ns=94)
            yield rstd_done
            xhat_done = dve.do(lambda e: e.tensor_scalar(ln.xhat.t[0:n, :], tokens, ln.mv.t[0:n, 0:1],
                                                         ln.rstd.t[0:n, 0:1], ALU.subtract, ALU.mult),
                               rstd_done, *ln.xhat.busy, ns=319)
            ln.mv.busy = [ln_done]
            ln.rstd.busy = [xhat_done]
            if bank and not own:
                give(bank, xhat_done)
            yield xhat_done
            back = own or (yield from free_bank())
            turned = pe.do(lambda e: e.transpose(back.t[:, 0:n], ln.xhat.t[0:n, :], ident[0:n, 0:n]),
                           xhat_done, *(back.busy if not own else ()), ns=100)
            ln.xhat.busy = [turned]
            ln.done = act.do(lambda e: e.activation(dst, back.t[:, 0:n], ACT.Identity, bias=bias, scale=scale),
                             turned, affine_done, *dst_busy, ns=344)
            if own:
                own.busy = [ln.done]
            else:
                give(back, ln.done)
            yield ln.done

        eps_col = sb("eps_col", [128, 1])
        eps_done = pool.do(lambda e: e.memset(eps_col[:, :], EPS))

        def place_values(prep, bank, at, n, *after):
            prep.v_free = False
            step = NJ * TILE + VW
            first = prep.v.t[0:n, 0:3 * step].rearrange("p (g c) -> p g c", c=step)[:, :, 0:NJ * TILE].rearrange(
                "p g (j c) -> p g j c", j=NJ)[:, :, :, 0:HD]
            last = prep.v.t[0:n, 3 * NJ * TILE:].rearrange("p (j c) -> p j c", j=NJ)[:, :, 0:HD]
            act.do(lambda e: e.copy(first, bank.t[0:n, at:at + 96].rearrange("p (g j d) -> p g j d", g=3, j=NJ)),
                   *after, *prep.v.busy, *prep.ready, ns=act_ns(96))
            return act.do(lambda e: e.copy(last, bank.t[0:n, at + 96:at + 128].rearrange(
                "p (j d) -> p j d", j=NJ)), ns=act_ns(32))

        own_head = W["own_head"]

        def until(condition):
            while not condition():
                yield condition

        jobs = {}
        all_queued = Job(0)
        all_queued.turned = all_queued.weighted = NG
        all_queued.rows_queued = all_queued.exps_queued = all_queued.tail_queued = True
        all_queued.exp_done = [None] * NG

        def before(job, n):
            return jobs.get(job.n - n, all_queued)

        def spread_keys(job, nk, k_done):
            prep, turn = job.prep, job.turn
            for g in range(NG):
                keys = prep.k[:, 0:nk].unsqueeze(1).to_broadcast([128, NJ, nk])
                own = own_head[:, g * NJ:(g + 1) * NJ].unsqueeze(2).to_broadcast([128, NJ, nk])
                view = lambda t, g=g: t[:, g * NJ * nk:(g + 1) * NJ * nk].rearrange("p (h k) -> p h k", h=NJ)
                exact = pool.do(lambda e, keys=keys, own=own, view=view: e.tensor_tensor(
                    view(turn.kblk.t), keys, own, ALU.mult), k_done, loaded["const"], *turn.kblk.busy,
                    ns=pool_ns(NJ * nk))
                rounded = dve.do(lambda e, keys=keys, own=own, view=view: e.tensor_tensor(
                    view(turn.kblk_r.t), keys, own, ALU.mult), k_done, *turn.kblk_r.busy,
                    ns=dve_ns(NJ * nk))
                job.spread_done.append((exact, rounded))
                yield rounded

        def row_maxima(job, nk, q_done, mask):
            prep, turn, bank = job.prep, job.turn, row_scores
            at = bank.t[:, 0:NJ * nk]
            for g in range(NG):
                yield from until(lambda: len(job.spread_done) > g)
                yield job.spread_done[g][1], *bank.busy
                first = True
                if mask and mask[0] == "qk":
                    pe.do(lambda e: e.matmul(at, ident_bf[:, :], neg_qk[:, :].unsqueeze(1).to_broadcast([S, NJ, S]),
                                             start=True, stop=False, skip_group_check=True),
                          neg_qk_done, ident_bf_done, *bank.busy, ns=mm_ns(NJ * S, 1))
                    first = False
                elif mask:
                    pe.do(lambda e: e.matmul(at, ones_bf[0:1, :],
                                             neg_row[0:1, mask[1]:mask[1] + 1, :].to_broadcast([1, NJ, SK]),
                                             start=True, stop=False, skip_group_check=True),
                          neg_row_done, ones_bf_done, *bank.busy, ns=mm_ns(NJ * SK, 1))
                    first = False
                mm = pe.do(lambda e, g=g, first=first: e.matmul(
                    at, prep.qr.t[:, :], turn.kblk_r.t[:, g * NJ * nk:(g + 1) * NJ * nk], start=first, stop=True,
                    skip_group_check=True), q_done, job.spread_done[g][1], *bank.busy, ns=mm_ns(NJ * nk, 1))
                max_done = dve.do(lambda e, g=g: e.tensor_reduce(
                    turn.negmax.t[:, g * NJ:(g + 1) * NJ], at.rearrange("p (j k) -> p j k", j=NJ), AX_X, ALU.max,
                    negate=True), mm, *turn.negmax.busy, ns=dve_ns(NJ * nk))
                bank.busy = [max_done]
            prep.qr.busy = turn.kblk_r.busy = [mm]
            hi = dve.do(lambda e: e.tensor_copy(turn.negm.t[:, 0:NH], turn.negmax.t[:, :]), max_done,
                        turn.negm_zero, *turn.negm.busy, ns=dve_ns(NH))
            lo = dve.do(lambda e: e.tensor_tensor(turn.negm.t[:, NH:2 * NH], turn.negmax.t[:, :],
                                                  turn.negm.t[:, 0:NH], ALU.subtract), hi, ns=dve_ns(NH))
            turn.negmax.busy = [lo]
            yield lo
            mT = bank.t[:, 0:S // 2].bitcast(BF16)
            turned = pe.do(lambda e: e.transpose(mT, turn.negm.t[:, :], ident_bf[:, :]), lo, *bank.busy,
                           ns=mm_ns(S, 1))
            turn.negm.busy = [turned]
            job.negmT_done = act.do(lambda e: e.copy(turn.negmT.t[:, :], mT), turned, *turn.negmT.busy)
            bank.busy = [job.negmT_done]
            job.rows_queued = True

        def turned_scores(job, nk, q_done, mask):
            prep, turn = job.prep, job.turn
            for g in range(NG):
                yield from until(lambda: len(job.spread_done) > g and len(before(job, 1).exp_done) > g)
                for half in range(2):
                    yield job.spread_done[g][0], score_busy[g]
                    first = half == 0
                    if mask and mask[0] == "qk" and first:
                        pe.do(lambda e, g=g: e.matmul(scores[:, g, :], ident_bf[:, :],
                                                      neg_kq[:, :].unsqueeze(1).to_broadcast([S, NJ, S]),
                                                      start=True, stop=False, skip_group_check=True),
                              score_busy[g], neg_kq_done, ns=mm_ns(NJ * S, 1))
                        first = False
                    for j in range(2 * half, 2 * half + 2):
                        mm = pe.do(lambda e, g=g, j=j, first=first and j == 0: e.matmul(
                            scores[0:nk, g, j * S:(j + 1) * S], turn.kblk.t[:, (g * NJ + j) * nk:(g * NJ + j + 1) * nk],
                            prep.q, start=first, stop=False, skip_group_check=True),
                            q_done, job.spread_done[g][0], score_busy[g])
                job.turned = g + 1
            prep.qk.busy = [mm, *job.spread_done[-1]]
            turn.kblk.busy = [mm]

        def exponentiate(job, nk, mask):
            turn = job.turn
            hide = neg_kb[:, mask[1]:mask[1] + 1] if mask and mask[0] == "kv" else 0.0
            for g in range(NG):
                yield job.negmT_done
                for j in range(NJ):
                    mm = pe.do(lambda e, g=g, j=j: e.matmul(
                        scores[0:nk, g, j * S:(j + 1) * S], pick_max[:, g * NJ + j, 0:nk], turn.negmT.t[:, :],
                        start=False, stop=(j == NJ - 1), skip_group_check=True), job.negmT_done, pick_max_done,
                        ns=mm_ns(S, 1))
                done = act.do(lambda e, g=g: e.activation(
                    turn.p[g].t[0:nk, :, :], scores[0:nk, g, :].rearrange("p (j q) -> p j q", j=NJ), ACT.Exp,
                    bias=hide, scale=HEAD_SCALE), mm, *turn.p[g].busy, neg_kb_done, ns=act_ns(NJ * S))
                score_busy[g] = done
                job.exp_done.append(done)
                if g < NG - 1:
                    yield from until(lambda: job.turned > g + 1 and before(job, 2).weighted > g + 1)
            turn.negmT.busy = [mm]
            job.exps_queued = True

        def attend(job, nk, v_done, wo, wo_done, finish, b):
            prep, turn = job.prep, job.turn
            yield from until(lambda: job.exp_done)
            yield job.exp_done[0]
            bank = yield from free_bank()
            for g in range(NG):
                yield from until(lambda: len(job.exp_done) > g)
                yield job.exp_done[g]
                blk = 1 if g == 3 else 0
                for j in range(NJ):
                    mm = pe.do(lambda e, j=j, g=g, blk=blk: e.matmul(
                        bank.t[TILE * j:TILE * j + TILE, blk * S:(blk + 1) * S],
                        prep.v.t[0:nk, (g * NJ + j) * TILE:(g * NJ + j + 1) * TILE], turn.p[g].t[0:nk, j, :],
                        start=(g == 0 or g == 3), stop=(g >= 2), skip_group_check=True,
                        tile_position=(0, TILE * j)), v_done, job.exp_done[g], *bank.busy, ns=mm_ns(S) / 3)
                turn.p[g].busy = prep.v.busy = [mm]
                job.weighted = g + 1
            prep.v_free = True
            yield from until(lambda: before(job, 2).tail_queued)
            yield mm
            pair, sums = turn.pair.t[:, :, :], turn.sums.t[:, :, :]
            both = bank.t[:, 0:2 * S].rearrange("p (c s) -> p c s", c=2)
            os_done = act.do(lambda e: e.copy(pair, both), mm, *turn.pair.busy, ns=act_ns(2 * S))
            yield os_done
            for c in range(2):
                mm = pe.do(lambda e, c=c: e.matmul(bank.t[:, (2 + c) * S:(3 + c) * S],
                                                   W["pick_den"][:, c * 128:(c + 1) * 128],
                                                   turn.pair.t[:, c, :], start=True, stop=True), os_done)
            ld_done = act.do(lambda e: e.activation(sums, bank.t[:, 2 * S:4 * S].rearrange(
                "p (c s) -> p c s", c=2), ACT.Ln), mm, *turn.sums.busy, ns=act_ns(2 * S))
            rd_done = act.do(lambda e: e.activation(sums, sums, ACT.Exp, scale=-1.0), ld_done, ns=act_ns(2 * S))
            yield rd_done
            on_done = dve.do(lambda e: e.tensor_tensor(pair, pair, sums, ALU.mult), rd_done, ns=dve_ns(2 * S))
            turn.sums.busy = [on_done]
            yield on_done
            for c in range(2):
                mm = pe.do(lambda e, c=c: e.matmul(bank.t[:, 0:S], wo[:, c * D:(c + 1) * D], turn.pair.t[:, c, :],
                                                   start=(c == 0), stop=(c == 1)), on_done, wo_done, ld_done)
            turn.pair.busy = [mm]
            x_last[b] = finish(bank.t[:, 0:S], mm)
            give(bank, x_last[b])
            job.tail_queued = True

        def gated(b, gate, gate_done):
            return lambda o, mm: dve.do(lambda e: e.scalar_tensor_tensor(
                xT[:, b, :], o, gate, xT[:, b, :], ALU.mult, ALU.add), mm, gate_done, ns=263)

        def biased(b, bias, bias_done):
            return lambda o, mm: dve.do(lambda e: e.scalar_tensor_tensor(
                xT[:, b, :], o, bias, xT[:, b, :], ALU.add, ALU.add), mm, bias_done, ns=263)

        def l0_self_head(job, b):
            prep, xn = job.prep, job.prep.xn
            yield from layer_norm(prep.norm, xT[:, b, :], x_last[b], S, l0A[0][0][:, b:b + 1],
                                  l0mod[:, 0, b:b + 1], l0A[0][1], xn.t[:, :], xn.busy)
            yield from until(lambda: prep.v_free)
            bank = yield from free_bank()
            for i, w in enumerate(("l0_q", "l0_k", "l0_qswap", "l0_kswap")):
                mm = pe.do(lambda e, i=i, w=w: e.matmul(bank.t[:, i * S:(i + 1) * S], W[w], xn.t[:, :],
                                                        start=True, stop=True), prep.norm.done, L(w), *bank.busy)
            half = lambda i: bank.t[:, i * 2 * S:(i + 1) * 2 * S].rearrange("p (c s) -> p c s", c=2)
            qk = prep.qk.t[:, :, :]
            cos_part = dve.do(lambda e: e.tensor_tensor(qk, half(0), cos_live[:, :, :], ALU.mult),
                              mm, *rope_tables, *prep.qk.busy, ns=dve_ns(2 * S))
            sin_part = dve.do(lambda e: e.tensor_tensor(rot.t[:, :, :], half(1), sin_live[:, :, :], ALU.mult),
                              mm, *rot.busy, ns=dve_ns(2 * S))
            qk_done = dve.do(lambda e: e.tensor_tensor(qk, qk, rot.t[:, :, :], ALU.add), cos_part, sin_part,
                             ns=dve_ns(2 * S))
            rot.busy = [qk_done]
            q_done = (qk_done, act.do(lambda e: e.copy(prep.qr.t[:, :], prep.q), qk_done, *prep.qr.busy))
            yield sin_part
            v_mm = pe.do(lambda e: e.matmul(bank.t[:, 0:D], xn.t[:, :], W["l0_v"], start=True, stop=True), sin_part)
            v_done = place_values(prep, bank, 0, S, v_mm)
            give(bank, v_done)
            xn.busy = [v_mm]
            yield qk_done
            job.spread = lambda: spread_keys(job, S, qk_done)
            job.rows = lambda: row_maxima(job, S, q_done[1], ("qk",))
            job.turning = lambda: turned_scores(job, S, q_done[0], ("qk",))
            job.exponentials = lambda: exponentiate(job, S, ("qk",))
            job.tail = lambda: attend(job, S, v_done, W["l0_o"], L("l0_o"),
                                      gated(b, l0mod[:, 2, b:b + 1], l0mod_done), b)

        def cross_head(job, q_src, q_src_done, kv_src, kv_done, nk, names, q_bias, k_bias, live, mask, finish, b):
            prep = job.prep
            wq, wk, wv, wo = names
            yield from until(lambda: prep.v_free)
            yield q_src_done, kv_done
            bank = yield from free_bank()
            q_at, k_at = bank.t[:, 0:S], bank.t[:, S:S + nk]
            pe.do(lambda e: e.matmul(k_at, W[wk], kv_src, start=True, stop=True), L(wq), kv_done, *bank.busy,
                  ns=mm_ns(nk))
            pe.do(lambda e: e.matmul(q_at, W[wq], q_src, start=True, stop=True), q_src_done)
            v_mm = pe.do(lambda e: e.matmul(bank.t[0:nk, 2 * S:3 * S], kv_src, W[wv], start=True, stop=True))
            keys = prep.k[:, 0:nk]
            if k_bias is None:
                q_ok = dve.do(lambda e: e.tensor_scalar(prep.q, q_at, live, None, ALU.mult),
                              v_mm, live_bc_done, *prep.qk.busy)
                k_ok = dve.do(lambda e: e.tensor_copy(keys, k_at))
            else:
                q_ok = dve.do(lambda e: e.tensor_scalar(prep.q, q_at, q_bias, None, ALU.add), v_mm, *prep.qk.busy)
                k_ok = dve.do(lambda e: e.tensor_scalar(keys, k_at, k_bias, None, ALU.add))
            v_done = place_values(prep, bank, 2 * S, nk, k_ok)
            give(bank, v_done)
            q_done = (q_ok, act.do(lambda e: e.copy(prep.qr.t[:, :], prep.q), q_ok, *prep.qr.busy))
            prep.xn.busy = [v_mm]
            yield k_ok
            job.spread = lambda: spread_keys(job, nk, k_ok)
            job.rows = lambda: row_maxima(job, nk, q_done[1], mask)
            job.turning = lambda: turned_scores(job, nk, q_done[0], mask)
            job.exponentials = lambda: exponentiate(job, nk, mask)
            job.tail = lambda: attend(job, nk, v_done, W[wo], L(wo), finish, b)

        def l0_cross_head(job, b):
            norm, xn = job.prep.norm, job.prep.xn
            yield from layer_norm(norm, xT[:, b, :], x_last[b], S, l0A[1][0][:, b:b + 1],
                                  l0mod[:, 3, b:b + 1], l0A[1][1], xn.t[:, :], xn.busy)
            yield from cross_head(job, xn.t[:, :], norm.done, ctxT[:, b, :], loaded["ctx"], SK,
                                  ("l0c_q", "l0c_k", "l0c_v", "l0c_o"), None, None, live_bc[:, b:b + 1], ("kv", b),
                                  gated(b, l0mod[:, 5, b:b + 1], l0mod_done), b)

        norm_done = [None] * B

        def l0_mlp_norm(norm, b):
            yield from layer_norm(norm, xT[:, b, :], x_last[b], S, l0A[2][0][:, b:b + 1],
                                  l0mod[:, 6, b:b + 1], l0A[2][1], normT[:, b, :], [])
            norm_done[b] = norm.done

        WAYS = 8
        SHIFTS = [w // (WAYS // 2) for w in range(WAYS)]

        class Task:
            def __init__(self, gen, rank=0):
                self.gen, self.rank, self.ended, self.waits = gen, rank, False, None
                self.step()

            def step(self):
                try:
                    self.waits = next(self.gen)
                except StopIteration:
                    self.ended = True

            def begin(self):
                if callable(self.waits):
                    return 0.0 if self.waits() else None
                ops = self.waits if isinstance(self.waits, tuple) else (self.waits,)
                return max([op.end + HOP for op in ops if op is not None], default=0.0)

        def interleave(more):
            tasks = []
            while True:
                more(tasks)
                tasks[:] = [t for t in tasks if not t.ended]
                if not tasks:
                    return
                ready = [(max(t.begin(), pe.free), t.rank, i) for i, t in enumerate(tasks)
                         if t.begin() is not None]
                assert ready, "every task waits for another"
                tasks[min(ready)[2]].step()

        def attentions(heads, after):
            total = len(heads) * B
            jobs.clear()

            order = [((step - SHIFTS[w]) // len(heads) * WAYS + w, (step - SHIFTS[w]) % len(heads))
                     for step in range(total // WAYS + max(SHIFTS)) for w in range(WAYS)
                     if 0 <= step - SHIFTS[w] < total // WAYS]
            number = {at: n for n, at in enumerate(order)}

            late_queued = set()

            def prepare(job):
                b, h = order[job.n]
                yield from until(lambda: h == 0 or jobs[number[b, h - 1]].tail_queued)
                yield from until(lambda: before(job, len(preps)).turned == NG)
                yield from heads[h](job, b)
                yield from until(lambda: before(job, 2).turned == NG and before(job, 2).rows_queued)
                yield from job.spread()

            def rows(job):
                yield from until(lambda: job.spread_done and before(job, 1).rows_queued
                                 and before(job, 2).exps_queued)
                yield from job.rows()

            def turning(job):
                yield from until(lambda: job.spread_done and before(job, 1).turned == NG)
                yield from job.turning()

            def exps(job):
                yield from until(lambda: job.negmT_done and job.turned and before(job, 2).weighted == NG)
                yield from job.exponentials()

            def tail(job):
                b, h = order[job.n]
                yield from until(lambda: job.exp_done)
                yield from job.tail()
                if h == len(heads) - 1:
                    yield from until(lambda: b < len(late_norms) or b - len(late_norms) in late_queued)
                    yield from after(late_norms[b % len(late_norms)], b)
                    late_queued.add(b)

            def more(tasks):
                n = len(jobs)
                if n < total and (n < 6 or jobs[n - 6].exps_queued):
                    jobs[n] = Job(n)
                    tasks.extend(Task(stage(jobs[n]), rank) for rank, stage in enumerate(
                        (tail, rows, prepare, exps, turning)))

            interleave(more)

        attentions([l0_self_head, l0_cross_head], l0_mlp_norm)

        hid_all = sb("hid", [128, 6, QUAD * S])
        hid = Buf([hid_all[:, k, :] for k in range(6)])
        delta = turns[1].p[1:3]
        dense_banks = [Buf(scores[:, j, :]) for j in range(NJ)] + [row_scores] + work_banks
        for j in range(NJ):
            dense_banks[j].busy = [score_busy[j]]
        turn = [0]

        def dense():
            turn[0] += 1
            return dense_banks[turn[0] % len(dense_banks)]

        def end_dense():
            for j in range(NJ):
                score_busy[j] = dense_banks[j].busy[-1]

        def mlp(c, w1, b1, w2, act_fn, finish):
            src = normT[:, c * QUAD:(c + 1) * QUAD, :].rearrange("p b s -> p (b s)")
            h = hid
            acts = []
            for f in range(4):
                bank = dense()
                mm = pe.do(lambda e, f=f, bank=bank: e.matmul(bank.t[:, :], W[w1][:, f * 128:(f + 1) * 128], src,
                                                              start=True, stop=True),
                           L(w1), *norm_done[c * QUAD:(c + 1) * QUAD], *bank.busy)
                acts.append(act.do(lambda e, f=f, bank=bank: e.activation(
                    h.t[f], bank.t[:, :], act_fn, bias=W[b1][:, f:f + 1]), mm, *h.busy))
                bank.busy = [acts[-1]]
            bank = dense()
            for f in range(4):
                mm = pe.do(lambda e, f=f: e.matmul(bank.t[:, :], W[w2][:, f * 128:(f + 1) * 128], h.t[f],
                                                   start=(f == 0), stop=(f == 3)), acts[f], L(w2), *bank.busy)
            h.busy = [mm]
            bank.busy = [finish(c, bank, mm)]

        g_b2_done = dve.do(lambda e: e.tensor_scalar(g_b2[:, :], l0mod[:, 8, :], W["l0_b2"][:, 0:1], None, ALU.mult),
                           l0mod_done, L("l0_b2"))

        def l0_mlp_out(c, bank, mm):
            t = delta[c % 2]
            for i in range(QUAD):
                b = c * QUAD + i
                done = act.do(lambda e, i=i, b=b: e.activation(
                    t.t[:, i, :], bank.t[:, i * S:(i + 1) * S], ACT.Identity, bias=g_b2[:, b:b + 1],
                    scale=l0mod[:, 8, b:b + 1]), mm, g_b2_done, *t.busy)
            seqs = slice(c * QUAD, (c + 1) * QUAD)
            added = pool.do(lambda e: e.tensor_tensor(xT[:, seqs, :], xT[:, seqs, :], t.t[:, :, :], ALU.add),
                            done, *x_last[seqs])
            t.busy = [added]
            x_last[seqs] = [added] * QUAD
            return done

        for c in range(B // QUAD):
            mlp(c, "l0_w1", "l0_b1", "l0_w2", ACT.Gelu_apprx_tanh, l0_mlp_out)
        end_dense()
        mlp_read = hid.busy[-1]

        def anchored(name, lhs, lhs_name, bias, chunks, width=128):
            m = sb(name, [128, chunks, B])
            bank = take()
            for c in range(chunks):
                mm = pe.do(lambda e, c=c: e.matmul(bank.t[0:width, c * B:(c + 1) * B],
                                                   lhs[:, c * width:(c + 1) * width], condT, start=True, stop=True),
                           L(lhs_name), *bank.busy)
            done = dve.do(lambda e: e.tensor_tensor(
                m[0:width, :, :], bank.t[0:width, 0:chunks * B].rearrange("p (c b) -> p c b", c=chunks),
                bias[0:width, 0:chunks].unsqueeze(2).to_broadcast([width, chunks, B]), ALU.add), mm)
            give(bank, done)
            return m, done

        h_anchor, h_anchor_done = anchored("h_anchor", W["l1_w1"][:, 2 * NE * RH:3 * NE * RH], "l1_w1", W["l1_b1"], 6)
        g_anchor, g_anchor_done = anchored("g_anchor", W["l1_gw1"][:, 2 * D:3 * D], "l1_gw1", W["l1_gb1"], 1)
        r_anchor, r_anchor_done = anchored("r_anchor", W["l1_router"][:, 2 * NE:3 * NE], "l1_router",
                                           W["l1_router_b"], 1, NE)
        b2_rows = sb("b2_rows", [128, NE * D])
        b2_bank = take()
        mm = pe.do(lambda e: e.matmul(b2_bank.t[:, 0:NE * D], W["ones"][0:1, :], W["l1_b2row"][0:1, :],
                                      start=True, stop=True), L("l1_b2row"), *b2_bank.busy)
        b2_rows_done = dve.do(lambda e: e.tensor_copy(b2_rows[:, :], b2_bank.t[:, 0:NE * D]), mm)
        give(b2_bank, b2_rows_done)

        exp_ln_tables()
        probs = sb("probs", [128, B, NE])
        l1_done = [None] * B

        class L1Buffers:
            def __init__(self, i):
                p = turns[i // NG].p[i % NG].t
                self.norm = Norm(f"l1_{i}", p[:, 0, :])
                self.norm.xhat.busy = [x_last[B - 1]]
                self.v = Buf(p[0:SK, 0, :])
                self.q = Buf(p[:, 1, :])
                self.pT = Buf(p[0:SK, 1, :])
                self.k = Buf(p[:, 2, 0:SK])
                self.lT = Buf(p[0:NE, 2, :])
                self.e = self.pn = Buf(p[:, 3, 0:SK])
                self.m = Buf(sb(f"l1m{i}", [128, 1]))
                self.den = Buf(sb(f"l1den{i}", [128, 1]))
                self.rden = Buf(sb(f"l1rden{i}", [128, 1]))
                self.rm = Buf(sb(f"l1rm{i}", [128, 1]))
                self.re = Buf(sb(f"l1re{i}", [128, NE]))
                self.rsum = Buf(sb(f"l1rsum{i}", [128, 1]))
                self.rr = Buf(sb(f"l1rr{i}", [128, 1]))
                self.qk_read = self.v_read = self.e_read = self.pn_read = self.pT_read = None
                self.lT_read = self.m_read = self.re_read = self.rm_read = None

        def l1_attention(t, bank, b):
            nx = normT[:, b, :]
            yield from layer_norm(t.norm, xT[:, b, :], x_last[b], S, W["l1_gamma"], W["l1_beta"], L("l1_gamma"),
                                  nx, [mlp_read], own=bank)
            nx_done = t.norm.done
            ps = bank.t
            q_at, k_at, v_at, s_at = ps[:, 0:S], ps[:, S:S + SK], ps[0:SK, 2 * S:3 * S], ps[:, 3 * S:3 * S + SK]
            k_mm = pe.do(lambda e: e.matmul(k_at, W["l1_k"], ctxT[:, b, :], start=True, stop=True), *bank.busy)
            v_mm = pe.do(lambda e: e.matmul(v_at, ctxT[:, b, :], W["l1_v"], start=True, stop=True))
            q_mm = pe.do(lambda e: e.matmul(q_at, W["l1_q"], nx, start=True, stop=True), nx_done)
            dve.do(lambda e: e.tensor_scalar(t.q.t, q_at, L1_SCALE, None, ALU.mult), q_mm, t.qk_read)
            dve.do(lambda e: e.tensor_copy(t.k.t, k_at))
            v_done = dve.do(lambda e: e.tensor_copy(t.v.t, v_at), t.v_read)
            yield v_done
            s_mm = pe.do(lambda e: e.matmul(s_at, t.q.t, t.k.t, start=True, stop=True), v_done)
            t.qk_read = s_mm
            m_done = dve.do(lambda e: e.tensor_reduce(t.m.t[:, :], s_at, AX_X, ALU.max, negate=True),
                            s_mm, t.m_read)
            yield m_done
            e_done = act.do(lambda e: e.activation(t.e.t, s_at, ACT.Exp, bias=t.m.t[:, 0:1],
                                                   accum_out=t.den.t[:, :]), m_done, t.e_read)
            t.m_read = e_done
            yield e_done
            r_done = dve.do(lambda e: e.reciprocal(t.rden.t[:, :], t.den.t[:, :]), e_done)
            pn_done = dve.do(lambda e: e.tensor_scalar(t.pn.t, t.e.t, t.rden.t[:, 0:1], None, ALU.mult),
                             r_done, t.pn_read)
            t.e_read = pn_done
            yield pn_done
            t_mm = pe.do(lambda e: e.transpose(ps[0:SK, 0:S], t.pn.t, ident), pn_done)
            t.pn_read = t_mm
            pT_done = act.do(lambda e: e.copy(t.pT.t, ps[0:SK, 0:S]), t_mm, t.pT_read)
            yield pT_done
            ev_mm = pe.do(lambda e: e.matmul(ps[:, S:2 * S], t.v.t, t.pT.t, start=True, stop=True), pT_done)
            t.v_read = t.pT_read = ev_mm
            ev_done = dve.do(lambda e: e.tensor_copy(evT[b], ps[:, S:2 * S]), ev_mm)
            yield ev_done
            pe.do(lambda e: e.matmul(ps[0:NE, 0:S], W["l1_router"][:, 0:NE], nx, start=True, stop=False), ev_done)
            l_mm = pe.do(lambda e: e.matmul(ps[0:NE, 0:S], W["l1_router"][:, NE:2 * NE], evT[b],
                                            start=False, stop=True))
            l_done = act.do(lambda e: e.activation(t.lT.t, ps[0:NE, 0:S], ACT.Identity,
                                                   bias=r_anchor[0:NE, 0, b:b + 1]), l_mm, r_anchor_done, t.lT_read)
            yield l_done
            t.lT_read = lt_mm = pe.do(lambda e: e.transpose(ps[:, 2 * S:2 * S + NE], t.lT.t, ident[0:NE, 0:NE]),
                                      l_done)
            rm_done = dve.do(lambda e: e.tensor_reduce(t.rm.t[:, :], ps[:, 2 * S:2 * S + NE], AX_X, ALU.max,
                                                       negate=True), lt_mm, t.rm_read)
            yield rm_done
            re_done = act.do(lambda e: e.activation(t.re.t[:, :], ps[:, 2 * S:2 * S + NE], ACT.Exp,
                                                    bias=t.rm.t[:, 0:1], accum_out=t.rsum.t[:, :]), rm_done, t.re_read)
            t.rm_read = re_done
            bank.busy = [re_done]
            yield re_done
            rr_done = dve.do(lambda e: e.reciprocal(t.rr.t[:, :], t.rsum.t[:, :]), re_done)
            l1_done[b] = dve.do(lambda e: e.tensor_scalar(probs[:, b, :], t.re.t[:, :], t.rr.t[:, 0:1], None,
                                                          ALU.mult), rr_done)
            t.re_read = l1_done[b]
            yield l1_done[b]

        l1_buf = [L1Buffers(i) for i in range(WAYS)]

        def l1_chain(i):
            for b in range(i, B, WAYS):
                yield from l1_attention(l1_buf[i], dense_banks[i], b)

        l1_chains = [lambda i=i: Task(l1_chain(i)) for i in range(WAYS)]
        interleave(lambda tasks: tasks.extend(l1_chains.pop()() for _ in list(l1_chains)))

        silu_c = sb("silu_c", [128, B])
        sig_c = sb("sig_c", [128, B])
        s1 = act.do(lambda e: e.activation(sig_c[:, :], condT, ACT.Sigmoid))
        silu_c_done = dve.do(lambda e: e.tensor_tensor(silu_c[:, :], condT, sig_c[:, :], ALU.mult), s1)

        PAIR = 2

        class Experts:

            def __init__(self, i):
                half = lambda buf: Buf(buf.t[:, PAIR * i:PAIR * (i + 1), :])
                flat = lambda buf: buf.t[:, :, :].rearrange("p a b -> p (a b)")
                self.sig = [half(turns[0].p[k]) for k in range(2)]
                self.gate_h, self.gate = half(turns[0].p[2]), half(turns[0].p[3])
                self.mixT, self.delta = half(turns[1].p[0]), half(turns[1].p[1])
                self.mix_in = Buf(flat(turns[1].p[2 + i])[:, 0:NE * D])
                self.mix = [Buf(p.xn.t[:, :] if i else p.norm.xhat.t[:, :]) for p in preps[0:NE]]
                self.h = [Buf(hid_all[:, k, i * PAIR * S:(i + 1) * PAIR * S]) for k in range(2 * NE)]

        shared = take()
        free_banks = dense_banks[0:NJ + 1] + [shared]

        def any_bank():
            while not free_banks:
                yield lambda: free_banks
            return free_banks.pop(0)

        def release(bank, *last):
            bank.busy = list(last)
            free_banks.append(bank)

        def silu(x, bank, mm, anchor, anchor_done, chunk, c, dst, k):
            sig = x.sig[k % 2]
            for i in range(PAIR):
                b = c * PAIR + i
                s_done = act.do(lambda e, i=i, b=b: e.activation(
                    sig.t[:, i, :], bank.t[:, i * S:(i + 1) * S], ACT.Sigmoid, bias=anchor[:, chunk, b:b + 1]),
                    mm, anchor_done, *sig.busy)
            yield s_done
            for i in range(PAIR):
                b = c * PAIR + i
                done = dve.do(lambda e, i=i, b=b: e.scalar_tensor_tensor(
                    dst.t[:, i * S:(i + 1) * S], bank.t[:, i * S:(i + 1) * S], anchor[:, chunk, b:b + 1],
                    sig.t[:, i, :], ALU.add, ALU.mult), s_done, *dst.busy)
            sig.busy = [done]
            release(bank, done)
            return done

        def l1_experts(x, c):
            seqs = slice(c * PAIR, (c + 1) * PAIR)
            cols = PAIR * S
            nx = normT[:, seqs, :].rearrange("p b s -> p (b s)")
            ev = turns[c // 8].kblk.t[:, (c % 8) * cols:(c % 8 + 1) * cols]
            gate_h = Buf(x.gate_h.t.rearrange("p b s -> p (b s)"))
            gate_h.busy = x.gate_h.busy
            h_done = []
            for k in range(2 * NE + 1):
                bank = yield from any_bank()
                for part, src in ((0, nx), (1, ev)):
                    if k:
                        at = part * NE * RH + (k - 1) * 128
                        w = W["l1_w1"][:, at:at + 128]
                    else:
                        w = W["l1_gw1"][:, part * D:(part + 1) * D]
                    mm = pe.do(lambda e, w=w, src=src, part=part, bank=bank: e.matmul(
                        bank.t[:, 0:cols], w, src, start=(part == 0), stop=(part == 1)),
                        *l1_done[seqs], *l1_done[B - WAYS:], *bank.busy, ns=mm_ns(cols))
                yield mm
                if k:
                    h_done.append((yield from silu(x, bank, mm, h_anchor, h_anchor_done, k - 1, c, x.h[k - 1], k)))
                else:
                    gh_done = yield from silu(x, bank, mm, g_anchor, g_anchor_done, 0, c, gate_h, k)
                yield None
            for i in range(PAIR):
                b = c * PAIR + i
                yield h_done[-1]
                bank = yield from any_bank()
                for n in range(NE):
                    for r in range(2):
                        k = 2 * n + r
                        mm = pe.do(lambda e, n=n, r=r, k=k, i=i, bank=bank: e.matmul(
                            bank.t[:, n * D:(n + 1) * D], x.h[k].t[:, i * S:(i + 1) * S],
                            W["l1_w2"][:, k * D:(k + 1) * D], start=(r == 0), stop=(r == 1)),
                            h_done[k], *bank.busy)
                for h in x.h:
                    h.busy = [mm]
                in_done = dve.do(lambda e, bank=bank: e.tensor_tensor(x.mix_in.t, bank.t[:, 0:NE * D],
                                                                      b2_rows[:, :], ALU.add), mm, ns=dve_ns(NE * D))
                release(bank, in_done)
                yield in_done
                m_done = dve.do(lambda e, b=b: e.tensor_scalar(x.mix[0].t, x.mix_in.t[:, 0:D], probs[:, b, 0:1],
                                                               None, ALU.mult), in_done)
                for n in range(1, NE):
                    m_done = dve.do(lambda e, b=b, n=n: e.scalar_tensor_tensor(
                        x.mix[n].t, x.mix_in.t[:, n * D:(n + 1) * D], probs[:, b, n:n + 1], x.mix[n - 1].t,
                        ALU.mult, ALU.add), m_done, *x.mix[n].busy)
                yield m_done
                bank = yield from any_bank()
                turned = pe.do(lambda e, bank=bank: e.transpose(bank.t[:, 0:S], x.mix[2].t, ident),
                               m_done, *bank.busy, ns=100)
                x.mix[2].busy = [turned]
                mT_done = act.do(lambda e, i=i, bank=bank: e.copy(x.mixT.t[:, i, :], bank.t[:, 0:S]),
                                 turned, *x.mixT.busy)
                release(bank, mT_done)
            bank = yield from any_bank()
            g_mm = pe.do(lambda e, bank=bank: e.matmul(bank.t[:, 0:cols], W["l1_gw2"], gate_h.t, start=True,
                                                       stop=True), gh_done, *bank.busy, ns=mm_ns(cols))
            x.gate_h.busy = [g_mm]
            g_done = act.do(lambda e, bank=bank: e.activation(
                x.gate.t.rearrange("p b s -> p (b s)"), bank.t[:, 0:cols], ACT.Sigmoid, bias=W["l1_gb2"]),
                g_mm, *x.gate.busy, ns=act_ns(cols))
            release(bank, g_done)
            yield mT_done
            bank = yield from any_bank()
            o_mm = pe.do(lambda e, bank=bank: e.matmul(bank.t[:, 0:cols], W["l1_ow"], x.mixT.t.rearrange(
                "p b s -> p (b s)"), start=True, stop=True), mT_done, *bank.busy, ns=mm_ns(cols))
            x.mixT.busy = [o_mm]
            d_done = dve.do(lambda e, bank=bank: e.scalar_tensor_tensor(
                x.delta.t.rearrange("p b s -> p (b s)"), bank.t[:, 0:cols], W["l1_ob"],
                x.gate.t.rearrange("p b s -> p (b s)"), ALU.add, ALU.mult), o_mm, g_done, *x.delta.busy,
                ns=dve_ns(cols))
            x.gate.busy = [d_done]
            release(bank, d_done)
            added = pool.do(lambda e: e.tensor_tensor(xT[:, seqs, :], xT[:, seqs, :], x.delta.t, ALU.add),
                            d_done, *x_last[seqs], ns=pool_ns(cols))
            x.delta.busy = [added]
            x_last[seqs] = [added] * PAIR
            experts_read[c % 2] = o_mm
            yield None

        later = {}

        def folded(name):
            bo = sb(name + "_bo", [128, 1])
            bank = take()
            for c in range(2):
                mm = pe.do(lambda e, c=c, bank=bank: e.matmul(
                    bank.t[:, 0:1], W[name + "_o"][:, c * D:(c + 1) * D], W[name + "_vb"][:, c:c + 1],
                    start=(c == 0), stop=(c == 1)), L(name + "_o"), *bank.busy)
            bo_done = dve.do(lambda e, bank=bank: e.tensor_scalar(bo[:, :], bank.t[:, 0:1], W[name + "_ob"], None,
                                                                  ALU.add), mm)
            give(bank, bo_done)
            later[name + "_bo"] = bo[:, 0:1], bo_done

        def l2_l3_modulations():
            for n, w in (("l2q", "l2_ssq"), ("l2k", "l2_sskv")):
                m, done = conditioned(n + "_mod", W[w], W[w + "_b"], 2, silu_c[:, :], silu_c_done)
                yield done
                scale, scale_done = affine_scale(n + "A", m[:, 0, :], done, W["ones"][:, 0:1], None)
                later[n] = scale, m[:, 1, :], scale_done
                yield scale_done
            for n in ("1", "2"):
                m, done = conditioned("l3_mod" + n, W["l3_aff" + n], W[f"l3_aff{n}_b"], 2, condT, None)
                yield done
                scale, shift = sb("l3A" + n, [128, B]), sb("l3B" + n, [128, B])
                dve.do(lambda e, m=m, t=scale, n=n: e.tensor_scalar(t[:, :], m[:, 0, :], W[f"l3_ln{n}g"], None,
                                                                    ALU.mult), done)
                shift_done = dve.do(lambda e, m=m, t=shift, n=n: e.scalar_tensor_tensor(
                    t[:, :], m[:, 0, :], W[f"l3_ln{n}b"], m[:, 1, :], ALU.mult, ALU.add), done)
                later["l3_" + n] = scale, shift, shift_done
                yield shift_done
            for n in ("l2", "l3s", "l3c"):
                folded(n)
                yield later[n + "_bo"][1]

        experts_read = [None, None]

        def expert_chain(i):
            x = Experts(i)
            for c in range(i, B // PAIR, 2):
                yield from l1_experts(x, c)

        expert_chains = [expert_chain(0), expert_chain(1), l2_l3_modulations()]
        interleave(lambda tasks: tasks.extend(Task(expert_chains.pop(0)) for _ in list(expert_chains)))
        work_free.append(free_banks.pop(free_banks.index(shared)))
        end_dense()
        exp_ln_tables()

        ctx_load = {}
        ctx_reads = {}

        def l2_head(job, b):
            c, i = divmod(b, QUAD)
            norm, xn = job.prep.norm, job.prep.xn
            kvn = normT[:, b, 0:SK]
            kv_scale, kv_shift, kv_mod_done = later["l2k"]
            scale, shift, mod_done = later["l2q"]
            if c not in ctx_load:
                ctx_load[c] = sp.dma(lambda e: e.dma_start(ctx_tok[c % 2][:, :, :],
                                                           a["ctx_tok"][:, c * QUAD:(c + 1) * QUAD, :]),
                                     sem(f"ld_ctx_tok{c}"), *ctx_reads.get(c - 2, []))
            yield from layer_norm(norm, ctx_tok[c % 2][:, i, :], ctx_load[c], SK, kv_scale[:, b:b + 1],
                                  kv_shift[:, b:b + 1], kv_mod_done, kvn, experts_read, token_major=True)
            kv_done = norm.done
            ctx_reads.setdefault(c, []).append(kv_done)
            yield from layer_norm(norm, xT[:, b, :], x_last[b], S, scale[:, b:b + 1], shift[:, b:b + 1],
                                  mod_done, xn.t[:, :], xn.busy)
            yield from cross_head(job, xn.t[:, :], norm.done, kvn, kv_done, SK,
                                  ("l2_q", "l2_k", "l2_v", "l2_o"), W["l2_qb"], W["l2_kb"], None, None,
                                  biased(b, *later["l2_bo"]), b)

        def l3_self_head(job, b):
            norm, xn = job.prep.norm, job.prep.xn
            scale, shift, mod_done = later["l3_1"]
            yield from layer_norm(norm, xT[:, b, :], x_last[b], S, scale[:, b:b + 1], shift[:, b:b + 1],
                                  mod_done, xn.t[:, :], xn.busy)
            yield from cross_head(job, xn.t[:, :], norm.done, xn.t[:, :], norm.done, S,
                                  ("l3s_q", "l3s_k", "l3s_v", "l3s_o"), W["l3s_qb"], W["l3s_kb"], None, None,
                                  biased(b, *later["l3s_bo"]), b)

        def l3_cross_head(job, b):
            yield from cross_head(job, xT[:, b, :], x_last[b], ctxT[:, b, :], loaded["ctx"], SK,
                                  ("l3c_q", "l3c_k", "l3c_v", "l3c_o"), W["l3c_qb"], W["l3c_kb"], None, None,
                                  biased(b, *later["l3c_bo"]), b)

        def l3_ffn_norm(norm, b):
            scale, shift, mod_done = later["l3_2"]
            yield from layer_norm(norm, xT[:, b, :], x_last[b], S, scale[:, b:b + 1], shift[:, b:b + 1],
                                  mod_done, normT[:, b, :], experts_read)
            norm_done[b] = norm.done

        attentions([l2_head, l3_self_head, l3_cross_head], l3_ffn_norm)

        for j in range(NJ):
            dense_banks[j].busy = [score_busy[j]]
        stores = []

        def l3_out(c, bank, mm):
            seqs = slice(c * QUAD, (c + 1) * QUAD)
            flat = xT[:, seqs, :].rearrange("p b s -> p (b s)")
            done = dve.do(lambda e: e.scalar_tensor_tensor(flat, bank.t[:, :], W["l3_b2"], flat, ALU.add, ALU.add),
                          mm, *x_last[seqs])
            stores.append(sp.dma(lambda e: e.dma_start(out_xT[:, seqs, :], xT[:, seqs, :]), sem(f"store{c}"), done))
            return done

        for c in range(B // QUAD):
            mlp(c, "l3_w1", "l3_b1", "l3_w2", ACT.Gelu, l3_out)

        lanes = (pe, dve, act, pool, sp)
        for lane in lanes:
            lane.number()
        block = ctx.enter_context(nc.Block())

        @block.tensor
        def _(e):
            pe.run(e)

        @block.vector
        def _(e):
            dve.run(e)

        @block.scalar
        def _(e):
            act.run(e)

        @block.gpsimd
        def _(e):
            pool.run(e)

        @block.sync
        def _(e):
            sp.run(e)
            for s in stores:
                e.wait_ge(s.sem, 16)


def _pad_out(w):
    n = w.shape[1]
    heads = w.reshape(NG, NJ, HD, n)
    out = np.zeros((NJ, TILE, 2, n), w.dtype)
    for g in range(NG):
        at = VW * g if g < 3 else 0
        out[:, at:at + HD, 1 if g == 3 else 0, :] = heads[g]
    return out.reshape(128, 2 * n)


def _constants():
    ident = np.eye(128, dtype=np.float32)
    own_head = np.repeat(np.eye(NH, dtype=np.float32), HD, axis=0)
    n = S // 2
    inv_freq = 1.0 / 10000.0 ** (np.arange(0, HD, 2, dtype=np.float32) / HD)
    freqs = np.outer(np.arange(n, dtype=np.float32), inv_freq)
    emb = np.concatenate([freqs, freqs], axis=-1)
    sign = np.where(np.arange(HD) < HD // 2, -1.0, 1.0)
    cos = np.tile(np.tile(np.cos(emb).astype(np.float32).T, (NH, 1)), (1, 2))
    sin = np.tile(np.tile((np.sin(emb) * sign).astype(np.float32).T, (NH, 1)), (1, 2))
    pick = np.zeros((128, 2, 128), np.float32)
    for j in range(NJ):
        for r in range(TILE):
            g = r // VW if r < 3 * VW else 0
            pick[TILE * j + VW * g + HD, 0, TILE * j + r] = 1.0
            pick[TILE * j + HD, 1, TILE * j + r] = 1.0
    return {"ident": ident, "own_head": own_head, "rope_cos": cos, "rope_sin": sin,
            "pick_den": pick.reshape(128, 256), "ones": np.ones((128, 128), np.float32)}


def _swap(w):
    return w.reshape(w.shape[0], NH, 2, HD // 2)[:, :, ::-1].reshape(w.shape[0], D)


def _col(v):
    return v.reshape(-1, 128).T


def _rows(w):
    return w.reshape(-1, 128, w.shape[1]).transpose(1, 0, 2).reshape(128, -1)


def _head_bias(b):
    return _pad_out(b[:, None]).reshape(128, 2)


def kernel(**inputs):
    import concourse.bacc as bacc
    from concourse.bass_utils import run_bass_kernel_spmd

    i = {k: np.asarray(v) for k, v in inputs.items()}
    z = lambda layer, name: i[f"{layer}_xcond_{name}"]
    p = _constants()
    p["condT"] = i["cond_1024"].T
    p["l0_ada"], p["l0_ada_b"] = z("L0", "adaLN_W"), _col(z("L0", "adaLN_b"))
    for n in ("norm1", "normc", "norm2"):
        p["l0_" + n] = _col(z("L0", n + "_w"))
    wq, wk, wv = (z("L0", "qkv_W")[:, c * D:(c + 1) * D] for c in range(3))
    p["l0_q"], p["l0_qswap"], p["l0_k"], p["l0_kswap"] = wq, _swap(wq), wk, _swap(wk)
    p["l0_v"], p["l0_o"] = wv, _pad_out(z("L0", "attn_out_W"))
    p["l0c_q"], p["l0c_k"] = z("L0", "cq_W"), z("L0", "ck_W")
    p["l0c_v"], p["l0c_o"] = z("L0", "cv_W"), _pad_out(z("L0", "co_W"))
    for layer, n, names in (("L0", "l0", ("mlp_W1", "mlp_b1", "mlp_W2", "mlp_b2")),
                            ("L3", "l3", ("ffn_w1", "ffn_b1", "ffn_w2", "ffn_b2"))):
        p[n + "_w1"], p[n + "_b1"] = z(layer, names[0]), _col(z(layer, names[1]))
        p[n + "_w2"], p[n + "_b2"] = _rows(z(layer, names[2])), _col(z(layer, names[3]))
    p["l1_gamma"], p["l1_beta"] = _col(z("L1", "ln_gamma")), _col(z("L1", "ln_beta"))
    p["l1_q"], p["l1_k"], p["l1_v"] = z("L1", "Wq"), z("L1", "Wk"), z("L1", "Wv")
    p["l1_router"] = _rows(z("L1", "router_W"))
    rb = np.zeros((128, 1), np.float32)
    rb[:NE, 0] = z("L1", "router_b")
    p["l1_router_b"] = rb
    w1 = z("L1", "e_w1").transpose(1, 0, 2).reshape(3 * D, NE * RH)
    p["l1_w1"], p["l1_b1"] = _rows(w1), _col(z("L1", "e_b1"))
    p["l1_w2"] = _rows(z("L1", "e_w2").reshape(NE * RH, D))
    b2 = np.zeros((128, NE * D), np.float32)
    b2[0] = z("L1", "e_b2").reshape(-1)
    p["l1_b2row"] = b2
    p["l1_gw1"], p["l1_gb1"] = _rows(z("L1", "gate_w1")), _col(z("L1", "gate_b1"))
    p["l1_gw2"], p["l1_gb2"] = z("L1", "gate_w2"), _col(z("L1", "gate_b2"))
    p["l1_ow"], p["l1_ob"] = z("L1", "out_w"), _col(z("L1", "out_b"))
    p["l2_ssq"], p["l2_ssq_b"] = z("L2", "Wss_q"), _col(z("L2", "bss_q"))
    p["l2_sskv"], p["l2_sskv_b"] = z("L2", "Wss_kv"), _col(z("L2", "bss_kv"))
    kv, bkv = z("L2", "Wkv"), z("L2", "bkv")
    p["l3_aff1"], p["l3_aff1_b"] = z("L3", "aff1_w"), _col(z("L3", "aff1_b"))
    p["l3_aff2"], p["l3_aff2_b"] = z("L3", "aff2_w"), _col(z("L3", "aff2_b"))
    for n in ("ln1", "ln2"):
        p[f"l3_{n}g"], p[f"l3_{n}b"] = _col(z("L3", n + "_g")), _col(z("L3", n + "_b"))
    for n, (q, qb, k, kb, v, vb, o, ob) in {
        "l2": (z("L2", "Wq"), z("L2", "bq"), kv[:, :D], bkv[:D], kv[:, D:], bkv[D:], z("L2", "Wp"), z("L2", "bp")),
        "l3s": [z("L3", "sa_" + s) for s in ("qw", "qb", "kw", "kb", "vw", "vb", "ow", "ob")],
        "l3c": [z("L3", "ca_" + s) for s in ("qw", "qb", "kw", "kb", "vw", "vb", "ow", "ob")],
    }.items():
        p[n + "_q"], p[n + "_qb"] = q, _col(qb)
        p[n + "_k"], p[n + "_kb"] = k, _col(kb)
        p[n + "_v"], p[n + "_vb"] = v, _head_bias(vb)
        p[n + "_o"], p[n + "_ob"] = _pad_out(o), _col(ob)

    arrays = {name: np.ascontiguousarray(np.concatenate([p[n] for n, _ in items], axis=1))
              for name, items in PACKS}
    for name, items in PACKS:
        assert arrays[name].shape == (128, PACK_COLS[name]), name
    arrays["xT"] = np.ascontiguousarray(i["x"].transpose(2, 0, 1))
    arrays["ctxT"] = np.ascontiguousarray(i["ctx_1024"].transpose(2, 0, 1))
    arrays["ctx_tok"] = np.ascontiguousarray(i["ctx_1024"].transpose(1, 0, 2))
    arrays["mask_qk"] = np.ascontiguousarray(i["mask_SxS_bk0"]).view(np.uint32)
    arrays["mask_kv"] = np.ascontiguousarray(i["mask_BxS2_bf1"]).view(np.uint8)

    nc = bacc.Bacc("TRN2", target_bir_lowering=False, num_devices=1)
    aps = {n: nc.dram_tensor("in_" + n, v.shape, mybir.dt.from_np(v.dtype), kind="ExternalInput").ap()
           for n, v in arrays.items()}
    out = nc.dram_tensor("out_xT", (D, B, S), F32, kind="ExternalOutput").ap()
    build(nc, aps, out)
    r = run_bass_kernel_spmd(nc, [{"in_" + n: v for n, v in arrays.items()}], core_ids=[0])
    return np.ascontiguousarray(r.results[0]["out_xT"].transpose(1, 2, 0))
```
